# Optimizing a Trainium2 kernel written in Bass

```python
import numpy as np
import jax
import jax.numpy as jnp

def _softmax(x, axis=-1):
    return jax.nn.softmax(x, axis=axis)

def _gelu(x):
    return jax.nn.gelu(x, approximate=True)

def _silu(x):
    return jax.nn.silu(x)

def _sigmoid(x):
    return jax.nn.sigmoid(x)

def _layernorm(x, axis=-1, eps=1e-05):
    m = jnp.mean(x, axis=axis, keepdims=True)
    v = jnp.var(x, axis=axis, keepdims=True)
    return (x - m) / jnp.sqrt(v + eps)

def _scatter_add(tgt, idx, src, axis=0):
    return tgt.at[idx].add(src)

def _segment_sum(src, seg, n):
    return jax.ops.segment_sum(src, seg, n)
kernel_name = 'mk_adj_ffn_d1_adj_r2_b0f460'

def setup_inputs(seed: int=0):
    np.random.seed(seed)
    _w = jnp.asarray

    def _rec_inputs():
        import jax
        import jax.numpy as jnp
        _gk = jax.random.key(seed)
        x = -0.0002928 + 1 * jax.random.normal(jax.random.fold_in(_gk, 1), (4096, 256), jnp.float32)
        _w = (1.0 + jnp.arange(4096, dtype=jnp.float32)) ** (-0.5)
        _w = _w / _w.mean()
        _pij = jnp.clip(0.00195312 * _w[:, None] * _w[None, :], 0.0, 1.0)
        _a = jax.random.uniform(jax.random.fold_in(_gk, 2), (4096, 4096)) < _pij
        adj = _a
        return (x, adj)
    x, adj = _rec_inputs()

    def _L0_gnn_setup():
        import jax, jax.numpy as jnp
        import numpy as np
        N = 4096
        D = 256
        NEG = -1e+30
        key = jax.random.key(seed)
        ks = jax.random.split(key, 5)
        neuron_states = jax.random.normal(ks[0], (N, D), dtype=jnp.float32)
        adjacency = jax.random.bernoulli(ks[1], 0.05, (N, N))
        Wq = jax.random.normal(ks[2], (D, D), dtype=jnp.float32) / np.sqrt(D)
        Wk = jax.random.normal(ks[3], (D, D), dtype=jnp.float32) / np.sqrt(D)
        Wv = jax.random.normal(ks[4], (D, D), dtype=jnp.float32) / np.sqrt(D)
        return {'neuron_states': neuron_states, 'adjacency': adjacency, 'Wq': Wq, 'Wk': Wk, 'Wv': Wv}
    _L0_gnn_all = _L0_gnn_setup()
    _L0_gnn_in = {k: v for k, v in _L0_gnn_all.items() if k in ('Wq', 'Wk', 'Wv')}
    del _L0_gnn_all

    def _L0_ffn_setup():
        import jax, jax.numpy as jnp
        import numpy as np
        NUM_EXPERTS = 8
        TOP_K = 2
        key = jax.random.key(seed)
        ks = jax.random.split(key, 5)
        B, T, D, H, E = (8, 2048, 256, 768, NUM_EXPERTS)
        scale = 0.02
        x = jax.random.normal(ks[0], (B, T, D), dtype=jnp.float32)
        gate_w = jax.random.normal(ks[1], (E, D), dtype=jnp.float32) * scale
        w1 = jax.random.normal(ks[2], (E, H, D), dtype=jnp.float32) * scale
        w3 = jax.random.normal(ks[3], (E, H, D), dtype=jnp.float32) * scale
        w2 = jax.random.normal(ks[4], (E, D, H), dtype=jnp.float32) * scale
        return {'x': x, 'gate_w': gate_w, 'w1': w1, 'w3': w3, 'w2': w2}
    _L0_ffn_all = _L0_ffn_setup()
    _L0_ffn_in = {k: v for k, v in _L0_ffn_all.items() if k in ('gate_w', 'w1', 'w3', 'w2')}
    del _L0_ffn_all
    return {'x': x, 'adj': adj, 'L0_gnn_Wq': _L0_gnn_in['Wq'], 'L0_gnn_Wk': _L0_gnn_in['Wk'], 'L0_gnn_Wv': _L0_gnn_in['Wv'], 'L0_ffn_gate_w': _L0_ffn_in['gate_w'], 'L0_ffn_w1': _L0_ffn_in['w1'], 'L0_ffn_w3': _L0_ffn_in['w3'], 'L0_ffn_w2': _L0_ffn_in['w2']}

def reference(x, adj, L0_gnn_Wq, L0_gnn_Wk, L0_gnn_Wv, L0_ffn_gate_w, L0_ffn_w1, L0_ffn_w3, L0_ffn_w2):
    import jax
    import jax.numpy as jnp

    def _L0_gnn_ref(neuron_states, adjacency, Wq, Wk, Wv):
        import jax, jax.numpy as jnp
        import numpy as np
        N = 4096
        D = 256
        NEG = -1e+30
        q = neuron_states @ Wq.T
        k = neuron_states @ Wk.T
        v = neuron_states @ Wv.T
        mask = adjacency.T
        scores = jnp.where(mask, q @ k.T, NEG)
        attn = jax.nn.softmax(scores, axis=1)
        attn = jnp.where(mask, attn, 0.0)
        return attn @ v

    def _L0_ffn_ref(x, gate_w, w1, w3, w2):
        import jax, jax.numpy as jnp
        import numpy as np
        NUM_EXPERTS = 8
        TOP_K = 2
        B, T, D = x.shape
        E = gate_w.shape[0]
        xf = x.reshape(-1, D)
        N = xf.shape[0]
        gate_logits = xf @ gate_w.T
        weights, indices = jax.lax.top_k(gate_logits, TOP_K)
        weights = jax.nn.softmax(weights, axis=-1)
        combine = jnp.zeros((N, E), dtype=xf.dtype).at[jnp.arange(N)[:, None], indices].add(weights)
        out = jnp.zeros_like(xf)
        for e in range(E):
            h = jax.nn.silu(xf @ w1[e].T) * (xf @ w3[e].T)
            y = h @ w2[e].T
            out = out + combine[:, e:e + 1] * y
        return out.reshape(B, T, D)
    x = x + _L0_gnn_ref(_layernorm(x, axis=-1), adj, L0_gnn_Wq, L0_gnn_Wk, L0_gnn_Wv)
    x = x + _L0_ffn_ref(_layernorm(x, axis=-1)[None], L0_ffn_gate_w, L0_ffn_w1, L0_ffn_w3, L0_ffn_w2)[0]
    return x

_drawn_inputs = setup_inputs


def setup_inputs(seed=0):
    import zlib

    import numpy as np

    out = dict(_drawn_inputs(seed))
    spreads = {}
    factors = {'L0_ffn_gate_w': 4.325, 'L0_ffn_w1': 3.785, 'L0_ffn_w3': 3.748, 'L0_ffn_w2': 3.749}
    for name, (base, spread) in spreads.items():
        noise = np.random.default_rng([zlib.crc32(name.encode()), seed]).standard_normal(out[name].shape)
        drawn = base * np.exp(spread * noise) if base else spread * noise
        out[name] = jnp.asarray(drawn.astype(out[name].dtype))
    for name, factor in factors.items():
        out[name] = (out[name] * factor).astype(out[name].dtype)
    return out
```

```python
import concourse.bass as bass
from concourse import mybir
from contextlib import ExitStack


def gnn_moe(nc, x, adj, wq, wk, wv_t, gate_t, w1_t, w3_t, w2_t, out):
    fp32 = mybir.dt.float32
    fp16 = mybir.dt.float16
    bf16 = mybir.dt.bfloat16
    u8 = mybir.dt.uint8
    u32 = mybir.dt.uint32
    ALU = mybir.AluOpType
    ACT = mybir.ActivationFunctionType
    AX = mybir.AxisListType
    RMAX = bass.bass_isa.ReduceOp.max

    P = 128
    N, D = x.shape
    DC = D // P
    TILES = N // P
    EPS = 1e-5
    QB = 256
    QT = QB // P
    BLOCKS = N // QB
    KT = 4
    GROUPS = TILES // KT
    STEPS = BLOCKS * GROUPS
    GW = KT * QB
    SLOTS = 2 * GROUPS
    PASSES = STEPS // SLOTS
    SUB_LAG = GROUPS + 2
    LO_LAG = SUB_LAG + 1
    PV_LAG = SUB_LAG + 2
    OUT_LAG = 2 * GROUPS + 4
    RING = 4
    BIG = 1.0e30
    VW = D + 1
    VP = VW + 1

    E = w1_t.shape[0]
    ROWS = (2 * N // 256 + E - 1) * 256
    x1_d = nc.dram_tensor("x1_d", (N, D), fp32, kind="Internal").ap()
    xs_d = nc.dram_tensor("xs_d", (ROWS, 2 * D), fp16, kind="Internal").ap()
    ys_d = nc.dram_tensor("ys_d", (ROWS, D), fp32, kind="Internal").ap()

    ctx = ExitStack()
    with ctx:
        def sb(name, shape, dt):
            return ctx.enter_context(nc.sbuf_tensor(name, shape, dt))

        def sem(name):
            return ctx.enter_context(nc.semaphore(name))

        ps_s = [ctx.enter_context(nc.psum_tensor(f"ps_scores{i}", [P, KT, QB], fp32)) for i in range(2)]
        ps_o = [ctx.enter_context(nc.psum_tensor(f"ps_out{i}", [P, 512], fp32)) for i in range(QT)]
        ps_a = ctx.enter_context(nc.psum_tensor("ps_a", [P, 512], fp32))
        ps_b = ctx.enter_context(nc.psum_tensor("ps_b", [P, 512], fp32))

        kT = [sb(f"kT_{h}", [P, DC, N], fp16) for h in ("hi", "lo")]
        val = [sb(f"val_{h}", [P, TILES, VP], fp16) for h in ("hi", "lo")]
        m_w = [sb(f"m_{h}", [P, DC, D], fp16) for h in ("hi", "lo")]
        q_t = [sb(f"qT_{h}", [P, 2, DC, QB], fp16) for h in ("hi", "lo")]
        ident = sb("ident", [P, P], fp32)
        ident16 = sb("ident16", [P, P], fp16)
        ones = sb("ones", [P, P], fp32)
        scales = sb("scales", [P, 16], fp32)
        adj_sb = sb("adj_sb", [P, GROUPS, KT, 2 * QB], u8)
        mask = sb("mask", [P, RING, GW], bf16)
        t_sb = sb("t_sb", [P, SLOTS, GW], fp32)
        run_max = sb("run_max", [P, 2, GW], fp32)
        m_col = sb("m_col", [P, QT], fp32)
        diag = sb("diag", [P, QT, P], fp32)
        m_row = sb("m_row", [P, 2, QB], fp32)
        zero = sb("zero", [P, 2 * D], fp16)
        s_zset = sem("s_zset")
        s_zero = sem("s_zero")
        e_sb = sb("e_sb", [P, 2, GW], fp32)
        p_hi = sb("p_hi", [P, RING, GW], fp16)
        p_lo = sb("p_lo", [P, RING, GW], fp16)
        den = sb("den", [P, 2, QT], fp32)
        x_in = sb("x_in", [P, 2, QT, D], fp32)
        x_out = sb("x_out", [P, 2, QT, D], fp32)

        flat = t_sb[:, :, :].rearrange("p s w -> p (s w)")
        taken = [0]

        def early(width, dt=fp32):
            words = width if dt == fp32 else width // 2
            piece = flat[:, taken[0]:taken[0] + words]
            taken[0] += words
            return piece if dt == fp32 else piece.bitcast(dt)

        x_all = early(8192).rearrange("p (t d) -> p t d", d=D)
        wq_sb = early(DC * D).rearrange("p (c d) -> p c d", c=DC)
        wk_sb = early(DC * D).rearrange("p (c d) -> p c d", c=DC)
        wv_sb = early(DC * D).rearrange("p (c d) -> p c d", c=DC)
        wv_w = [early(DC * D, fp16).rearrange("p (c d) -> p c d", c=DC) for _ in range(2)]
        xn = early(2 * D).rearrange("p (r d) -> p r d", r=2)
        xn_w = [early(4 * D, fp16).rearrange("p (r d) -> p r d", r=4) for _ in range(2)]
        stats = early(TILES * 6).rearrange("p (t s) -> p t s", s=6)
        mv = early(TILES * 2).rearrange("p (t s) -> p t s", s=2)
        var = early(TILES)
        std = early(TILES)
        rstd = early(TILES)
        tmp = early(TILES)
        amax = early(2)
        amax_all = early(2)
        assert taken[0] <= SLOTS * GW

        INV_M, INV_V, S_M, S_V, EXP_SCALE, OUT_SCALE = range(6)

        def col(i):
            return scales[:, i:i + 1]


        tr_ps = [[ps_s[i][:, 2 * h:2 * h + 1, :].rearrange("p a b -> p (a b)").bitcast(fp16)[:, 0:DC * P]
                  .rearrange("p (c q) -> p c q", c=DC) for h in range(2)] for i in range(2)]
        v_ps = [ps_o[i][:, 0:D] for i in range(2)]

        s_x = [sem(f"s_x_load{i}") for i in range(4)]
        s_w = sem("s_w")
        s_const = sem("s_const")
        s_stats = sem("s_stats")
        s_var = sem("s_var")
        s_sqrt = sem("s_sqrt")
        s_chain = sem("s_chain")
        s_m_ps = sem("s_m_ps")
        s_amax = sem("s_amax")
        s_amax_all = sem("s_amax_all")
        s_scale = sem("s_scale")
        s_whi = sem("s_whi")
        s_wlo = sem("s_wlo")
        s_xn = sem("s_xn")
        s_xhi = sem("s_xhi")
        s_xlo = sem("s_xlo")
        s_tr = sem("s_tr")
        s_khi = sem("s_khi")
        s_klo = sem("s_klo")
        s_v_ps = sem("s_v_ps")
        s_vhi = sem("s_vhi")
        s_vlo = sem("s_vlo")
        s_adj = [sem(f"s_adj{g}") for g in range(GROUPS)]
        s_mask = sem("s_mask")
        s_q_ps = sem("s_q_ps")
        s_qhi = sem("s_qhi")
        s_qlo = sem("s_qlo")
        s_scores = sem("s_scores")
        s_evac = sem("s_evac")
        s_max = sem("s_max")
        s_max_t = sem("s_max_t")
        s_mcol = sem("s_mcol")
        s_diag = sem("s_diag")
        s_mrow_ps = sem("s_mrow_ps")
        s_mrow = sem("s_mrow")
        s_sub = sem("s_sub")
        s_exp = sem("s_exp")
        s_phi = sem("s_phi")
        s_plo = sem("s_plo")
        s_pv = sem("s_pv")
        s_den = sem("s_den")
        s_x1 = sem("s_x1")
        s_xin = [sem(f"s_xin{i}") for i in range(2)]
        s_out = [sem(f"s_out{i}") for i in range(2)]

        x_t = x.rearrange("(t p) d -> p t d", p=P)
        out_t = x1_d.rearrange("(t p) d -> p t d", p=P)
        adj_t = adj.rearrange("(g s p) i -> p g s i", p=P, s=KT)
        TERMS = ((0, 0), (0, 1), (1, 0))

        def before_start(v):
            return isinstance(v, int) and v < 0

        def passes(eng, step):
            for n in range(SLOTS):
                step(n, 0)
            with eng.Fori(1, PASSES - 1) as it:
                for n in range(SLOTS):
                    step(n, it)
            for n in range(SLOTS):
                step(n, PASSES - 1)
            for n in range(OUT_LAG - GROUPS + 1):
                step(n, PASSES)

        block = ctx.enter_context(nc.Block())

        @block.sync
        def _(sp):
            for i in range(4):
                sp.dma_start(x_all[:, 8 * i:8 * i + 8, :], x_t[:, 8 * i:8 * i + 8, :]).then_inc(s_x[i], 16)
            sp.dma_start(wq_sb, wq.rearrange("(c p) d -> p c d", p=P)).then_inc(s_w, 16)
            sp.dma_start(wk_sb, wk.rearrange("(c p) d -> p c d", p=P)).then_inc(s_w, 16)
            sp.dma_start(wv_sb, wv_t.rearrange("(c p) d -> p c d", p=P)).then_inc(s_w, 16)
            for g in range(GROUPS):
                sp.dma_start(adj_sb[:, g, :, :], adj_t[:, g, :, 0:2 * QB]).then_inc(s_adj[g], 16)
            for r in range(2):
                sp.dma_start(x_in[:, r, :, :], x_t[:, r * QT:r * QT + QT, :]).then_inc(s_xin[r], 16)
            with sp.Fori(1, PASSES) as it:
                adj_src = [adj_t[:, g, :, bass.ds(it * (2 * QB), 2 * QB)] for g in range(GROUPS)]
                x_src = [x_t[:, bass.ds(it * (2 * QT) + r * QT, QT), :] for r in range(2)]
                x1_dst = [out_t[:, bass.ds(it * (2 * QT) - (2 - r) * QT, QT), :] for r in range(2)]
                for ap in adj_src:
                    sp.compute_val(ap.offset)
                for ap in x_src + x1_dst:
                    sp.compute_val(ap.offset * 4)
                for g in range(GROUPS):
                    sp.wait_ge(s_mask, it * SLOTS - GROUPS + g + 1)
                    sp.dma_start(adj_sb[:, g, :, :], adj_src[g]).then_inc(s_adj[g], 16)
                for r in range(2):
                    sp.wait_ge(s_x1, it * 2 - 1 + r)
                    sp.dma_start(x_in[:, r, :, :], x_src[r]).then_inc(s_xin[r], 16)
                    sp.dma_start(x1_dst[r], x_out[:, r, :, :]).then_inc(s_out[r], 16)
            for r in range(2):
                sp.wait_ge(s_x1, BLOCKS - 1 + r)
                at = TILES - (2 - r) * QT
                sp.dma_start(out_t[:, at:at + QT, :], x_out[:, r, :, :]).then_inc(s_out[r], 16)
            for r in range(2):
                sp.wait_ge(s_out[r], 16 + 16 * BLOCKS // 2)

        @block.gpsimd
        def _(pool):
            for r in range(2):
                pool.sem_inc(s_out[r], 16)
            pool.memset(zero[:, :], 0.0).then_inc(s_zset, 1)
            pool.wait_ge(s_zset, 1)
            for i in range(ROWS // P // 6):
                pool.dma_start(xs_d.rearrange("(q p) r -> p q r", p=P)[:, 6 * i:6 * i + 6, :],
                               zero[:, None, :].to_broadcast([P, 6, 2 * D])).then_inc(s_zero, 16)
            pool.memset(ident[:, :], 0.0).then_inc(s_const, 1)
            pool.memset(ones[:, :], 1.0).then_inc(s_const, 1)
            pool.wait_ge(s_const, 2)
            pool.affine_select(out=ident[:, :], in_=ident[:, :], compare_op=ALU.not_equal, fill=1.0,
                               base=0, pattern=[[-1, P]], channel_multiplier=1).then_inc(s_const, 1)
            pool.wait_ge(s_const, 3)
            pool.tensor_copy(ident16[:, :], ident[:, :]).then_inc(s_const, 1)
            pool.memset(val[0][:, :, D:VP], 1.0).then_inc(s_const, 1)
            pool.memset(val[1][:, :, D:VP], 0.0).then_inc(s_const, 1)
            pool.wait_ge(s_amax, 2)
            pool.partition_all_reduce(amax_all, amax, P, RMAX).then_inc(s_amax_all, 1)
            pool.wait_ge(s_zero, 16 * (ROWS // P // 6))

        @block.tensor
        def _(pe):
            pe.wait_ge(s_w, 48)
            for c in range(DC):
                for k in range(DC):
                    last = pe.matmul(ps_a[:, c * D:(c + 1) * D], wq_sb[:, k, c * P:(c + 1) * P], wk_sb[:, k, :],
                                     start=(k == 0), stop=(k == DC - 1))
            last.then_inc(s_m_ps, 1)
            pe.wait_ge(s_const, 4)

            def transposes(t):
                pe.wait_ge(s_xhi, t + 1)
                pe.wait_ge(s_xlo, t + 1)
                if t >= 2:
                    pe.wait_ge(s_khi, t - 1)
                    pe.wait_ge(s_klo, t - 1)
                for h in range(2):
                    for c in range(DC):
                        last = pe.transpose(tr_ps[t % 2][h][:, c, :], xn_w[h][:, t % 4, c * P:(c + 1) * P],
                                            ident16[:, :])
                last.then_inc(s_tr, 1)

            def values(t):
                pe.wait_ge(s_khi, t + 1)
                pe.wait_ge(s_klo, t + 1)
                if t == 0:
                    pe.wait_ge(s_whi, 2)
                    pe.wait_ge(s_wlo, 2)
                if t >= 2:
                    pe.wait_ge(s_vlo, t - 1)
                terms = [(c, a, w) for c in range(DC) for a, w in TERMS]
                for i, (c, a, w) in enumerate(terms):
                    last = pe.matmul(v_ps[t % 2], kT[a][:, c, t * P:(t + 1) * P], wv_w[w][:, c, :],
                                     start=(i == 0), stop=(i == len(terms) - 1))
                last.then_inc(s_v_ps, 1)

            for t in range(TILES + 2):
                if t < TILES:
                    transposes(t)
                if t >= 2:
                    values(t - 2)

            def queries(b):
                terms = [(k, a, w) for k in range(DC) for a, w in TERMS]
                for c in range(DC):
                    for i, (k, a, w) in enumerate(terms):
                        last = pe.matmul(ps_b[:, c * QB:(c + 1) * QB], m_w[w][:, k, c * P:(c + 1) * P],
                                         kT[a][:, k, bass.ds(b * QB, QB)],
                                         start=(i == 0), stop=(i == len(terms) - 1))
                last.then_inc(s_q_ps, 1)

            queries(0)
            pe.wait_ge(s_vlo, TILES)
            pe.wait_ge(s_vhi, TILES)

            def scores(n, at):
                g, r = n % GROUPS, n // GROUPS % 2
                if not before_start(at - 2):
                    pe.wait_ge(s_evac, at - 1)
                terms = [(c, a, w) for c in range(DC) for a, w in TERMS]
                for s in range(KT):
                    kt = g * KT + s
                    for i, (c, a, w) in enumerate(terms):
                        last = pe.matmul(ps_s[n % 2][:, s, :], kT[a][:, c, kt * P:(kt + 1) * P],
                                         q_t[w][:, r, c, :], start=(i == 0), stop=(i == len(terms) - 1))
                last.then_inc(s_scores, 1)

            def maxima_transposed(n, b):
                pe.wait_ge(s_max, b * (GROUPS - 1))
                for q in range(QT):
                    for s in range(KT):
                        last = pe.transpose((ps_a, ps_b)[q][:, s * P:(s + 1) * P],
                                            run_max[:, (n // GROUPS + 1) % 2, s * QB + q * P:s * QB + (q + 1) * P],
                                            ident[:, :])
                last.then_inc(s_max_t, 1)

            def values_product(m, at):
                g, slot = m % GROUPS, m % RING
                pe.wait_ge(s_phi, at + 1)
                pe.wait_ge(s_plo, at + 1)
                for q in range(QT):
                    for s in range(KT):
                        kt = g * KT + s
                        for a, w in TERMS:
                            width = VW if w == 0 else D
                            last = pe.matmul(ps_o[q][:, 0:width],
                                             (p_hi, p_lo)[a][:, slot, s * QB + q * P:s * QB + (q + 1) * P],
                                             val[w][:, kt, 0:width],
                                             start=(g == 0 and s == 0 and (a, w) == TERMS[0]),
                                             stop=(g == GROUPS - 1 and s == KT - 1 and (a, w) == TERMS[-1]))
                last.then_inc(s_pv, 1)

            def step(n, it):
                at, b, g = it * SLOTS + n, it * (SLOTS // GROUPS) + n // GROUPS, n % GROUPS
                past = isinstance(it, int) and it == PASSES
                if not past:
                    if g == 0:
                        pe.wait_ge(s_qhi, b + 1)
                        pe.wait_ge(s_qlo, b + 1)
                    scores(n, at)
                    if g == 4 and not (isinstance(b, int) and b + 1 == BLOCKS):
                        if not before_start(b - 1):
                            pe.wait_ge(s_mrow, b)
                        queries(b + 1)
                if not before_start(b - 1) and (not past or n < GROUPS):
                    if g == 0:
                        maxima_transposed(n, b)
                    if g == 1:
                        pe.wait_ge(s_diag, b * QT)
                        last = pe.matmul(ps_b[:, 0:QB], ones[:, :], diag[:, :, :].rearrange("p q k -> p (q k)"),
                                         start=True, stop=True)
                        last.then_inc(s_mrow_ps, 1)
                if not before_start(at - PV_LAG) and not (past and n >= PV_LAG):
                    if (n - PV_LAG) % GROUPS == 0 and not before_start(at - PV_LAG - GROUPS):
                        done = it * (SLOTS // GROUPS) + (n - PV_LAG) // GROUPS
                        pe.wait_ge(s_x1, done)
                    values_product(n - PV_LAG, at - PV_LAG)

            passes(pe, step)

        @block.scalar
        def _(act):
            act.wait_ge(s_var, 1)
            act.activation(std, var, ACT.Sqrt).then_inc(s_sqrt, 1)
            act.wait_ge(s_scale, 1)
            act.activation(m_w[0][:, :, :], ps_a[:, :].rearrange("p (c d) -> p c d", c=DC), ACT.Copy,
                           scale=col(S_M)).then_inc(s_whi, 1)
            act.activation(wv_w[0], wv_sb, ACT.Copy, scale=col(S_V)).then_inc(s_whi, 1)
            for t in range(TILES + 2):
                if t < TILES:
                    act.wait_ge(s_xn, t + 1)
                    if t >= 4:
                        act.wait_ge(s_tr, t - 3)
                    act.activation(xn_w[0][:, t % 4, :], xn[:, t % 2, :], ACT.Copy).then_inc(s_xhi, 1)
                if 1 <= t <= TILES:
                    act.wait_ge(s_tr, t)
                    act.activation(kT[0][:, :, (t - 1) * P:t * P], tr_ps[(t - 1) % 2][0],
                                   ACT.Copy).then_inc(s_khi, 1)
                if t >= 2:
                    act.wait_ge(s_v_ps, t - 1)
                    act.activation(val[0][:, t - 2, 0:D], v_ps[t % 2], ACT.Copy, scale=0.25).then_inc(s_vhi, 1)

            def make_mask(n, it):
                at, g = it * SLOTS + n, n % GROUPS
                act.wait_ge(s_adj[g], it * 16 + 16)
                if not before_start(at - RING):
                    act.wait_ge(s_evac, at - RING + 1)
                h = n // GROUPS % 2
                act.activation(mask[:, n % RING, :].rearrange("p (s q) -> p s q", s=KT),
                               adj_sb[:, g, :, h * QB:(h + 1) * QB], ACT.Copy, scale=BIG, bias=-BIG
                               ).then_inc(s_mask, 1)

            def query_high(b, r):
                act.wait_ge(s_q_ps, b + 1)
                act.activation(q_t[0][:, r, :, :], ps_b[:, :].rearrange("p (c q) -> p c q", c=DC), ACT.Copy,
                               scale=0.25).then_inc(s_qhi, 1)

            query_high(0, 0)
            make_mask(0, 0)

            def step(n, it):
                at, b, g = it * SLOTS + n, it * (SLOTS // GROUPS) + n // GROUPS, n % GROUPS
                past = isinstance(it, int) and it == PASSES
                if g == 1 and not before_start(b - 1) and not (past and n > GROUPS):
                    act.wait_ge(s_mrow_ps, b)
                    if not before_start(b - 3):
                        act.wait_ge(s_sub, b * GROUPS - 2 * GROUPS + 1)
                    act.activation(m_row[:, (n // GROUPS + 1) % 2, :], ps_b[:, 0:QB], ACT.Copy
                                   ).then_inc(s_mrow, 1)
                if not past:
                    if not (isinstance(at, int) and at + 1 == STEPS):
                        make_mask((n + 1) % SLOTS, it + (n + 1) // SLOTS)
                    if g == 5 and not (isinstance(b, int) and b + 1 == BLOCKS):
                        query_high(b + 1, (n // GROUPS + 1) % 2)
                m = at - SUB_LAG
                if not before_start(m) and not (past and n >= SUB_LAG):
                    slot = (n - SUB_LAG) % SLOTS
                    act.wait_ge(s_sub, m + 1)
                    if not before_start(m - 2):
                        act.wait_ge(s_plo, m - 1)
                    act.activation(e_sb[:, (n - SUB_LAG) % 2, :], t_sb[:, slot, :], ACT.Exp,
                                   scale=col(EXP_SCALE)).then_inc(s_exp, 1)
                    if not before_start(m - RING):
                        act.wait_ge(s_pv, m - RING + 1)
                    act.activation(p_hi[:, (n - SUB_LAG) % RING, :], t_sb[:, slot, :], ACT.Exp,
                                   scale=col(EXP_SCALE)).then_inc(s_phi, 1)

            passes(act, step)

        @block.vector
        def _(dve):
            chain = [0]

            def link(ins):
                chain[0] += 1
                ins.then_inc(s_chain, 1)
                dve.wait_ge(s_chain, chain[0])

            for t in range(TILES):
                if t % 8 == 0:
                    dve.wait_ge(s_x[t // 8], 16)
                dve.bn_stats(stats[:, t, :], x_all[:, t, :]).then_inc(s_stats, 1)
            for t in range(TILES):
                if t == 0:
                    dve.wait_ge(s_stats, TILES)
                last = dve.bn_aggr(mv[:, t, :], stats[:, t, :])
            link(last)
            dve.tensor_scalar(var, mv[:, :, 1], EPS, None, ALU.add).then_inc(s_var, 1)

            dve.wait_ge(s_m_ps, 1)
            dve.tensor_reduce(amax[:, 0:1], ps_a[:, :], axis=AX.X, op=ALU.max,
                              apply_absolute_value=True).then_inc(s_amax, 1)
            dve.wait_ge(s_w, 48)
            dve.tensor_reduce(amax[:, 1:2], wv_sb.rearrange("p c d -> p (c d)"), axis=AX.X, op=ALU.max,
                              apply_absolute_value=True).then_inc(s_amax, 1)
            dve.wait_ge(s_amax_all, 1)
            link(dve.tensor_scalar(amax, amax_all, 2.0 ** -100, None, ALU.max))
            link(dve.tensor_single_scalar(amax.bitcast(u32), amax.bitcast(u32), 0x7F800000, ALU.bitwise_and))
            link(dve.tensor_scalar(scales[:, INV_M:INV_V + 1], amax, 2.0 ** -8, None, ALU.mult))
            link(dve.reciprocal(scales[:, S_M:S_V + 1], scales[:, INV_M:INV_V + 1]))
            dve.tensor_scalar(scales[:, EXP_SCALE:OUT_SCALE + 1], scales[:, INV_M:INV_V + 1], 4.0, None, ALU.mult
                              ).then_inc(s_scale, 1)
            dve.wait_ge(s_scale, 1)
            dve.wait_ge(s_whi, 1)
            dve.scalar_tensor_tensor(m_w[1][:, :, :].rearrange("p c d -> p (c d)"), ps_a[:, :], col(S_M),
                                     m_w[0][:, :, :].rearrange("p c d -> p (c d)"), ALU.mult, ALU.subtract
                                     ).then_inc(s_wlo, 1)
            dve.wait_ge(s_whi, 2)
            dve.scalar_tensor_tensor(wv_w[1], wv_sb, col(S_V), wv_w[0], ALU.mult, ALU.subtract).then_inc(s_wlo, 1)

            dve.wait_ge(s_sqrt, 1)
            link(dve.reciprocal(rstd, std))
            link(dve.tensor_tensor(tmp, rstd, rstd, ALU.mult))
            link(dve.tensor_tensor(tmp, tmp, var, ALU.mult))
            link(dve.tensor_scalar(tmp, tmp, -0.5, 1.5, ALU.mult, ALU.add))
            link(dve.tensor_tensor(rstd, rstd, tmp, ALU.mult))

            for t in range(TILES + 2):
                if t < TILES:
                    if t >= 2:
                        dve.wait_ge(s_xhi, t - 1)
                        dve.wait_ge(s_xlo, t - 1)
                    dve.tensor_scalar(xn[:, t % 2, :], x_all[:, t, :], mv[:, t, 0:1], rstd[:, t:t + 1],
                                      ALU.subtract, ALU.mult).then_inc(s_xn, 1)
                if 1 <= t <= TILES:
                    dve.wait_ge(s_tr, t)
                    dve.tensor_copy(kT[1][:, :, (t - 1) * P:t * P], tr_ps[(t - 1) % 2][1]
                                    ).then_inc(s_klo, 1)
                if t < TILES:
                    dve.wait_ge(s_xn, t + 1)
                    dve.wait_ge(s_xhi, t + 1)
                    dve.tensor_tensor(xn_w[1][:, t % 4, :], xn[:, t % 2, :], xn_w[0][:, t % 4, :], ALU.subtract
                                      ).then_inc(s_xlo, 1)
                if t >= 2:
                    dve.wait_ge(s_vhi, t - 1)
                    dve.scalar_tensor_tensor(val[1][:, t - 2, 0:D], v_ps[t % 2], 0.25, val[0][:, t - 2, 0:D],
                                             ALU.mult, ALU.subtract).then_inc(s_vlo, 1)

            def query_low(b, r):
                dve.wait_ge(s_qhi, b + 1)
                dve.scalar_tensor_tensor(q_t[1][:, r, :, :], ps_b[:, :].rearrange("p (c q) -> p c q", c=DC), 0.25,
                                         q_t[0][:, r, :, :], ALU.mult, ALU.subtract).then_inc(s_qlo, 1)

            query_low(0, 0)

            def output(bb, r):
                dve.wait_ge(s_pv, bb * GROUPS + GROUPS)
                for q in range(QT):
                    last = dve.tensor_scalar(den[:, 0, q:q + 1], ps_o[q][:, D:VW], 0.5, None, ALU.max)
                last.then_inc(s_den, 1)
                dve.wait_ge(s_den, bb * 3 + 1)
                dve.reciprocal(den[:, 1, :], den[:, 0, :]).then_inc(s_den, 1)
                dve.wait_ge(s_den, bb * 3 + 2)
                dve.tensor_scalar(den[:, 0, :], den[:, 1, :], col(OUT_SCALE), None, ALU.mult).then_inc(s_den, 1)
                dve.wait_ge(s_den, bb * 3 + 3)
                return r

            def step(n, it):
                at, b, g = it * SLOTS + n, it * (SLOTS // GROUPS) + n // GROUPS, n % GROUPS
                r = n // GROUPS % 2
                past = isinstance(it, int) and it == PASSES
                if g == 4 and not before_start(b - 2):
                    output(b - 2, r)
                    dve.wait_ge(s_xin[r], it * 16)
                    if not before_start(it - 1):
                        dve.wait_ge(s_out[r], it * 16)
                    for q in range(QT):
                        last = dve.scalar_tensor_tensor(x_out[:, r, q, :], ps_o[q][:, 0:D], den[:, 0, q:q + 1],
                                                        x_in[:, r, q, :], ALU.mult, ALU.add)
                    last.then_inc(s_x1, 1)
                if g == 5 and not past and not (isinstance(b, int) and b + 1 == BLOCKS):
                    query_low(b + 1, (r + 1) % 2)
                if not past:
                    slot = n % SLOTS
                    dve.wait_ge(s_scores, at + 1)
                    dve.wait_ge(s_mask, at + 1)
                    if not before_start(at - SLOTS):
                        dve.wait_ge(s_phi, at - SLOTS + 1)
                    dve.tensor_tensor(t_sb[:, slot, :], ps_s[n % 2][:, :, :].rearrange("p s q -> p (s q)"),
                                      mask[:, n % RING, :], ALU.add).then_inc(s_evac, 1)
                    if g >= 1:
                        dve.wait_ge(s_evac, at + 1)
                        if g == 1:
                            if not before_start(b - 2):
                                dve.wait_ge(s_max_t, b - 1)
                            before = t_sb[:, slot - 1, :]
                        else:
                            dve.wait_ge(s_max, b * (GROUPS - 1) + g - 1)
                            before = run_max[:, r, :]
                        dve.tensor_tensor(run_max[:, r, :], before, t_sb[:, slot, :], ALU.max).then_inc(s_max, 1)
                if g == 0 and not before_start(b - 1) and not (past and n >= GROUPS):
                    dve.wait_ge(s_max_t, b)
                    if not before_start(b - 2):
                        dve.wait_ge(s_diag, QT * (b - 1))
                    for q in range(QT):
                        dve.tensor_reduce(m_col[:, q:q + 1], (ps_a, ps_b)[q][:, :], axis=AX.X, op=ALU.max
                                          ).then_inc(s_mcol, 1)
                    for q in range(QT):
                        dve.wait_ge(s_mcol, QT * (b - 1) + q + 1)
                        if not before_start(b - 2):
                            dve.wait_ge(s_mrow_ps, b - 1)
                        dve.tensor_scalar(diag[:, q, :], ident[:, :], m_col[:, q:q + 1], -0.1 * BIG,
                                          ALU.mult, ALU.max).then_inc(s_diag, 1)
                m = at - SUB_LAG
                if not before_start(m) and not (past and n >= SUB_LAG):
                    mb = it * (SLOTS // GROUPS) + (n - SUB_LAG) // GROUPS
                    dve.wait_ge(s_mrow, mb + 1)
                    part = t_sb[:, (n - SUB_LAG) % SLOTS, :].rearrange("p (s q) -> p s q", s=KT)
                    row = m_row[:, (n - SUB_LAG) // GROUPS % 2, None, :].to_broadcast([P, KT, QB])
                    dve.tensor_tensor(part, part, row, ALU.subtract).then_inc(s_sub, 1)
                m = at - LO_LAG
                if not before_start(m) and not (past and n >= LO_LAG):
                    dve.wait_ge(s_exp, m + 1)
                    dve.wait_ge(s_phi, m + 1)
                    if not before_start(m - RING):
                        dve.wait_ge(s_pv, m - RING + 1)
                    dve.tensor_tensor(p_lo[:, (n - LO_LAG) % RING, :], e_sb[:, (n - LO_LAG) % 2, :],
                                      p_hi[:, (n - LO_LAG) % RING, :], ALU.subtract).then_inc(s_plo, 1)

            passes(dve, step)

    E, _, H = w1_t.shape
    HC = H // P
    TB = 256
    TBT = TB // P
    TOP = 2
    NB = (TOP * N) // TB + E - 1
    BU = 3
    assert NB % BU == 0 and HC % BU == 0
    NBP = NB // BU
    S2_LAG = 2
    W_SCALE = 2.0 ** 8
    A_INV = 1.0 / W_SCALE
    H_SCALE = 2.0 ** -5
    Y_INV = 1.0 / (W_SCALE * W_SCALE * H_SCALE)
    ROW = 2 * D

    ctx = ExitStack()
    with ctx:
        def sb(name, shape, dt):
            return ctx.enter_context(nc.sbuf_tensor(name, shape, dt))

        def sem(name):
            return ctx.enter_context(nc.semaphore(name))

        ps_ab = [ctx.enter_context(nc.psum_tensor(f"ps_ab{i}", [P, 2, TB], fp32)) for i in range(BU)]
        ps_y = [ctx.enter_context(nc.psum_tensor(f"ps_y{i}", [P, 512], fp32)) for i in range(TBT)]
        ps_t = [ctx.enter_context(nc.psum_tensor(f"ps_t{i}", [P, 512], fp32)) for i in range(2)]
        ps_c = ctx.enter_context(nc.psum_tensor("ps_c", [P, 512], fp32))

        w_all = [sb(f"w_{h}", [P, E, 3, DC * H], fp16) for h in ("hi", "lo")]
        stage = sb("w_stage", [P, 2, DC * H], fp32)
        x_rows = sb("x_rows", [P, BU, TBT, ROW], fp16)
        xs_t = [sb(f"xs_t_{h}", [P, BU, DC, TB], fp16) for h in ("hi", "lo")]
        act_a = sb("act_a", [P, BU, TB], fp32)
        hid = sb("hid", [P, BU, TB], fp32)
        h_w = [sb(f"h_{h}", [P, BU, TB], fp16) for h in ("hi", "lo")]
        y_sb = sb("y_sb", [P, TBT, D], fp32)
        ident16 = sb("b_ident16", [P, P], fp16)
        eid = sb("eid", [1, NB], mybir.dt.int32)
        pos = sb("pos", [P, TOP, TILES], u32)
        w_top = sb("w_top", [P, TOP, TILES], fp32)

        flat = w_all[1][:, E // 2:, :, :].rearrange("p e k n -> p (e k n)").bitcast(fp32)
        flat0 = w_all[0][:, E // 2:, :, :].rearrange("p e k n -> p (e k n)").bitcast(fp32)
        x1 = flat0[:, 0:TILES * D].rearrange("p (t d) -> p t d", d=D)
        rows = flat[:, 0:TILES * D].bitcast(fp16).rearrange("p (t r) -> p t r", r=ROW)
        shared = sb("shared", [P, (RING * (TOP + 2) + 2) * D], fp32)
        y_in = shared[:, 0:RING * TOP * D].rearrange("p (r k d) -> p r k d", r=RING, k=TOP)
        x_c, o_c = (shared[:, i * RING * D:(i + 1) * RING * D].rearrange("p (r d) -> p r d", r=RING)
                    for i in (TOP, TOP + 1))
        o_h = shared[:, RING * (TOP + 2) * D:].rearrange("p (r d) -> p r d", r=2)
        taken = [0]

        def piece(width):
            taken[0] += width
            assert taken[0] <= RING * (TOP + 2) * D + 2 * D
            return shared[:, taken[0] - width:taken[0]]

        xn = x_rows[:, 0:2, :, :].rearrange("p r q c -> p (r q c)").bitcast(fp32)[:, 0:2 * D].rearrange("p (r d) -> p r d", r=2)
        xn_t = act_a[:, :, :].rearrange("p r d -> p (r d)")[:, 0:2 * D].rearrange("p (r c q) -> p r c q", r=2, c=DC)
        ident = piece(P)
        ones = piece(P)
        tri = piece(P)
        gate_sb = piece(DC * E).rearrange("p (c e) -> p c e", e=E)
        stats = piece(TILES * 6).rearrange("p (t s) -> p t s", s=6)
        mv = piece(TILES * 2).rearrange("p (t s) -> p t s", s=2)
        var, std, rstd, tmp = (piece(TILES) for _ in range(4))
        logits, top, top_i, experts, hot1, hot2, both, cont, tot, incl, rank, mixed = (
            piece(TILES * E) for _ in range(12))
        top_if = piece(TILES * TOP)
        count, blocks, b_incl, b_first, ones_e = (piece(E) for _ in range(5))
        posf = piece(TOP * TILES).rearrange("p (k t) -> p k t", k=TOP)
        iota_b = piece(NB * E)
        eidf = piece(NB)
        by_te = lambda v: v.rearrange("p (t e) -> p t e", e=E)
        by_et = lambda v: v.rearrange("p (e t) -> p e t", e=E)

        s_x1l = [sem(f"b_x1l{i}") for i in range(4)]
        s_gate = sem("b_gate")
        s_const = sem("b_const")
        s_zero = sem("b_zero")
        s_chain = sem("b_chain")
        s_var = sem("b_var")
        s_sqrt = sem("b_sqrt")
        s_xn = sem("b_xn")
        s_xt_ps = sem("b_xt_ps")
        s_xt = sem("b_xt")
        s_lg_ps = sem("b_lg_ps")
        s_rhi = sem("b_rhi")
        s_rlo = sem("b_rlo")
        s_diff = sem("b_diff")
        s_expd = sem("b_expd")
        s_both = sem("b_both")
        s_rank_ps = sem("b_rank_ps")
        s_pos = sem("b_pos")
        s_eid = sem("b_eid")
        s_scat = sem("b_scat")
        s_stage = [sem(f"b_stage{i}") for i in range(2)]
        s_whi = sem("b_whi")
        s_wlo = sem("b_wlo")
        s_xr = [sem(f"b_xr{i}") for i in range(BU)]
        s_tps = sem("b_tps")
        s_txhi = sem("b_txhi")
        s_txlo = sem("b_txlo")
        s_ab = sem("b_ab")
        s_silu = sem("b_silu")
        s_hid = sem("b_hid")
        s_hhi = sem("b_hhi")
        s_hlo = sem("b_hlo")
        s_y_ps = sem("b_y_ps")
        s_y = sem("b_y")
        s_ys = sem("b_ys")
        s_gather = [sem(f"b_gather{i}") for i in range(RING)]
        s_xc = [sem(f"b_xc{i}") for i in range(RING)]
        s_comb = sem("b_comb")
        s_half = sem("b_half")
        s_h_used = sem("b_h_used")
        s_fin = sem("b_fin")

        x1_t = x1_d.rearrange("(t p) d -> p t d", p=P)
        out_t = out.rearrange("(t p) d -> p t d", p=P)
        xs_v = xs_d.rearrange("(q p) r -> p q r", p=P)
        ys_v = ys_d.rearrange("(q p) d -> p q d", p=P)
        W = (w1_t, w3_t, w2_t)
        TERMS = ((0, 0), (0, 1), (1, 0))

        block = ctx.enter_context(nc.Block())

        def passes(eng, step, tail):
            for n in range(BU):
                step(n, 0)
            with eng.Fori(1, NBP - 1) as it:
                for n in range(BU):
                    step(n, it)
            for n in range(BU):
                step(n, NBP - 1)
            tail()

        @block.sync
        def _(sp):
            for i in range(4):
                sp.dma_start(x1[:, 8 * i:8 * i + 8, :], x1_t[:, 8 * i:8 * i + 8, :]).then_inc(s_x1l[i], 16)
            sp.dma_start(gate_sb, gate_t.rearrange("(c p) e -> p c e", p=P)).then_inc(s_gate, 16)
            for i in range(3 * E):
                e, k = divmod(i, 3)
                if i >= 2:
                    sp.wait_ge(s_wlo, i - 1)
                    sp.wait_ge(s_whi, i - 1)
                src = W[k][e].rearrange("(c p) n -> p c n", p=P)
                sp.dma_start(stage[:, i % 2, :].rearrange("p (c n) -> p c n", n=W[k].shape[2]), src
                             ).then_inc(s_stage[i % 2], 16)
            sp.wait_ge(s_scat, 16 * TOP * TILES)

            def step(n, it):
                b = it * BU + n
                src = xs_v[:, bass.ds(b * TBT, TBT), :]
                if not isinstance(b, int):
                    sp.compute_val(src.offset * 2)
                if not (isinstance(it, int) and it == 0):
                    sp.wait_ge(s_tps, b - BU + 1)
                sp.dma_start(x_rows[:, n, :, :], src).then_inc(s_xr[n], 16)

            passes(sp, step, lambda: None)

        @block.gpsimd
        def _(pool):
            pool.memset(ident, 0.0).then_inc(s_const, 1)
            pool.memset(ones, 1.0).then_inc(s_const, 1)
            pool.memset(tri, 1.0).then_inc(s_const, 1)
            pool.memset(cont, 1.0).then_inc(s_const, 1)
            pool.memset(ones_e, 1.0).then_inc(s_const, 1)
            pool.wait_ge(s_const, 5)
            pool.memset(by_et(cont)[:, :, 0:1], 0.0).then_inc(s_const, 1)
            pool.affine_select(out=ident, in_=ident, compare_op=ALU.not_equal, fill=1.0,
                               base=0, pattern=[[-1, P]], channel_multiplier=1).then_inc(s_const, 1)
            pool.affine_select(out=tri, in_=tri, compare_op=ALU.is_gt, fill=0.0,
                               base=0, pattern=[[1, P]], channel_multiplier=-1).then_inc(s_const, 1)
            pool.iota(experts.bitcast(mybir.dt.int32), pattern=[[1, E], [0, TILES]], base=0, channel_multiplier=0
                      ).then_inc(s_const, 1)
            pool.iota(iota_b.bitcast(mybir.dt.int32), pattern=[[1, NB], [0, E]], base=0, channel_multiplier=0
                      ).then_inc(s_const, 1)
            pool.wait_ge(s_const, 10)
            pool.tensor_copy(ident16[:, :], ident).then_inc(s_const, 1)
            pool.tensor_copy(experts, experts.bitcast(mybir.dt.int32)).then_inc(s_const, 1)
            pool.tensor_copy(iota_b, iota_b.bitcast(mybir.dt.int32)).then_inc(s_const, 1)
            for t in range(TILES):
                if t == 0:
                    pool.wait_ge(s_pos, 1)
                    pool.wait_ge(s_rhi, TILES)
                    pool.wait_ge(s_rlo, TILES)
                for k in range(TOP):
                    pool.indirect_dma_start(xs_d, bass.IndirectOffsetOnAxis(ap=pos[:, k, t:t + 1], axis=0),
                                            rows[:, t, :], None).then_inc(s_scat, 16)
            pool.wait_ge(s_ys, 16 * NB)
            for t in range(TILES):
                if t >= RING:
                    pool.wait_ge(s_comb, t - RING + 1)
                for k in range(TOP):
                    pool.indirect_dma_start(y_in[:, t % RING, k, :], None, ys_d,
                                            bass.IndirectOffsetOnAxis(ap=pos[:, k, t:t + 1], axis=0)
                                            ).then_inc(s_gather[t % RING], 16)

        @block.tensor
        def _(pe):
            pe.wait_ge(s_const, 13)
            pe.wait_ge(s_gate, 16)
            for t in range(TILES + 1):
                if t < TILES:
                    pe.wait_ge(s_xn, t + 1)
                    if t >= 2:
                        pe.wait_ge(s_xt, t - 1)
                    for c in range(DC):
                        last = pe.transpose(ps_t[t % 2][:, c * P:(c + 1) * P], xn[:, t % 2, c * P:(c + 1) * P], ident)
                    last.then_inc(s_xt_ps, 1)
                if t >= 1:
                    pe.wait_ge(s_xt, t)
                    for c in range(DC):
                        last = pe.matmul(ps_c[:, (t - 1) * E:t * E], xn_t[:, (t - 1) % 2, c, :], gate_sb[:, c, :],
                                         start=(c == 0), stop=(c == DC - 1))
                    last.then_inc(s_lg_ps, 1)
            pe.wait_ge(s_both, 1)
            pe.matmul(ps_t[0][:, 0:TILES * E], tri, both, start=True, stop=True)
            pe.matmul(ps_t[1][:, 0:TILES * E], ones, both, start=True, stop=True).then_inc(s_rank_ps, 1)
            pe.wait_ge(s_pos, 1)
            pe.wait_ge(s_eid, 1)
            pe.wait_ge(s_whi, 3 * E)
            pe.wait_ge(s_wlo, 3 * E)

            def transposes(n, b):
                for h in range(2):
                    if not (isinstance(b, int) and b == 0):
                        pe.wait_ge(s_txhi, b)
                        pe.wait_ge(s_txlo, b)
                    dst = ps_t[h][:, :].bitcast(fp16)
                    for c in range(DC):
                        for q in range(TBT):
                            at = c * TB + q * P
                            last = pe.transpose(dst[:, at:at + P],
                                                x_rows[:, n % BU, q, h * D + c * P:h * D + (c + 1) * P], ident16[:, :])
                last.then_inc(s_tps, 1)

            def expert(b):
                return pe.value_load(eid[0:1, bass.ds(b, 1)], min_val=0, max_val=E - 1)

            def first(n, b, hc, e):
                k = b * HC + hc
                if not (isinstance(b, int) and b == 0 and hc < BU):
                    pe.wait_ge(s_hid, k - BU + 1)
                for i, which in enumerate((0, 1)):
                    terms = [(c, a, w) for c in range(DC) for w, a in TERMS]
                    for j, (c, a, w) in enumerate(terms):
                        at = c * H + hc * P
                        last = pe.matmul(ps_ab[hc % BU][:, i, :],
                                         w_all[w][:, bass.ds(e, 1), which, at:at + P].rearrange("p e n -> p (e n)"),
                                         xs_t[a][:, n % BU, c, :], start=(j == 0), stop=(j == len(terms) - 1))
                last.then_inc(s_ab, 1)

            def second(b, hc, e):
                k = b * HC + hc
                if hc == 0 and not (isinstance(b, int) and b == 0):
                    pe.wait_ge(s_y, b)
                pe.wait_ge(s_hhi, k + 1)
                pe.wait_ge(s_hlo, k + 1)
                for q in range(TBT):
                    for a, w in TERMS:
                        last = pe.matmul(ps_y[q][:, 0:D], h_w[a][:, hc % BU, q * P:(q + 1) * P],
                                         w_all[w][:, bass.ds(e, 1), 2, hc * D:(hc + 1) * D].rearrange("p e n -> p (e n)"),
                                         start=(hc == 0 and (a, w) == TERMS[0]),
                                         stop=(hc == HC - 1 and (a, w) == TERMS[-1]))
                if hc == HC - 1:
                    last.then_inc(s_y_ps, 1)
                else:
                    last.then_inc(s_h_used, 1)

            pe.wait_ge(s_xr[0], 16)
            transposes(0, 0)

            held = [None]

            def step(n, it):
                b = it * BU + n
                e = expert(b)
                if n == 0 and not (isinstance(it, int) and it == 0):
                    held[0] = expert(b - 1)
                pe.wait_ge(s_txhi, b + 1)
                pe.wait_ge(s_txlo, b + 1)
                for hc in range(HC):
                    first(n, b, hc, e)
                    if hc >= S2_LAG:
                        second(b, hc - S2_LAG, e)
                    elif not (isinstance(b, int) and b == 0):
                        second(b - 1, HC - S2_LAG + hc, held[0])
                    if hc == 3 and not (isinstance(b, int) and b + 1 == NB):
                        pe.wait_ge(s_xr[(n + 1) % BU], (it + (n + 1) // BU) * 16 + 16)
                        transposes(n + 1, b + 1)
                held[0] = e

            def tail():
                for hc in range(HC - S2_LAG, HC):
                    second(NB - 1, hc, held[0])

            passes(pe, step, tail)

        @block.scalar
        def _(act):
            act.wait_ge(s_var, 1)
            act.activation(std, var, ACT.Sqrt).then_inc(s_sqrt, 1)
            for t in range(TILES):
                act.wait_ge(s_xn, t + 1)
                act.activation(rows[:, t, 0:D], xn[:, t % 2, :], ACT.Copy).then_inc(s_rhi, 1)
                act.wait_ge(s_xt_ps, t + 1)
                if t >= 2:
                    act.wait_ge(s_lg_ps, t - 1)
                act.activation(xn_t[:, t % 2, :, :], ps_t[t % 2][:, 0:D].rearrange("p (c q) -> p c q", c=DC),
                               ACT.Copy).then_inc(s_xt, 1)
            act.wait_ge(s_diff, 1)
            act.activation(w_top[:, 1, :], w_top[:, 0, :], ACT.Exp).then_inc(s_expd, 1)
            for i in range(3 * E):
                e, k = divmod(i, 3)
                act.wait_ge(s_stage[i % 2], 16 * (i // 2 + 1))
                if e == E // 2:
                    act.wait_ge(s_scat, 16 * TOP * TILES)
                    act.wait_ge(s_eid, 1)
                act.activation(w_all[0][:, e, k, :], stage[:, i % 2, :], ACT.Copy, scale=W_SCALE).then_inc(s_whi, 1)

            def x_high(b, n):
                act.wait_ge(s_tps, b + 1)
                act.activation(xs_t[0][:, n % BU, :, :], ps_t[0][:, :].bitcast(fp16)[:, 0:DC * TB]
                               .rearrange("p (c q) -> p c q", c=DC), ACT.Copy).then_inc(s_txhi, 1)

            def y_out(b):
                act.wait_ge(s_y_ps, b + 1)
                if not (isinstance(b, int) and b == 0):
                    act.wait_ge(s_ys, b * 16)
                for q in range(TBT):
                    last = act.activation(y_sb[:, q, :], ps_y[q][:, 0:D], ACT.Copy, scale=Y_INV)
                last.then_inc(s_y, 1)
                act.wait_ge(s_y, b + 1)
                act.dma_start(ys_v[:, bass.ds(b * TBT, TBT), :], y_sb[:, :, :]).then_inc(s_ys, 16)

            def silu(b, hc):
                k = b * HC + hc
                act.wait_ge(s_ab, k + 1)
                act.activation(act_a[:, hc % BU, :], ps_ab[hc % BU][:, 0, :], ACT.Silu, scale=A_INV).then_inc(s_silu, 1)

            def high(b, hc):
                k = b * HC + hc
                act.wait_ge(s_hid, k + 1)
                if not (isinstance(b, int) and b == 0 and hc < BU):
                    if hc < BU:
                        act.wait_ge(s_h_used, b * (HC - 1) - (BU - 1) + hc if hc < BU - 1 else b * (HC - 1))
                        if hc == BU - 1:
                            act.wait_ge(s_y_ps, b)
                    else:
                        act.wait_ge(s_h_used, b * (HC - 1) + hc - BU + 1)
                act.activation(h_w[0][:, hc % BU, :], hid[:, hc % BU, :], ACT.Copy).then_inc(s_hhi, 1)

            x_high(0, 0)

            def step(n, it):
                b = it * BU + n
                for hc in range(HC):
                    silu(b, hc)
                    if hc >= 1:
                        high(b, hc - 1)
                    elif not (isinstance(b, int) and b == 0):
                        high(b - 1, HC - 1)
                    if hc == 2 and not (isinstance(b, int) and b == 0):
                        y_out(b - 1)
                    if hc == 4 and not (isinstance(b, int) and b + 1 == NB):
                        x_high(b + 1, n + 1)

            def tail():
                high(NB - 1, HC - 1)
                y_out(NB - 1)

            passes(act, step, tail)
            act.wait_ge(s_ys, 16 * NB)
            for t in range(TILES):
                if t >= RING:
                    act.wait_ge(s_comb, t - RING + 1)
                act.dma_start(x_c[:, t % RING, :], x1_t[:, t, :]).then_inc(s_xc[t % RING], 16)
                if t >= 2:
                    act.wait_ge(s_comb, t - 1)
                    act.dma_start(out_t[:, t - 2, :], o_c[:, (t - 2) % RING, :]).then_inc(s_fin, 16)
            for t in range(TILES - 2, TILES):
                act.wait_ge(s_comb, t + 1)
                act.dma_start(out_t[:, t, :], o_c[:, t % RING, :]).then_inc(s_fin, 16)
            act.wait_ge(s_fin, 16 * TILES)

        @block.vector
        def _(dve):
            chain = [0]

            def link(ins):
                chain[0] += 1
                ins.then_inc(s_chain, 1)
                dve.wait_ge(s_chain, chain[0])

            for t in range(TILES):
                if t % 8 == 0:
                    dve.wait_ge(s_x1l[t // 8], 16)
                last = dve.bn_stats(stats[:, t, :], x1[:, t, :])
            link(last)
            for t in range(TILES):
                last = dve.bn_aggr(mv[:, t, :], stats[:, t, :])
            link(last)
            dve.tensor_scalar(var, mv[:, :, 1], EPS, None, ALU.add).then_inc(s_var, 1)
            dve.wait_ge(s_sqrt, 1)
            link(dve.reciprocal(rstd, std))
            link(dve.tensor_tensor(tmp, rstd, rstd, ALU.mult))
            link(dve.tensor_tensor(tmp, tmp, var, ALU.mult))
            link(dve.tensor_scalar(tmp, tmp, -0.5, 1.5, ALU.mult, ALU.add))
            link(dve.tensor_tensor(rstd, rstd, tmp, ALU.mult))
            for t in range(TILES):
                if t >= 2:
                    dve.wait_ge(s_rhi, t - 1)
                    dve.wait_ge(s_rlo, t - 1)
                    dve.wait_ge(s_xt_ps, t - 1)
                dve.tensor_scalar(xn[:, t % 2, :], x1[:, t, :], mv[:, t, 0:1], rstd[:, t:t + 1],
                                  ALU.subtract, ALU.mult).then_inc(s_xn, 1)
                dve.wait_ge(s_xn, t + 1)
                dve.wait_ge(s_rhi, t + 1)
                dve.tensor_tensor(rows[:, t, D:ROW], xn[:, t % 2, :], rows[:, t, 0:D], ALU.subtract
                                  ).then_inc(s_rlo, 1)
            dve.wait_ge(s_lg_ps, TILES)
            link(dve.tensor_copy(logits, ps_c[:, 0:TILES * E]))
            for t in range(TILES):
                last = dve.max(by_te(top)[:, t, :], by_te(logits)[:, t, :])
            link(last)
            for t in range(TILES):
                last = dve.max_index(by_te(top_i).bitcast(u32)[:, t, :], by_te(top)[:, t, :], by_te(logits)[:, t, :])
            link(last)
            dve.tensor_tensor(w_top[:, 0, :], by_te(top)[:, :, 1], by_te(top)[:, :, 0], ALU.subtract
                              ).then_inc(s_diff, 1)
            top_k = top_if.rearrange("p (k t) -> p k t", k=TOP)
            link(dve.tensor_copy(top_k, by_te(top_i).bitcast(u32)[:, :, 0:TOP].rearrange("p t k -> p k t")))
            dve.wait_ge(s_const, 13)
            for k, hot in enumerate((hot1, hot2)):
                last = dve.tensor_tensor(by_et(hot), top_k[:, k, None, :].to_broadcast([P, E, TILES]), by_et(experts),
                                         ALU.is_equal)
            link(last)
            dve.tensor_tensor(both, hot1, hot2, ALU.add).then_inc(s_both, 1)
            dve.wait_ge(s_expd, 1)
            link(dve.tensor_scalar(tmp, w_top[:, 1, :], 1.0, None, ALU.add))
            link(dve.reciprocal(w_top[:, 0, :], tmp))
            link(dve.tensor_tensor(w_top[:, 1, :], w_top[:, 1, :], w_top[:, 0, :], ALU.mult))
            dve.wait_ge(s_rank_ps, 1)
            link(dve.tensor_copy(tot, ps_t[1][:, 0:TILES * E]))
            link(dve.tensor_tensor_scan(incl, cont, tot, 0.0, ALU.mult, ALU.add))
            link(dve.tensor_scalar(count, by_et(incl)[:, :, TILES - 1], 1.0 / TB,
                                   (TB - 1.0) / TB - 0.5 + 0.5 / TB, ALU.mult, ALU.add))
            ROUND = 1.5 * 2.0 ** 23
            link(dve.tensor_scalar(blocks, count, ROUND, ROUND, ALU.add, ALU.subtract))
            link(dve.tensor_tensor_scan(b_incl, ones_e, blocks, 0.0, ALU.mult, ALU.add))
            link(dve.tensor_tensor(b_first, b_incl, blocks, ALU.subtract))
            link(dve.tensor_scalar(b_first, b_first, float(TB), None, ALU.mult))
            link(dve.tensor_tensor(rank, incl, tot, ALU.subtract))
            link(dve.tensor_tensor(rank, ps_t[0][:, 0:TILES * E], rank, ALU.add))
            link(dve.tensor_tensor(by_et(rank), by_et(rank), b_first[:, :, None].to_broadcast([P, E, TILES]), ALU.add))
            for k, hot in enumerate((hot1, hot2)):
                link(dve.tensor_tensor(mixed, rank, hot, ALU.mult))
                link(dve.tensor_reduce(posf[:, k, :], by_et(mixed).rearrange("p e t -> p t e"), axis=AX.X, op=ALU.add))
            dve.tensor_copy(pos[:, :, :], posf).then_inc(s_pos, 1)
            each = iota_b[0:1, :].rearrange("p (b e) -> p b e", e=E)
            link(dve.tensor_tensor(each, each, b_incl[0:1, None, :].to_broadcast([1, NB, E]), ALU.is_ge))
            link(dve.tensor_reduce(eidf[0:1, :], each, axis=AX.X, op=ALU.add))
            link(dve.tensor_scalar(eidf[0:1, :], eidf[0:1, :], E - 1.0, None, ALU.min))
            dve.tensor_copy(eid[:, :], eidf[0:1, :]).then_inc(s_eid, 1)

            for i in range(3 * E):
                e, k = divmod(i, 3)
                dve.wait_ge(s_whi, i + 1)
                dve.scalar_tensor_tensor(w_all[1][:, e, k, :], stage[:, i % 2, :], W_SCALE, w_all[0][:, e, k, :],
                                         ALU.mult, ALU.subtract).then_inc(s_wlo, 1)

            def x_low(b, n):
                dve.wait_ge(s_tps, b + 1)
                dve.tensor_copy(xs_t[1][:, n % BU, :, :], ps_t[1][:, :].bitcast(fp16)[:, 0:DC * TB]
                                .rearrange("p (c q) -> p c q", c=DC)).then_inc(s_txlo, 1)

            def hidden(b, hc):
                k = b * HC + hc
                dve.wait_ge(s_silu, k + 1)
                if not (isinstance(b, int) and b == 0 and hc < BU):
                    dve.wait_ge(s_hhi, k - BU + 1)
                    dve.wait_ge(s_hlo, k - BU + 1)
                dve.scalar_tensor_tensor(hid[:, hc % BU, :], act_a[:, hc % BU, :], H_SCALE, ps_ab[hc % BU][:, 1, :],
                                         ALU.mult, ALU.mult).then_inc(s_hid, 1)

            def low(b, hc):
                k = b * HC + hc
                dve.wait_ge(s_hhi, k + 1)
                dve.tensor_tensor(h_w[1][:, hc % BU, :], hid[:, hc % BU, :], h_w[0][:, hc % BU, :], ALU.subtract
                                  ).then_inc(s_hlo, 1)

            x_low(0, 0)

            def step(n, it):
                b = it * BU + n
                for hc in range(HC):
                    hidden(b, hc)
                    if hc >= 1:
                        low(b, hc - 1)
                    elif not (isinstance(b, int) and b == 0):
                        low(b - 1, HC - 1)
                    if hc == 4 and not (isinstance(b, int) and b + 1 == NB):
                        x_low(b + 1, n + 1)

            passes(dve, step, lambda: low(NB - 1, HC - 1))

            for t in range(TILES):
                dve.wait_ge(s_gather[t % RING], 32 * (t // RING + 1))
                dve.wait_ge(s_xc[t % RING], 16 * (t // RING + 1))
                if t >= RING:
                    dve.wait_ge(s_fin, 16 * (t - RING + 1))
                dve.scalar_tensor_tensor(o_h[:, t % 2, :], y_in[:, t % RING, 0, :], w_top[:, 0, t:t + 1],
                                         x_c[:, t % RING, :], ALU.mult, ALU.add).then_inc(s_half, 1)
                dve.wait_ge(s_half, t + 1)
                dve.scalar_tensor_tensor(o_c[:, t % RING, :], y_in[:, t % RING, 1, :], w_top[:, 1, t:t + 1],
                                         o_h[:, t % 2, :], ALU.mult, ALU.add).then_inc(s_comb, 1)


def kernel(**inputs):
    import numpy as np
    import concourse.bacc as bacc
    from concourse.bass_utils import run_bass_kernel_spmd

    nc = bacc.Bacc("TRN2", target_bir_lowering=False, num_devices=1)
    laid_out = {
        "x": inputs["x"],
        "adj": inputs["adj"],
        "wq": inputs["L0_gnn_Wq"],
        "wk": inputs["L0_gnn_Wk"],
        "wv_t": np.asarray(inputs["L0_gnn_Wv"]).T,
        "gate_t": np.asarray(inputs["L0_ffn_gate_w"]).T,
        "w1_t": np.asarray(inputs["L0_ffn_w1"]).transpose(0, 2, 1),
        "w3_t": np.asarray(inputs["L0_ffn_w3"]).transpose(0, 2, 1),
        "w2_t": np.asarray(inputs["L0_ffn_w2"]).transpose(0, 2, 1),
    }
    arrays, args = {}, []
    for name, a in laid_out.items():
        a = np.ascontiguousarray(a)
        arrays[f"in_{name}"] = a
        args.append(nc.dram_tensor(f"in_{name}", a.shape, mybir.dt.from_np(a.dtype), kind="ExternalInput").ap())
    args.append(nc.dram_tensor("out_0", laid_out["x"].shape, mybir.dt.float32, kind="ExternalOutput").ap())
    gnn_moe(nc, *args)
    return run_bass_kernel_spmd(nc, [arrays], core_ids=[0]).results[0]["out_0"]
```

```python
import concourse.bass as bass
from concourse import mybir
from contextlib import ExitStack

fp32 = mybir.dt.float32
fp16 = mybir.dt.float16
bf16 = mybir.dt.bfloat16
u8 = mybir.dt.uint8
u32 = mybir.dt.uint32
i32 = mybir.dt.int32
ALU = mybir.AluOpType
ACT = mybir.ActivationFunctionType
AX = mybir.AxisListType
RMAX = bass.bass_isa.ReduceOp.max

P = 128
EPS = 1e-5
TOP = 2
TERMS = ((0, 0), (0, 1), (1, 0))
TB = 256
TBT = TB // P


def before_start(v):
    return isinstance(v, int) and v < 0


def gnn_moe(nc, x, adj, wq, wk, wv_t, gate_t, w1_t, w3_t, w2_t, out):
    N, D = x.shape
    E = w1_t.shape[0]
    TILES = N // P
    REGION = N + TB
    NB = TOP * N // TB + E - 1
    x1_d = nc.dram_tensor("x1_d", (N, D), fp32, kind="Internal").ap()
    xs_d = nc.dram_tensor("xs_d", (E * REGION, 2 * D), fp16, kind="Internal").ap()
    ys_d = nc.dram_tensor("ys_d", (NB * TB, D), fp32, kind="Internal").ap()
    with ExitStack() as ctx:
        def sb(name, shape, dt):
            return ctx.enter_context(nc.sbuf_tensor(name, shape, dt))

        kept = {
            "place": sb("place", [P, TOP, TILES], fp32),
            "chosen": sb("chosen", [P, TOP, TILES], fp32),
            "logit": sb("logit", [P, TOP, TILES], fp32),
            "next_row": sb("next_row", [P, E], fp32),
            "expert_ids": sb("expert_ids", [P, E], fp32),
            "ident16": sb("ident16", [P, P], fp16),
        }
        attention(nc, x, adj, wq, wk, wv_t, gate_t, x1_d, xs_d, ys_d, kept, E, REGION)
        experts(nc, w1_t, w3_t, w2_t, x1_d, xs_d, ys_d, out, kept, REGION, NB)


def attention(nc, x, adj, wq, wk, wv_t, gate_t, x1_d, xs_d, ys_d, kept, E, REGION):
    N, D = x.shape
    DC = D // P
    TILES = N // P
    QB = 256
    QT = QB // P
    BLOCKS = N // QB
    KT = 4
    GROUPS = TILES // KT
    STEPS = BLOCKS * GROUPS
    GW = KT * QB
    SLOTS = 2 * GROUPS
    PASSES = STEPS // SLOTS
    PEELED = 2
    SUB_LAG = GROUPS + 2
    LO_LAG = SUB_LAG + 1
    PV_LAG = SUB_LAG + 2
    DRAIN = 2 * GROUPS + 5
    RING = 4
    BIG = 1.0e30
    VW = D + 1
    VP = VW + 1
    ROW = 2 * D
    FILLS = 6

    ctx = ExitStack()
    with ctx:
        def sb(name, shape, dt):
            return ctx.enter_context(nc.sbuf_tensor(name, shape, dt))

        def pb(name, shape):
            return ctx.enter_context(nc.psum_tensor(name, shape, fp32))

        def sem(name):
            return ctx.enter_context(nc.semaphore(name))

        ps_s = [pb(f"ps_scores{i}", [P, KT, QB]) for i in range(2)]
        ps_out = pb("ps_out", [P, QT, 512])
        ps_misc = pb("ps_misc", [P, 2, 512])
        ps_o = [ps_out[:, q, :] for q in range(QT)]
        ps_a, ps_b = ps_misc[:, 0, :], ps_misc[:, 1, :]

        kT = [sb(f"kT_{h}", [P, DC, N], fp16) for h in ("hi", "lo")]
        val = [sb(f"val_{h}", [P, TILES, VP], fp16) for h in ("hi", "lo")]
        m_w = [sb(f"m_{h}", [P, DC, D], fp16) for h in ("hi", "lo")]
        q_t = [sb(f"qT_{h}", [P, 2, DC, QB], fp16) for h in ("hi", "lo")]
        ident = sb("ident", [P, P], fp32)
        ident16 = kept["ident16"]
        ones = sb("ones", [P, P], fp32)
        tri = sb("tri", [P, P], fp32)
        scales = sb("scales", [P, 8], fp32)
        adj_sb = sb("adj_sb", [P, GROUPS, KT, 2 * QB], u8)
        mask = sb("mask", [P, 2, GW], bf16)
        t_sb = sb("t_sb", [P, SLOTS, GW], fp32)
        run_max = sb("run_max", [P, 2, GW], fp32)
        m_col = sb("m_col", [P, QT], fp32)
        diag = sb("diag", [P, QT, P], fp32)
        m_row = sb("m_row", [P, 2, QB], fp32)
        e_sb = sb("e_sb", [P, 2, GW], fp32)
        p_hi = sb("p_hi", [P, RING, GW], fp16)
        p_lo = sb("p_lo", [P, RING, GW], fp16)
        den = sb("den", [P, 3, QT], fp32)
        x_io = sb("x_io", [P, 2, QT, D], fp32)
        stats2 = sb("stats2", [P, QT, 6], fp32)
        mv2 = sb("mv2", [P, QT, 2], fp32)
        rstd2 = sb("rstd2", [P, 2, QT], fp32)
        xn2 = sb("xn2", [P, QT, D], fp32)
        xn2_t = sb("xn2_t", [P, QT, DC, P], fp32)
        rows = sb("rows", [P, 2, QT, ROW], fp16)
        gate_sb = sb("gate_sb", [P, DC, E], fp32)
        logits = sb("logits", [P, QT, E], fp32)
        top = sb("top", [P, QT, E], fp32)
        top_i = sb("top_i", [P, QT, E], u32)
        hot = sb("hot", [P, TOP, QT, E], fp32)
        both = sb("both", [P, QT, E], fp32)
        rank = sb("rank", [P, QT, E], fp32)
        mixed = sb("mixed", [P, TOP, QT, E], fp32)
        picked = sb("picked", [P, TOP, QT], fp32)
        put = sb("put", [P, TOP, QT], fp32)
        place_u = sb("place_u", [P, 2, TOP, QT], u32)
        end_row = sb("end_row", [1, E], i32)
        zero = sb("zero", [P, ROW], fp16)
        powers = sb("powers", [P, KT], fp32)

        flat = t_sb[:, :, :].rearrange("p s w -> p (s w)")
        taken = [0]

        def early(width, dt=fp32):
            words = width if dt == fp32 else width // 2
            piece = flat[:, taken[0]:taken[0] + words]
            taken[0] += words
            return piece if dt == fp32 else piece.bitcast(dt)

        x_all = early(TILES * D).rearrange("p (t d) -> p t d", d=D)
        wq_sb = early(DC * D).rearrange("p (c d) -> p c d", c=DC)
        wk_sb = early(DC * D).rearrange("p (c d) -> p c d", c=DC)
        wv_sb = early(DC * D).rearrange("p (c d) -> p c d", c=DC)
        wv_w = [early(DC * D, fp16).rearrange("p (c d) -> p c d", c=DC) for _ in range(2)]
        xn = early(KT * D).rearrange("p (s d) -> p s d", s=KT)
        xn_w = [early(2 * KT * D, fp16).rearrange("p (r s d) -> p r s d", r=2, s=KT) for _ in range(2)]
        stats = early(TILES * 6).rearrange("p (t s) -> p t s", s=6)
        mv = early(TILES * 2).rearrange("p (t s) -> p t s", s=2)
        var = early(TILES)
        rstd = early(TILES)
        amax = early(2)
        amax_all = early(2)
        assert taken[0] <= SLOTS * GW

        INV_M, INV_V, S_M, S_V, EXP_SCALE, OUT_SCALE = range(6)

        def col(i):
            return scales[:, i:i + 1]

        tr_ps = [[ps_s[i][:, 2 * h:2 * h + 2, :].rearrange("p a b -> p (a b)").bitcast(fp16)
                  .rearrange("p (c q) -> p c q", c=DC) for h in range(2)] for i in range(2)]
        v_ps = [t[:, :, :].rearrange("p a (b d) -> p (a b) d", d=D) for t in (ps_out, ps_misc)]

        s_x_load = [sem(f"s_x_load{i}") for i in range(GROUPS)]
        s_w = sem("s_w")
        s_gate = sem("s_gate")
        s_const = sem("s_const")
        s_stats = sem("s_stats")
        s_mv = sem("s_mv")
        s_var = sem("s_var")
        s_rstd = sem("s_rstd")
        s_chain = sem("s_chain")
        s_m_ps = sem("s_m_ps")
        s_amax = sem("s_amax")
        s_amax_all = sem("s_amax_all")
        s_scale = sem("s_scale")
        s_whi = sem("s_whi")
        s_wlo = sem("s_wlo")
        s_xn = sem("s_xn")
        s_xhi = sem("s_xhi")
        s_xlo = sem("s_xlo")
        s_tr = sem("s_tr")
        s_khi = sem("s_khi")
        s_klo = sem("s_klo")
        s_v_ps = sem("s_v_ps")
        s_vhi = sem("s_vhi")
        s_vlo = sem("s_vlo")
        s_adj = [sem(f"s_adj{g}") for g in range(GROUPS)]
        s_mask = sem("s_mask")
        s_q_ps = sem("s_q_ps")
        s_qhi = sem("s_qhi")
        s_qlo = sem("s_qlo")
        s_scores = sem("s_scores")
        s_evac = sem("s_evac")
        s_max = sem("s_max")
        s_max_t = sem("s_max_t")
        s_mcol = sem("s_mcol")
        s_diag = sem("s_diag")
        s_mrow_ps = sem("s_mrow_ps")
        s_mrow = sem("s_mrow")
        s_sub = sem("s_sub")
        s_exp = sem("s_exp")
        s_phi = sem("s_phi")
        s_plo = sem("s_plo")
        s_pv = sem("s_pv")
        s_den = sem("s_den")
        s_x1 = sem("s_x1")
        s_xin = [sem(f"s_xin{i}") for i in range(2)]
        s_x1_out = [sem(f"s_x1_out{i}") for i in range(2)]
        s_stats2 = sem("s_stats2")
        s_mv2 = sem("s_mv2")
        s_var2 = sem("s_var2")
        s_rstd2 = sem("s_rstd2")
        s_xn2 = sem("s_xn2")
        s_rhi = sem("s_rhi")
        s_rlo = sem("s_rlo")
        s_xn2_ps = sem("s_xn2_ps")
        s_xn2_t = sem("s_xn2_t")
        s_logit_ps = sem("s_logit_ps")
        s_both = sem("s_both")
        s_rank_ps = sem("s_rank_ps")
        s_pick = sem("s_pick")
        s_put = sem("s_put")
        s_place = sem("s_place")
        s_route = sem("s_route")
        s_scatter = [sem(f"s_scatter{i}") for i in range(2)]
        s_end_row = sem("s_end_row")
        s_pad = sem("s_pad")
        s_fill = sem("s_fill")

        x_t = x.rearrange("(t p) d -> p t d", p=P)
        x1_t = x1_d.rearrange("(t p) d -> p t d", p=P)
        adj_t = adj.rearrange("(g s p) i -> p g s i", p=P, s=KT)

        def alive(b):
            return not isinstance(b, int) or 0 <= b < BLOCKS

        def alive_step(at):
            return not isinstance(at, int) or 0 <= at < STEPS

        def passes(eng, step):
            for it in range(PEELED):
                for n in range(SLOTS):
                    step(n, it)
            with eng.Fori(PEELED, PASSES - 1) as it:
                for n in range(SLOTS):
                    step(n, it)
            for n in range(SLOTS):
                step(n, PASSES - 1)
            for n in range(DRAIN):
                step(n, PASSES)

        def where(n, it):
            return it * SLOTS + n, it * (SLOTS // GROUPS) + n // GROUPS, n % GROUPS

        block = ctx.enter_context(nc.Block())

        @block.sync
        def _(sp):
            for i in range(GROUPS):
                sp.dma_start(x_all[:, KT * i:KT * (i + 1), :], x_t[:, KT * i:KT * (i + 1), :]
                             ).then_inc(s_x_load[i], 16)
                if i == 0:
                    sp.dma_start(wq_sb, wq.rearrange("(c p) d -> p c d", p=P)).then_inc(s_w, 16)
                    sp.dma_start(wk_sb, wk.rearrange("(c p) d -> p c d", p=P)).then_inc(s_w, 16)
                    sp.dma_start(wv_sb, wv_t.rearrange("(c p) d -> p c d", p=P)).then_inc(s_w, 16)
            sp.dma_start(gate_sb[:, :, :], gate_t.rearrange("(c p) e -> p c e", p=P)).then_inc(s_gate, 16)
            for g in range(GROUPS):
                sp.dma_start(adj_sb[:, g, :, :], adj_t[:, g, :, 0:2 * QB]).then_inc(s_adj[g], 16)
            for r in range(2):
                sp.dma_start(x_io[:, r, :, :], x_t[:, r * QT:r * QT + QT, :]).then_inc(s_xin[r], 16)

            sp.wait_ge(s_const, 7)
            fill = ys_d.rearrange("(a q p) d -> p a q d", p=P, a=FILLS)
            for i in range(FILLS):
                sp.dma_start(fill[:, i, :, :], zero[:, :].bitcast(fp32)[:, None, :]
                             .to_broadcast([P, ys_d.shape[0] // P // FILLS, D])).then_inc(s_fill, 16)

            def one_pass(it):
                adj_src = [adj_t[:, g, :, bass.ds(it * (2 * QB), 2 * QB)] for g in range(GROUPS)]
                x_src = [x_t[:, bass.ds(it * (2 * QT) + r * QT, QT), :] for r in range(2)]
                x1_dst = [x1_t[:, bass.ds(it * (2 * QT) - (2 - r) * QT, QT), :] for r in range(2)]
                if not isinstance(it, int):
                    for ap in adj_src:
                        sp.compute_val(ap.offset)
                    for ap in x_src + x1_dst:
                        sp.compute_val(ap.offset * 4)
                for g in range(GROUPS):
                    sp.wait_ge(s_mask, it * SLOTS - GROUPS + g + 1)
                    sp.dma_start(adj_sb[:, g, :, :], adj_src[g]).then_inc(s_adj[g], 16)
                for r in range(2):
                    sp.wait_ge(s_x1, it * 2 - 1 + r)
                    sp.dma_start(x1_dst[r], x_io[:, r, :, :]).then_inc(s_x1_out[r], 16)
                    sp.wait_ge(s_xn2, it * 2 - 1 + r)
                    sp.wait_ge(s_x1_out[r], it * 16)
                    sp.dma_start(x_io[:, r, :, :], x_src[r]).then_inc(s_xin[r], 16)

            with sp.Fori(1, PASSES) as it:
                one_pass(it)
            for r in range(2):
                sp.wait_ge(s_x1, BLOCKS - 1 + r)
                at = TILES - (2 - r) * QT
                sp.dma_start(x1_t[:, at:at + QT, :], x_io[:, r, :, :]).then_inc(s_x1_out[r], 16)
            sp.wait_ge(s_const, 7)
            sp.wait_ge(s_end_row, 1)
            for e in range(E):
                end = sp.value_load(end_row[0:1, e:e + 1], min_val=e * REGION, max_val=e * REGION + N)
                sp.dma_start(xs_d[bass.ds(end, TB), :].rearrange("(q p) r -> p q r", p=P),
                             zero[:, None, :].to_broadcast([P, TBT, ROW])).then_inc(s_pad, 16)
            for r in range(2):
                sp.wait_ge(s_x1_out[r], 16 * BLOCKS // 2)
            sp.wait_ge(s_pad, 16 * E)
            sp.wait_ge(s_fill, 16 * FILLS)

        @block.gpsimd
        def _(pool):
            pool.memset(ident[:, :], 0.0).then_inc(s_const, 1)
            pool.memset(ones[:, :], 1.0).then_inc(s_const, 1)
            pool.memset(tri[:, :], 1.0).then_inc(s_const, 1)
            pool.memset(powers[:, :], -0.5).then_inc(s_const, 1)
            pool.memset(val[0][:, :, D:VP], 1.0).then_inc(s_const, 1)
            pool.memset(val[1][:, :, D:VP], 0.0).then_inc(s_const, 1)
            pool.memset(zero[:, :], 0.0).then_inc(s_const, 1)
            pool.wait_ge(s_const, 7)
            pool.affine_select(out=ident[:, :], in_=ident[:, :], compare_op=ALU.not_equal, fill=1.0,
                               base=0, pattern=[[-1, P]], channel_multiplier=1).then_inc(s_const, 1)
            pool.affine_select(out=tri[:, :], in_=tri[:, :], compare_op=ALU.is_gt, fill=0.0,
                               base=0, pattern=[[1, P]], channel_multiplier=-1).then_inc(s_const, 1)
            pool.iota(kept["expert_ids"][:, :].bitcast(i32), pattern=[[1, E]], base=0, channel_multiplier=0
                      ).then_inc(s_const, 1)
            pool.iota(kept["next_row"][:, :].bitcast(i32), pattern=[[REGION, E]], base=0, channel_multiplier=0
                      ).then_inc(s_const, 1)
            pool.wait_ge(s_const, 11)
            pool.tensor_copy(ident16[:, :], ident[:, :]).then_inc(s_const, 1)
            pool.tensor_copy(kept["expert_ids"][:, :], kept["expert_ids"][:, :].bitcast(i32)).then_inc(s_const, 1)
            pool.tensor_copy(kept["next_row"][:, :], kept["next_row"][:, :].bitcast(i32)).then_inc(s_const, 1)

            def inverse_root(dst, src, tmp, ready, s_sum, s_done, n):
                if not isinstance(n, int):
                    pool.compute_val(n)
                pool.wait_ge(s_const, 14)
                pool.wait_ge(ready, n)
                pool.tensor_scalar(tmp, src, EPS, 1.0, ALU.add, ALU.mult).then_inc(s_sum, 1)
                pool.wait_ge(s_sum, n)
                pool.tensor_tensor(dst, tmp, powers[:, 0:dst.shape[1]], ALU.pow).then_inc(s_done, 1)

            def first_norm(i):
                cut = slice(i * KT, (i + 1) * KT)
                inverse_root(rstd[:, cut], mv[:, cut, 1], var[:, cut], s_mv, s_var, s_rstd, i + 1)

            first_norm(0)
            first_norm(1)
            pool.wait_ge(s_amax, 2)
            pool.partition_all_reduce(amax_all, amax, P, RMAX).then_inc(s_amax_all, 1)
            for i in range(2, GROUPS):
                first_norm(i)

            def second_norm(b):
                if not before_start(b - 1):
                    pool.wait_ge(s_xn2, b)
                inverse_root(rstd2[:, 0, :], mv2[:, :, 1], rstd2[:, 1, :], s_mv2, s_var2, s_rstd2, b + 1)

            def scatter(b, r):
                pool.wait_ge(s_const, 14)
                pool.wait_ge(s_route, b + 1)
                pool.wait_ge(s_rhi, b + 1)
                pool.wait_ge(s_rlo, b + 1)
                for q in range(QT):
                    for k in range(TOP):
                        pool.indirect_dma_start(
                            xs_d, bass.IndirectOffsetOnAxis(ap=place_u[:, r, k, q:q + 1], axis=0),
                            rows[:, r, q, :], None).then_inc(s_scatter[r], 16)

            def pair(it):
                for r in range(2):
                    b = it * 2 + r
                    if alive(b):
                        second_norm(b)
                    if alive(b - 1):
                        scatter(b - 1, (r + 1) % 2)

            pair(0)
            with pool.Fori(1, BLOCKS // 2) as it:
                pair(it)
            pair(BLOCKS // 2)
            for r in range(2):
                pool.wait_ge(s_scatter[r], 16 * TOP * QT * BLOCKS // 2)

        @block.tensor
        def _(pe):
            pe.wait_ge(s_w, 48)
            for c in range(DC):
                for k in range(DC):
                    last = pe.matmul(ps_a[:, c * D:(c + 1) * D], wq_sb[:, k, c * P:(c + 1) * P], wk_sb[:, k, :],
                                     start=(k == 0), stop=(k == DC - 1))
            last.then_inc(s_m_ps, 1)
            pe.wait_ge(s_const, 14)

            def transposes(i):
                pe.wait_ge(s_xhi, i + 1)
                pe.wait_ge(s_xlo, i + 1)
                if i >= 2:
                    pe.wait_ge(s_khi, i - 1)
                    pe.wait_ge(s_klo, i - 1)
                for h in range(2):
                    for c in range(DC):
                        for s in range(KT):
                            last = pe.transpose(tr_ps[i % 2][h][:, c, s * P:(s + 1) * P],
                                                xn_w[h][:, i % 2, s, c * P:(c + 1) * P], ident16[:, :])
                last.then_inc(s_tr, 1)

            def values(i):
                pe.wait_ge(s_khi, i + 1)
                pe.wait_ge(s_klo, i + 1)
                if i == 0:
                    pe.wait_ge(s_whi, 2)
                    pe.wait_ge(s_wlo, 2)
                if i >= 2:
                    pe.wait_ge(s_vhi, i - 1)
                    pe.wait_ge(s_vlo, i - 1)
                terms = [(c, a, w) for c in range(DC) for a, w in TERMS]
                for s in range(KT):
                    t = i * KT + s
                    for j, (c, a, w) in enumerate(terms):
                        last = pe.matmul(v_ps[i % 2][:, s, :], kT[a][:, c, t * P:(t + 1) * P], wv_w[w][:, c, :],
                                         start=(j == 0), stop=(j == len(terms) - 1))
                last.then_inc(s_v_ps, 1)

            for i in range(GROUPS + 1):
                if i >= 1:
                    values(i - 1)
                if i < GROUPS:
                    transposes(i)

            def queries(b):
                terms = [(k, a, w) for k in range(DC) for a, w in TERMS]
                for c in range(DC):
                    for i, (k, a, w) in enumerate(terms):
                        last = pe.matmul(ps_b[:, c * QB:(c + 1) * QB], m_w[w][:, k, c * P:(c + 1) * P],
                                         kT[a][:, k, bass.ds(b * QB, QB)],
                                         start=(i == 0), stop=(i == len(terms) - 1))
                last.then_inc(s_q_ps, 1)

            pe.wait_ge(s_vlo, GROUPS)
            pe.wait_ge(s_vhi, GROUPS)
            queries(0)

            def scores(n, at):
                g, r = n % GROUPS, n // GROUPS % 2
                if not before_start(at - 2):
                    pe.wait_ge(s_evac, at - 1)
                terms = [(c, a, w) for c in range(DC) for a, w in TERMS]
                for s in range(KT):
                    kt = g * KT + s
                    for i, (c, a, w) in enumerate(terms):
                        last = pe.matmul(ps_s[n % 2][:, s, :], kT[a][:, c, kt * P:(kt + 1) * P],
                                         q_t[w][:, r, c, :], start=(i == 0), stop=(i == len(terms) - 1))
                last.then_inc(s_scores, 1)

            def maxima_transposed(n, b):
                pe.wait_ge(s_max, (b + 1) * (GROUPS - 1))
                for q in range(QT):
                    for s in range(KT):
                        last = pe.transpose((ps_a, ps_b)[q][:, s * P:(s + 1) * P],
                                            run_max[:, (n // GROUPS + 1) % 2, s * QB + q * P:s * QB + (q + 1) * P],
                                            ident[:, :])
                last.then_inc(s_max_t, 1)

            def maxima_spread(b):
                pe.wait_ge(s_diag, (b + 1) * QT)
                pe.matmul(ps_b[:, 0:QB], ones[:, :], diag[:, :, :].rearrange("p q k -> p (q k)"),
                          start=True, stop=True).then_inc(s_mrow_ps, 1)

            def values_product(n, m):
                g, slot = (n - PV_LAG) % GROUPS, (n - PV_LAG) % RING
                pe.wait_ge(s_phi, m + 1)
                pe.wait_ge(s_plo, m + 1)
                for q in range(QT):
                    for s in range(KT):
                        kt = g * KT + s
                        for a, w in TERMS:
                            width = VW if w == 0 else D
                            last = pe.matmul(ps_o[q][:, 0:width],
                                             (p_hi, p_lo)[a][:, slot, s * QB + q * P:s * QB + (q + 1) * P],
                                             val[w][:, kt, 0:width],
                                             start=(g == 0 and s == 0 and (a, w) == TERMS[0]),
                                             stop=(g == GROUPS - 1 and s == KT - 1 and (a, w) == TERMS[-1]))
                last.then_inc(s_pv, 1)

            def tokens_transposed(b):
                pe.wait_ge(s_xn2, b + 1)
                if not before_start(b - 1):
                    pe.wait_ge(s_place, b)
                for q in range(QT):
                    for c in range(DC):
                        at = (q * DC + c) * P
                        last = pe.transpose(ps_a[:, at:at + P], xn2[:, q, c * P:(c + 1) * P], ident[:, :])
                last.then_inc(s_xn2_ps, 1)

            def gate(b):
                pe.wait_ge(s_xn2_t, b + 1)
                for q in range(QT):
                    for c in range(DC):
                        last = pe.matmul(ps_a[:, q * E:(q + 1) * E], xn2_t[:, q, c, :], gate_sb[:, c, :],
                                         start=(c == 0), stop=(c == DC - 1))
                last.then_inc(s_logit_ps, 1)

            def ranks(b):
                pe.wait_ge(s_both, b + 1)
                for q in range(QT + 1):
                    for j in range(min(q + 1, QT)):
                        last = pe.matmul(ps_a[:, q * E:(q + 1) * E], (tri if j == q else ones)[:, :], both[:, j, :],
                                         start=(j == 0), stop=(j == min(q, QT - 1)))
                last.then_inc(s_rank_ps, 1)

            pe.wait_ge(s_gate, 16)

            def step(n, it):
                at, b, g = where(n, it)
                if alive(b):
                    if g == 0:
                        pe.wait_ge(s_qhi, b + 1)
                        pe.wait_ge(s_qlo, b + 1)
                    scores(n, at)
                    if g == 4 and alive(b + 1):
                        if alive(b - 1):
                            pe.wait_ge(s_mrow, b)
                        queries(b + 1)
                if alive(b - 1):
                    if g == 0:
                        if alive(b - 3):
                            pe.wait_ge(s_xn2_t, b - 2)
                        maxima_transposed(n, b - 1)
                    if g == 1:
                        maxima_spread(b - 1)
                if alive_step(at - PV_LAG):
                    if (n - PV_LAG) % GROUPS == 0 and not before_start(at - PV_LAG - GROUPS):
                        pe.wait_ge(s_x1, it * (SLOTS // GROUPS) + (n - PV_LAG) // GROUPS)
                    values_product(n, at - PV_LAG)
                if g == 6 and alive(b - 2):
                    tokens_transposed(b - 2)
                if g == 1 and alive(b - 3):
                    gate(b - 3)
                if g == 3 and alive(b - 3):
                    ranks(b - 3)

            passes(pe, step)

        @block.scalar
        def _(act):
            def query_high(b, r):
                act.wait_ge(s_q_ps, b + 1)
                act.activation(q_t[0][:, r, :, :], ps_b.rearrange("p (c q) -> p c q", c=DC), ACT.Copy,
                               scale=0.25).then_inc(s_qhi, 1)

            for i in range(GROUPS + 2):
                if i == 1:
                    act.wait_ge(s_scale, 1)
                    act.activation(m_w[0][:, :, :], ps_a.rearrange("p (c d) -> p c d", c=DC), ACT.Copy,
                                   scale=col(S_M)).then_inc(s_whi, 1)
                    act.activation(wv_w[0], wv_sb, ACT.Copy, scale=col(S_V)).then_inc(s_whi, 1)
                if i < GROUPS:
                    act.wait_ge(s_xn, i + 1)
                    if i >= 2:
                        act.wait_ge(s_tr, i - 1)
                    act.activation(xn_w[0][:, i % 2, :, :], xn, ACT.Copy).then_inc(s_xhi, 1)
                if 1 <= i <= GROUPS:
                    act.wait_ge(s_tr, i)
                    act.activation(kT[0][:, :, (i - 1) * KT * P:i * KT * P], tr_ps[(i - 1) % 2][0],
                                   ACT.Copy).then_inc(s_khi, 1)
                if i >= 2:
                    act.wait_ge(s_v_ps, i - 1)
                    act.activation(val[0][:, (i - 2) * KT:(i - 1) * KT, 0:D], v_ps[i % 2], ACT.Copy, scale=0.25
                                   ).then_inc(s_vhi, 1)

            def make_mask(n, it):
                at, _, g = where(n, it)
                act.wait_ge(s_adj[g], it * 16 + 16)
                if not before_start(at - 2):
                    act.wait_ge(s_evac, at - 1)
                h = n // GROUPS % 2
                act.activation(mask[:, n % 2, :].rearrange("p (s q) -> p s q", s=KT),
                               adj_sb[:, g, :, h * QB:(h + 1) * QB], ACT.Copy, scale=BIG, bias=-BIG
                               ).then_inc(s_mask, 1)

            query_high(0, 0)
            make_mask(0, 0)

            def step(n, it):
                at, b, g = where(n, it)
                if alive_step(at) and alive_step(at + 1):
                    make_mask((n + 1) % SLOTS, it + (n + 1) // SLOTS)
                if g == 7 and alive(b - 2):
                    act.wait_ge(s_xn2_ps, b - 1)
                    if alive(b - 3):
                        act.wait_ge(s_logit_ps, b - 2)
                    act.activation(xn2_t[:, :, :, :].rearrange("p q c k -> p (q c k)"), ps_a, ACT.Copy
                                   ).then_inc(s_xn2_t, 1)
                if g == 1 and alive(b - 1):
                    act.wait_ge(s_mrow_ps, b)
                    if not before_start(b - 3):
                        act.wait_ge(s_sub, (b - 2) * GROUPS)
                    act.activation(m_row[:, (n // GROUPS + 1) % 2, :], ps_b[:, 0:QB], ACT.Copy
                                   ).then_inc(s_mrow, 1)
                if g == 5 and alive(b) and alive(b + 1):
                    query_high(b + 1, (n // GROUPS + 1) % 2)
                m = at - SUB_LAG
                if alive_step(m):
                    slot = (n - SUB_LAG) % SLOTS
                    act.wait_ge(s_sub, m + 1)
                    if not before_start(m - 2):
                        act.wait_ge(s_plo, m - 1)
                    act.activation(e_sb[:, (n - SUB_LAG) % 2, :], t_sb[:, slot, :], ACT.Exp,
                                   scale=col(EXP_SCALE)).then_inc(s_exp, 1)
                    if not before_start(m - RING):
                        act.wait_ge(s_pv, m - RING + 1)
                    act.activation(p_hi[:, (n - SUB_LAG) % RING, :], t_sb[:, slot, :], ACT.Exp,
                                   scale=col(EXP_SCALE)).then_inc(s_phi, 1)
                if g == 7 and alive(b - 2):
                    r = n // GROUPS % 2
                    act.wait_ge(s_xn2, b - 1)
                    if alive(b - 4):
                        act.wait_ge(s_scatter[r], 16 * TOP * QT * (it - 1))
                    act.activation(rows[:, r, :, 0:D], xn2[:, :, :], ACT.Copy).then_inc(s_rhi, 1)

            passes(act, step)

        @block.vector
        def _(dve):
            chain = [0]

            def link(ins):
                chain[0] += 1
                ins.then_inc(s_chain, 1)
                dve.wait_ge(s_chain, chain[0])

            def statistics(i):
                dve.wait_ge(s_x_load[i], 16)
                for t in range(i * KT, (i + 1) * KT):
                    last = dve.bn_stats(stats[:, t, :], x_all[:, t, :])
                last.then_inc(s_stats, 1)
                dve.wait_ge(s_stats, i + 1)
                for t in range(i * KT, (i + 1) * KT):
                    last = dve.bn_aggr(mv[:, t, :], stats[:, t, :])
                last.then_inc(s_mv, 1)

            def weight_scales():
                link(dve.tensor_scalar(amax, amax_all, 2.0 ** -100, None, ALU.max))
                link(dve.tensor_single_scalar(amax.bitcast(u32), amax.bitcast(u32), 0x7F800000, ALU.bitwise_and))
                link(dve.tensor_scalar(scales[:, INV_M:INV_V + 1], amax, 2.0 ** -8, None, ALU.mult))
                link(dve.reciprocal(scales[:, S_M:S_V + 1], scales[:, INV_M:INV_V + 1]))
                dve.tensor_scalar(scales[:, EXP_SCALE:OUT_SCALE + 1], scales[:, INV_M:INV_V + 1], 4.0, None, ALU.mult
                                  ).then_inc(s_scale, 1)
                dve.wait_ge(s_scale, 1)

            statistics(0)
            statistics(1)
            dve.wait_ge(s_m_ps, 1)
            dve.tensor_reduce(amax[:, 0:1], ps_a, axis=AX.X, op=ALU.max,
                              apply_absolute_value=True).then_inc(s_amax, 1)
            dve.wait_ge(s_w, 48)
            dve.tensor_reduce(amax[:, 1:2], wv_sb.rearrange("p c d -> p (c d)"), axis=AX.X, op=ALU.max,
                              apply_absolute_value=True).then_inc(s_amax, 1)
            for i in range(GROUPS + 2):
                if i < GROUPS:
                    dve.wait_ge(s_rstd, i + 1)
                    if i >= 1:
                        dve.wait_ge(s_xhi, i)
                        dve.wait_ge(s_xlo, i)
                    for s in range(KT):
                        t = i * KT + s
                        last = dve.tensor_scalar(xn[:, s, :], x_all[:, t, :], mv[:, t, 0:1], rstd[:, t:t + 1],
                                                 ALU.subtract, ALU.mult)
                    last.then_inc(s_xn, 1)
                if i + 2 < GROUPS:
                    statistics(i + 2)
                if 2 <= i:
                    dve.wait_ge(s_vhi, i - 1)
                    dve.scalar_tensor_tensor(val[1][:, (i - 2) * KT:(i - 1) * KT, 0:D], v_ps[i % 2], 0.25,
                                             val[0][:, (i - 2) * KT:(i - 1) * KT, 0:D],
                                             ALU.mult, ALU.subtract).then_inc(s_vlo, 1)
                if i < GROUPS:
                    dve.wait_ge(s_xn, i + 1)
                    dve.wait_ge(s_xhi, i + 1)
                    dve.tensor_tensor(xn_w[1][:, i % 2, :, :], xn, xn_w[0][:, i % 2, :, :], ALU.subtract
                                      ).then_inc(s_xlo, 1)
                if i == 0:
                    dve.wait_ge(s_amax_all, 1)
                    weight_scales()
                if i == 1:
                    dve.wait_ge(s_whi, 1)
                    dve.scalar_tensor_tensor(m_w[1][:, :, :].rearrange("p c d -> p (c d)"), ps_a, col(S_M),
                                             m_w[0][:, :, :].rearrange("p c d -> p (c d)"), ALU.mult, ALU.subtract
                                             ).then_inc(s_wlo, 1)
                    dve.wait_ge(s_whi, 2)
                    dve.scalar_tensor_tensor(wv_w[1], wv_sb, col(S_V), wv_w[0], ALU.mult, ALU.subtract
                                             ).then_inc(s_wlo, 1)
                if 1 <= i <= GROUPS:
                    dve.wait_ge(s_tr, i)
                    dve.tensor_copy(kT[1][:, :, (i - 1) * KT * P:i * KT * P], tr_ps[(i - 1) % 2][1]
                                    ).then_inc(s_klo, 1)

            def query_low(b, r):
                dve.wait_ge(s_qhi, b + 1)
                dve.scalar_tensor_tensor(q_t[1][:, r, :, :], ps_b.rearrange("p (c q) -> p c q", c=DC), 0.25,
                                         q_t[0][:, r, :, :], ALU.mult, ALU.subtract).then_inc(s_qlo, 1)

            query_low(0, 0)

            def output(b, r, it):
                dve.wait_ge(s_pv, (b + 1) * GROUPS)
                for q in range(QT):
                    last = dve.tensor_scalar(den[:, 0, q:q + 1], ps_o[q][:, D:VW], 0.5, None, ALU.max)
                last.then_inc(s_den, 1)
                dve.wait_ge(s_den, b * 3 + 1)
                dve.reciprocal(den[:, 1, :], den[:, 0, :]).then_inc(s_den, 1)
                dve.wait_ge(s_den, b * 3 + 2)
                dve.tensor_scalar(den[:, 2, :], den[:, 1, :], col(OUT_SCALE), None, ALU.mult).then_inc(s_den, 1)
                dve.wait_ge(s_den, b * 3 + 3)
                dve.wait_ge(s_xin[r], it * 16)
                for q in range(QT):
                    last = dve.scalar_tensor_tensor(x_io[:, r, q, :], ps_o[q][:, 0:D], den[:, 2, q:q + 1],
                                                    x_io[:, r, q, :], ALU.mult, ALU.add)
                last.then_inc(s_x1, 1)
                dve.wait_ge(s_x1, b + 1)
                for q in range(QT):
                    last = dve.bn_stats(stats2[:, q, :], x_io[:, r, q, :])
                last.then_inc(s_stats2, 1)
                dve.wait_ge(s_const, 14)
                dve.wait_ge(s_stats2, b + 1)
                for q in range(QT):
                    last = dve.bn_aggr(mv2[:, q, :], stats2[:, q, :])
                last.then_inc(s_mv2, 1)

            def normalised(b, r):
                dve.wait_ge(s_rstd2, b + 1)
                if not before_start(b - 1):
                    dve.wait_ge(s_rhi, b)
                    dve.wait_ge(s_xn2_ps, b)
                for q in range(QT):
                    last = dve.tensor_scalar(xn2[:, q, :], x_io[:, r, q, :], mv2[:, q, 0:1], rstd2[:, 0, q:q + 1],
                                             ALU.subtract, ALU.mult)
                last.then_inc(s_xn2, 1)

            def row_low(b, r):
                dve.wait_ge(s_rhi, b + 1)
                dve.tensor_tensor(rows[:, r, :, D:ROW], xn2[:, :, :], rows[:, r, :, 0:D], ALU.subtract
                                  ).then_inc(s_rlo, 1)

            def choose(b, tiles):
                dve.wait_ge(s_logit_ps, b + 1)
                count = b * 6
                dve.tensor_copy(logits[:, :, :].rearrange("p q e -> p (q e)"), ps_a[:, 0:QT * E]).then_inc(s_pick, 1)
                dve.compute_val(count + 1)
                dve.wait_ge(s_const, 14)
                dve.wait_ge(s_pick, count + 1)
                for q in range(QT):
                    last = dve.max(top[:, q, :], logits[:, q, :])
                last.then_inc(s_pick, 1)
                dve.compute_val(count + 2)
                dve.wait_ge(s_const, 14)
                dve.wait_ge(s_pick, count + 2)
                for q in range(QT):
                    last = dve.max_index(top_i[:, q, :], top[:, q, :], logits[:, q, :])
                last.then_inc(s_pick, 1)
                dve.wait_ge(s_pick, count + 3)
                dve.tensor_copy(kept["logit"][:, :, tiles], top[:, :, 0:TOP].rearrange("p q k -> p k q")
                                ).then_inc(s_pick, 1)
                dve.tensor_copy(picked[:, :, :], top_i[:, :, 0:TOP].rearrange("p q k -> p k q")).then_inc(s_pick, 1)
                dve.wait_ge(s_pick, count + 5)
                dve.tensor_copy(kept["chosen"][:, :, tiles], picked[:, :, :])
                dve.tensor_tensor(hot[:, :, :, :].rearrange("p k q e -> p (k q) e"),
                                  picked[:, :, :].rearrange("p k q -> p (k q)")[:, :, None]
                                  .to_broadcast([P, TOP * QT, E]),
                                  kept["expert_ids"][:, None, :].to_broadcast([P, TOP * QT, E]), ALU.is_equal
                                  ).then_inc(s_pick, 1)
                dve.wait_ge(s_pick, count + 6)
                dve.tensor_tensor(both[:, :, :], hot[:, 0, :, :], hot[:, 1, :, :], ALU.add).then_inc(s_both, 1)

            def placed(b, r, tiles):
                dve.wait_ge(s_rank_ps, b + 1)
                ranks = ps_a[:, 0:QT * E].rearrange("p (q e) -> p q e", e=E)
                dve.tensor_tensor(rank[:, :, :], ranks, kept["next_row"][:, None, :].to_broadcast([P, QT, E]), ALU.add
                                  ).then_inc(s_put, 1)
                dve.wait_ge(s_put, b * 3 + 1)
                dve.tensor_tensor(kept["next_row"][:, :], ps_a[:, QT * E:(QT + 1) * E], kept["next_row"][:, :], ALU.add
                                  ).then_inc(s_place, 1)
                dve.tensor_tensor(mixed[:, :, :, :], hot[:, :, :, :],
                                  rank[:, None, :, :].to_broadcast([P, TOP, QT, E]), ALU.mult).then_inc(s_put, 1)
                dve.wait_ge(s_put, b * 3 + 2)
                dve.tensor_reduce(put[:, :, :], mixed[:, :, :, :], axis=AX.X, op=ALU.add).then_inc(s_put, 1)
                dve.wait_ge(s_put, b * 3 + 3)
                dve.tensor_copy(kept["place"][:, :, tiles], put[:, :, :])
                dve.tensor_copy(place_u[:, r, :, :], put[:, :, :]).then_inc(s_route, 1)

            dve.wait_ge(s_const, 14)

            def step(n, it):
                at, b, g = where(n, it)
                r = n // GROUPS % 2
                if alive(b - 3):
                    tiles = bass.ds(it * (2 * QT) + (n // GROUPS - 3) * QT, QT)
                m = at - LO_LAG
                if alive_step(m):
                    dve.wait_ge(s_exp, m + 1)
                    dve.wait_ge(s_phi, m + 1)
                    if not before_start(m - RING):
                        dve.wait_ge(s_pv, m - RING + 1)
                    dve.tensor_tensor(p_lo[:, (n - LO_LAG) % RING, :], e_sb[:, (n - LO_LAG) % 2, :],
                                      p_hi[:, (n - LO_LAG) % RING, :], ALU.subtract).then_inc(s_plo, 1)
                m = at - SUB_LAG
                if alive_step(m):
                    dve.wait_ge(s_mrow, it * (SLOTS // GROUPS) + (n - SUB_LAG) // GROUPS + 1)
                    part = t_sb[:, (n - SUB_LAG) % SLOTS, :].rearrange("p (s q) -> p s q", s=KT)
                    row = m_row[:, (n - SUB_LAG) // GROUPS % 2, None, :].to_broadcast([P, KT, QB])
                    dve.tensor_tensor(part, part, row, ALU.subtract).then_inc(s_sub, 1)
                if g == 4 and alive(b - 2):
                    output(b - 2, r, it + n // SLOTS)
                if g == 5 and alive(b) and alive(b + 1):
                    query_low(b + 1, (r + 1) % 2)
                if alive(b):
                    dve.wait_ge(s_scores, at + 1)
                    dve.wait_ge(s_mask, at + 1)
                    if not before_start(at - SLOTS):
                        dve.wait_ge(s_phi, at - SLOTS + 1)
                    dve.tensor_tensor(t_sb[:, n, :], ps_s[n % 2][:, :, :].rearrange("p s q -> p (s q)"),
                                      mask[:, n % 2, :], ALU.add).then_inc(s_evac, 1)
                    if g >= 1:
                        dve.wait_ge(s_evac, at + 1)
                        if g == 1:
                            if not before_start(b - 2):
                                dve.wait_ge(s_max_t, b - 1)
                            before = t_sb[:, n - 1, :]
                        else:
                            dve.wait_ge(s_max, b * (GROUPS - 1) + g - 1)
                            before = run_max[:, r, :]
                        dve.tensor_tensor(run_max[:, r, :], before, t_sb[:, n, :], ALU.max).then_inc(s_max, 1)
                if g == 0 and alive(b - 1):
                    dve.wait_ge(s_max_t, b)
                    for q in range(QT):
                        dve.tensor_reduce(m_col[:, q:q + 1], (ps_a, ps_b)[q], axis=AX.X, op=ALU.max
                                          ).then_inc(s_mcol, 1)
                    for q in range(QT):
                        dve.wait_ge(s_mcol, QT * (b - 1) + q + 1)
                        if not before_start(b - 2):
                            dve.wait_ge(s_mrow_ps, b - 1)
                        dve.tensor_scalar(diag[:, q, :], ident[:, :], m_col[:, q:q + 1], -0.1 * BIG,
                                          ALU.mult, ALU.max).then_inc(s_diag, 1)
                if g == 5 and alive(b - 2):
                    normalised(b - 2, r)
                if g == 0 and alive(b - 3):
                    row_low(b - 3, (r + 1) % 2)
                if g == 2 and alive(b - 3):
                    choose(b - 3, tiles)
                if g == 4 and alive(b - 3):
                    placed(b - 3, (r + 1) % 2, tiles)

            passes(dve, step)
            dve.wait_ge(s_place, BLOCKS)
            dve.tensor_copy(end_row[:, :], kept["next_row"][0:1, :]).then_inc(s_end_row, 1)


def experts(nc, w1_t, w3_t, w2_t, x1_d, xs_d, ys_d, out, kept, REGION, NB):
    N, D = x1_d.shape
    E, _, H = w1_t.shape
    DC = D // P
    TILES = N // P
    HC = H // P
    BU = 3
    assert NB % BU == 0 and HC % BU == 0
    PASSES = NB // BU
    S2_LAG = 2
    AHEAD = 3
    PIECES = 3 * E
    STAGES = 3
    QUART = 4
    QW = TILES // QUART
    W_SCALE = 2.0 ** 8
    A_INV = 1.0 / W_SCALE
    H_SCALE = 2.0 ** -5
    Y_INV = 1.0 / (W_SCALE * W_SCALE * H_SCALE)
    ROW = 2 * D
    ROUND = 1.5 * 2.0 ** 23

    ctx = ExitStack()
    with ctx:
        def sb(name, shape, dt):
            return ctx.enter_context(nc.sbuf_tensor(name, shape, dt))

        def pb(name, shape):
            return ctx.enter_context(nc.psum_tensor(name, shape, fp32))

        def sem(name):
            return ctx.enter_context(nc.semaphore(name))

        ps_ab = [pb(f"ps_ab{i}", [P, 2, TB]) for i in range(BU)]
        ps_y = [pb(f"ps_y{i}", [P, 512]) for i in range(TBT)]
        ps_t = [pb(f"ps_t{i}", [P, 512]) for i in range(2)]

        w_all = [sb(f"w_{h}", [P, E, 3, DC * H], fp16) for h in ("hi", "lo")]
        stage = sb("w_stage", [P, STAGES, DC * H], fp32)
        x_rows = sb("x_rows", [P, BU, TBT, ROW], fp16)
        xs_t = [sb(f"xs_t_{h}", [P, BU, DC, TB], fp16) for h in ("hi", "lo")]
        act_a = sb("act_a", [P, BU, TB], fp32)
        hid = sb("hid", [P, BU, TB], fp32)
        h_w = [sb(f"h_{h}", [P, BU, TB], fp16) for h in ("hi", "lo")]
        y_sb = sb("y_sb", [P, TBT, D], fp32)
        region = sb("region", [P, E], fp32)
        count = sb("count", [P, E], fp32)
        blocks = sb("blocks", [P, E], fp32)
        b_incl = sb("b_incl", [P, E], fp32)
        b_first = sb("b_first", [P, E], fp32)
        delta = sb("delta", [P, E], fp32)
        ones_e = sb("ones_e", [P, E], fp32)
        index = sb("index", [1, NB, E], fp32)
        each = sb("each", [1, NB, E], fp32)
        eidf = sb("eidf", [1, NB], fp32)
        row0f = sb("row0f", [1, NB], fp32)
        eid = sb("eid", [1, NB], i32)
        row0 = sb("row0", [1, NB], i32)
        limits = sb("limits", [1, 2], i32)
        which = sb("which", [P, TOP * TILES, E], fp32)
        y_row = sb("y_row", [P, TOP, TILES], fp32)
        first_lower = sb("first_lower", [P, TILES], fp32)
        first_upper = sb("first_upper", [P, TILES], fp32)
        part = sb("part", [P, TOP, TILES], fp32)
        w_top = sb("w_top", [P, TOP, TILES], fp32)
        mix = sb("mix", [P, TOP, TILES], fp32)
        y_at = sb("y_at", [P, TOP, TILES], u32)
        ident16 = kept["ident16"]

        done_w = [w_all[h][:, 0:E - 1, :, :].rearrange("p e k n -> p (e k n)").bitcast(fp32) for h in range(2)]
        cut = TILES // 2
        y_low = done_w[0][:, 0:TILES * D].rearrange("p (t d) -> p t d", d=D)
        x1_sb = done_w[1][:, 0:TILES * D].rearrange("p (t d) -> p t d", d=D)
        assert (TILES + cut) * D <= (E - 1) * 3 * DC * H // 2
        y_high = [done_w[h][:, TILES * D:(TILES + cut) * D].rearrange("p (t d) -> p t d", d=D) for h in range(2)]

        s_const = sem("b_const")
        s_table = sem("b_table")
        s_chain = sem("b_chain")
        s_diff = sem("b_diff")
        s_expd = sem("b_expd")
        s_rows = sem("b_rows")
        s_first_w = [sem(f"b_first_w{i}") for i in range(3)]
        s_stage = [sem(f"b_stage{i}") for i in range(STAGES)]
        s_whi = sem("b_whi")
        s_wlo = sem("b_wlo")
        s_split = sem("b_split")
        s_ready = sem("b_ready")
        s_xr = [sem(f"b_xr{i}") for i in range(BU)]
        s_tps = sem("b_tps")
        s_txhi = sem("b_txhi")
        s_txlo = sem("b_txlo")
        s_ab = sem("b_ab")
        s_silu = sem("b_silu")
        s_hid = sem("b_hid")
        s_hhi = sem("b_hhi")
        s_hlo = sem("b_hlo")
        s_h_used = sem("b_h_used")
        s_y_ps = sem("b_y_ps")
        s_y = sem("b_y")
        s_ys = sem("b_ys")
        s_x1_in = [sem(f"b_x1_in{i}") for i in range(QUART)]
        s_low_in = [sem(f"b_low_in{i}") for i in range(QUART)]
        s_high_in = [sem(f"b_high_in{i}") for i in range(QUART)]
        s_weighed = sem("b_weighed")
        s_half = sem("b_half")
        s_sum = [sem(f"b_sum{i}") for i in range(QUART)]
        s_fin = sem("b_fin")

        x1_t = x1_d.rearrange("(t p) d -> p t d", p=P)
        out_t = out.rearrange("(t p) d -> p t d", p=P)
        ys_v = ys_d.rearrange("(q p) d -> p q d", p=P)
        W = (w1_t, w3_t, w2_t)

        def load_piece(eng, i, s_loaded):
            e, k = divmod(i, 3)
            eng.dma_start(stage[:, i % STAGES, :].rearrange("p (c n) -> p c n", n=W[k].shape[2]),
                          W[k][e].rearrange("(c p) n -> p c n", p=P)).then_inc(s_loaded[i % STAGES], 16)

        def passes(eng, step):
            for n in range(BU):
                step(n, 0)
            with eng.Fori(1, PASSES - 1) as it:
                for n in range(BU):
                    step(n, it)
            for n in range(BU):
                step(n, PASSES - 1)

        def is_first(b):
            return isinstance(b, int) and b == 0

        def is_last(b):
            return isinstance(b, int) and b == NB - 1

        block = ctx.enter_context(nc.Block())

        @block.sync
        def _(sp):
            for i in range(3):
                load_piece(sp, i, s_first_w)
            sp.wait_ge(s_table, 1)

            def step(n, it):
                b = it * BU + n
                at = sp.value_load(row0[0:1, bass.ds(b, 1)], min_val=0, max_val=E * REGION - TB)
                src = xs_d[bass.ds(at, TB), :].rearrange("(q p) r -> p q r", p=P)
                sp.compute_val(src.offset * 2)
                if not (isinstance(it, int) and it == 0):
                    sp.wait_ge(s_tps, b - BU + 1)
                sp.dma_start(x_rows[:, n, :, :], src).then_inc(s_xr[n], 16)

            passes(sp, step)
            for i in range(QUART):
                sp.wait_ge(s_sum[i], QW)
                sp.dma_start(out_t[:, i * QW:(i + 1) * QW, :], x1_sb[:, i * QW:(i + 1) * QW, :]).then_inc(s_fin, 16)
            sp.wait_ge(s_fin, 16 * QUART)

        @block.gpsimd
        def _(pool):
            pool.iota(index[:, :, :].bitcast(i32), pattern=[[1, NB], [0, E]], base=0, channel_multiplier=0
                      ).then_inc(s_const, 1)
            pool.memset(ones_e[:, :], 1.0).then_inc(s_const, 1)
            pool.wait_ge(s_const, 2)
            pool.tensor_copy(index[:, :, :], index[:, :, :].bitcast(i32)).then_inc(s_const, 1)
            for i in range(3):
                pool.wait_ge(s_whi, i + 1)
                pool.wait_ge(s_wlo, i + 1)
                load_piece(pool, 3 + i, s_stage)
            pool.sem_inc(s_ready, 1)
            done = 0
            for i in range(3, PIECES):
                e, k = divmod(i, 3)
                pool.wait_ge(s_stage[i % STAGES], 16 * (i // STAGES))
                w = stage[:, i % STAGES, :]
                pool.tensor_scalar(w, w, W_SCALE, 0.0, ALU.mult, ALU.add).then_inc(s_split, 1)
                pool.wait_ge(s_split, done + 1)
                pool.tensor_scalar(w_all[0][:, e, k, :], w, 1.0, 0.0, ALU.mult, ALU.add).then_inc(s_split, 1)
                pool.wait_ge(s_split, done + 2)
                pool.tensor_tensor(w_all[1][:, e, k, :], w, w_all[0][:, e, k, :], ALU.subtract).then_inc(s_split, 1)
                done += 3
                if i + STAGES < PIECES or k == 2:
                    pool.wait_ge(s_split, done)
                if i + STAGES < PIECES:
                    load_piece(pool, i + STAGES, s_stage)
                if k == 2:
                    pool.sem_inc(s_ready, 1)
            pool.wait_ge(s_rows, 1)
            before_last = pool.value_load(limits[0:1, 0:1], min_val=1, max_val=NB)
            in_all = pool.value_load(limits[0:1, 1:2], min_val=1, max_val=NB)
            pool.compute_val(before_last * 16)
            pool.wait_ge(s_rows, 1)
            pool.wait_ge(s_ys, before_last * 16)
            for i in range(QUART):
                pool.dma_start(x1_sb[:, i * QW:(i + 1) * QW, :], x1_t[:, i * QW:(i + 1) * QW, :]
                               ).then_inc(s_x1_in[i], 16)
                for t in range(i * QW, (i + 1) * QW):
                    pool.indirect_dma_start(y_low[:, t, :], None, ys_d,
                                            bass.IndirectOffsetOnAxis(ap=y_at[:, 0, t:t + 1], axis=0)
                                            ).then_inc(s_low_in[i], 16)
            for i in range(QUART):
                quarter = slice(i * QW, (i + 1) * QW)
                pool.wait_ge(s_low_in[i], 16 * QW)
                for t in range(i * QW, (i + 1) * QW):
                    last = pool.tensor_scalar(y_low[:, t, :], y_low[:, t, :], mix[:, 0, t:t + 1], 0.0,
                                              ALU.mult, ALU.add)
                last.then_inc(s_weighed, 1)
                pool.wait_ge(s_weighed, i + 1)
                pool.wait_ge(s_x1_in[i], 16)
                pool.tensor_tensor(x1_sb[:, quarter, :], y_low[:, quarter, :], x1_sb[:, quarter, :], ALU.add
                                   ).then_inc(s_half, 1)
            pool.compute_val(in_all * 16)
            pool.wait_ge(s_rows, 1)
            pool.wait_ge(s_ys, in_all * 16)
            for t in range(TILES):
                pool.indirect_dma_start(y_high[t // cut][:, t % cut, :], None, ys_d,
                                        bass.IndirectOffsetOnAxis(ap=y_at[:, 1, t:t + 1], axis=0)
                                        ).then_inc(s_high_in[t // QW], 16)

        @block.tensor
        def _(pe):
            def transposes(n, b):
                if not is_first(b):
                    pe.wait_ge(s_txhi, b)
                    pe.wait_ge(s_txlo, b)
                for h in range(2):
                    dst = ps_t[h][:, :].bitcast(fp16)
                    for c in range(DC):
                        for q in range(TBT):
                            at = c * TB + q * P
                            last = pe.transpose(dst[:, at:at + P],
                                                x_rows[:, n % BU, q, h * D + c * P:h * D + (c + 1) * P], ident16[:, :])
                last.then_inc(s_tps, 1)

            def first(n, b, hc, e):
                if not (is_first(b) and hc < BU):
                    pe.wait_ge(s_hid, b * HC + hc - BU + 1)
                for i in range(2):
                    terms = [(c, a, w) for c in range(DC) for w, a in TERMS]
                    for j, (c, a, w) in enumerate(terms):
                        at = c * H + hc * P
                        last = pe.matmul(ps_ab[hc % BU][:, i, :],
                                         w_all[w][:, bass.ds(e, 1), i, at:at + P].rearrange("p e n -> p (e n)"),
                                         xs_t[a][:, n % BU, c, :], start=(j == 0), stop=(j == len(terms) - 1))
                last.then_inc(s_ab, 1)

            def second(b, hc, e):
                k = b * HC + hc
                if hc == 0 and not is_first(b):
                    pe.wait_ge(s_y, b)
                pe.wait_ge(s_hhi, k + 1)
                pe.wait_ge(s_hlo, k + 1)
                for q in range(TBT):
                    for a, w in TERMS:
                        last = pe.matmul(ps_y[q][:, 0:D], h_w[a][:, hc % BU, q * P:(q + 1) * P],
                                         w_all[w][:, bass.ds(e, 1), 2, hc * D:(hc + 1) * D].rearrange("p e n -> p (e n)"),
                                         start=(hc == 0 and (a, w) == TERMS[0]),
                                         stop=(hc == HC - 1 and (a, w) == TERMS[-1]))
                last.then_inc(s_y_ps if hc == HC - 1 else s_h_used, 1)

            def expert(b):
                return pe.value_load(eid[0:1, bass.ds(b, 1)], min_val=0, max_val=E - 1)

            carried = [pe.alloc_register(f"carried{i}") for i in range(2)]
            pe.wait_ge(s_table, 1)
            pe.wait_ge(s_xr[0], 16)
            transposes(0, 0)
            held = {0: expert(0), -1: None}

            def step(n, it):
                b = it * BU + n
                if n == 0 and not (isinstance(it, int) and it == 0):
                    held[0], held[-1] = (pe.snap(r, min_val=0, max_val=E - 1) for r in carried)
                e, e_before = held[n], held[n - 1]
                pe.wait_ge(s_ready, e + 1)
                pe.wait_ge(s_txhi, b + 1)
                pe.wait_ge(s_txlo, b + 1)
                for hc in range(HC):
                    first(n, b, hc, e)
                    if hc == AHEAD and not is_last(b):
                        held[n + 1] = expert(b + 1)
                    if hc >= S2_LAG:
                        second(b, hc - S2_LAG, e)
                    elif not is_first(b):
                        second(b - 1, HC - S2_LAG + hc, e_before)
                    if hc == AHEAD and not is_last(b):
                        pe.wait_ge(s_xr[(n + 1) % BU], (it + (n + 1) // BU) * 16 + 16)
                        transposes(n + 1, b + 1)
                if n == BU - 1 and not is_last(b):
                    pe.reg_mov(carried[0], held[BU])
                    pe.reg_mov(carried[1], held[BU - 1])

            passes(pe, step)
            for hc in range(HC - S2_LAG, HC):
                second(NB - 1, hc, held[BU - 1])

        @block.scalar
        def _(act):
            act.wait_ge(s_diff, 1)
            act.activation(w_top[:, 1, :], w_top[:, 0, :], ACT.Exp).then_inc(s_expd, 1)
            for k in range(3):
                act.wait_ge(s_first_w[k], 16)
                act.activation(w_all[0][:, 0, k, :], stage[:, k, :], ACT.Copy, scale=W_SCALE).then_inc(s_whi, 1)

            def x_high(b, n):
                act.wait_ge(s_tps, b + 1)
                act.activation(xs_t[0][:, n % BU, :, :], ps_t[0][:, :].bitcast(fp16)[:, 0:DC * TB]
                               .rearrange("p (c q) -> p c q", c=DC), ACT.Copy).then_inc(s_txhi, 1)

            def y_out(b):
                act.wait_ge(s_y_ps, b + 1)
                if not is_first(b):
                    act.wait_ge(s_ys, b * 16)
                for q in range(TBT):
                    last = act.activation(y_sb[:, q, :], ps_y[q][:, 0:D], ACT.Copy, scale=Y_INV)
                last.then_inc(s_y, 1)
                act.wait_ge(s_y, b + 1)
                act.dma_start(ys_v[:, bass.ds(b * TBT, TBT), :], y_sb[:, :, :]).then_inc(s_ys, 16)

            def silu(b, hc):
                act.wait_ge(s_ab, b * HC + hc + 1)
                act.activation(act_a[:, hc % BU, :], ps_ab[hc % BU][:, 0, :], ACT.Silu, scale=A_INV).then_inc(s_silu, 1)

            def high(b, hc):
                act.wait_ge(s_hid, b * HC + hc + 1)
                if not (is_first(b) and hc < BU):
                    if hc < BU:
                        act.wait_ge(s_h_used, b * (HC - 1) - (BU - 1) + hc if hc < BU - 1 else b * (HC - 1))
                        if hc == BU - 1:
                            act.wait_ge(s_y_ps, b)
                    else:
                        act.wait_ge(s_h_used, b * (HC - 1) + hc - BU + 1)
                act.activation(h_w[0][:, hc % BU, :], hid[:, hc % BU, :], ACT.Copy).then_inc(s_hhi, 1)

            x_high(0, 0)

            def step(n, it):
                b = it * BU + n
                for hc in range(HC):
                    if hc == S2_LAG and not is_first(b):
                        y_out(b - 1)
                    silu(b, hc)
                    if hc >= 1:
                        high(b, hc - 1)
                    elif not is_first(b):
                        high(b - 1, HC - 1)
                    if hc == AHEAD + 1 and not is_last(b):
                        x_high(b + 1, n + 1)

            passes(act, step)
            high(NB - 1, HC - 1)
            y_out(NB - 1)
            act.wait_ge(s_ys, 16 * NB)

        @block.vector
        def _(dve):
            chain = [0]

            def link(ins):
                chain[0] += 1
                ins.then_inc(s_chain, 1)
                dve.wait_ge(s_chain, chain[0])

            expert_ids, next_row = kept["expert_ids"], kept["next_row"]
            link(dve.tensor_scalar(region[:, :], expert_ids[:, :], float(REGION), None, ALU.mult))
            link(dve.tensor_tensor(count[:, :], next_row[:, :], region[:, :], ALU.subtract))
            link(dve.tensor_scalar(count[:, :], count[:, :], 1.0 / TB, (TB - 1.0) / TB - 0.5 + 0.5 / TB,
                                   ALU.mult, ALU.add))
            link(dve.tensor_scalar(blocks[:, :], count[:, :], ROUND, ROUND, ALU.add, ALU.subtract))
            dve.wait_ge(s_const, 3)
            link(dve.tensor_tensor_scan(b_incl[:, :], ones_e[:, :], blocks[:, :], 0.0, ALU.mult, ALU.add))
            link(dve.tensor_tensor(b_first[:, :], b_incl[:, :], blocks[:, :], ALU.subtract))
            link(dve.scalar_tensor_tensor(delta[:, :], b_first[:, :], float(TB), region[:, :],
                                          ALU.mult, ALU.subtract))
            link(dve.tensor_tensor(each[:, :, :], index[:, :, :], b_incl[0:1, None, :].to_broadcast([1, NB, E]),
                                   ALU.is_ge))
            link(dve.tensor_reduce(eidf[:, :], each[:, :, :], axis=AX.X, op=ALU.add))
            link(dve.tensor_scalar(eidf[:, :], eidf[:, :], E - 1.0, None, ALU.min))
            link(dve.tensor_tensor(each[:, :, :], eidf[:, :, None].to_broadcast([1, NB, E]),
                                   expert_ids[0:1, None, :].to_broadcast([1, NB, E]), ALU.is_equal))
            link(dve.tensor_tensor(each[:, :, :], each[:, :, :], delta[0:1, None, :].to_broadcast([1, NB, E]),
                                   ALU.mult))
            link(dve.tensor_reduce(row0f[:, :], each[:, :, :], axis=AX.X, op=ALU.add))
            link(dve.scalar_tensor_tensor(row0f[:, :], index[:, :, 0], float(TB), row0f[:, :],
                                          ALU.mult, ALU.subtract))
            link(dve.tensor_scalar(row0f[:, :], row0f[:, :], next_row[0:1, E - 1:E], None, ALU.min))
            dve.tensor_copy(eid[:, :], eidf[:, :])
            dve.tensor_copy(limits[:, :], b_incl[0:1, E - 2:E])
            dve.tensor_copy(row0[:, :], row0f[:, :]).then_inc(s_table, 1)
            logit, chosen, place = kept["logit"], kept["chosen"], kept["place"]
            dve.tensor_tensor(w_top[:, 0, :], logit[:, 1, :], logit[:, 0, :], ALU.subtract).then_inc(s_diff, 1)
            flat = lambda v: v[:, :, :].rearrange("p k t -> p (k t)")
            every = [P, TOP * TILES, E]
            link(dve.tensor_tensor(which[:, :, :], flat(chosen)[:, :, None].to_broadcast(every),
                                   expert_ids[:, None, :].to_broadcast(every), ALU.is_equal))
            link(dve.tensor_tensor(which[:, :, :], which[:, :, :], delta[:, None, :].to_broadcast(every), ALU.mult))
            link(dve.tensor_reduce(flat(y_row), which[:, :, :], axis=AX.X, op=ALU.add))
            link(dve.tensor_tensor(flat(y_row), flat(y_row), flat(place), ALU.add))
            dve.tensor_tensor(y_at[:, 0, :], y_row[:, 0, :], y_row[:, 1, :], ALU.min)
            dve.tensor_tensor(y_at[:, 1, :], y_row[:, 0, :], y_row[:, 1, :], ALU.max)
            dve.tensor_tensor(first_upper[:, :], y_row[:, 0, :], y_row[:, 1, :], ALU.is_gt)
            link(dve.tensor_tensor(first_lower[:, :], y_row[:, 0, :], y_row[:, 1, :], ALU.is_lt))
            dve.wait_ge(s_expd, 1)
            link(dve.tensor_scalar(part[:, 0, :], w_top[:, 1, :], 1.0, None, ALU.add))
            link(dve.reciprocal(w_top[:, 0, :], part[:, 0, :]))
            link(dve.tensor_tensor(w_top[:, 1, :], w_top[:, 1, :], w_top[:, 0, :], ALU.mult))
            for k, own in enumerate((first_lower, first_upper)):
                other = (first_upper, first_lower)[k]
                dve.tensor_tensor(part[:, 0, :], own[:, :], w_top[:, 0, :], ALU.mult)
                link(dve.tensor_tensor(part[:, 1, :], other[:, :], w_top[:, 1, :], ALU.mult))
                link(dve.tensor_tensor(mix[:, k, :], part[:, 0, :], part[:, 1, :], ALU.add))
            dve.sem_inc(s_rows, 1)
            for k in range(3):
                dve.wait_ge(s_whi, k + 1)
                dve.scalar_tensor_tensor(w_all[1][:, 0, k, :], stage[:, k, :], W_SCALE, w_all[0][:, 0, k, :],
                                         ALU.mult, ALU.subtract).then_inc(s_wlo, 1)

            def x_low(b, n):
                dve.wait_ge(s_tps, b + 1)
                dve.tensor_copy(xs_t[1][:, n % BU, :, :], ps_t[1][:, :].bitcast(fp16)[:, 0:DC * TB]
                                .rearrange("p (c q) -> p c q", c=DC)).then_inc(s_txlo, 1)

            def hidden(b, hc):
                k = b * HC + hc
                dve.wait_ge(s_silu, k + 1)
                if not (is_first(b) and hc < BU):
                    dve.wait_ge(s_hhi, k - BU + 1)
                    dve.wait_ge(s_hlo, k - BU + 1)
                dve.scalar_tensor_tensor(hid[:, hc % BU, :], act_a[:, hc % BU, :], H_SCALE, ps_ab[hc % BU][:, 1, :],
                                         ALU.mult, ALU.mult).then_inc(s_hid, 1)

            def low(b, hc):
                dve.wait_ge(s_hhi, b * HC + hc + 1)
                dve.tensor_tensor(h_w[1][:, hc % BU, :], hid[:, hc % BU, :], h_w[0][:, hc % BU, :], ALU.subtract
                                  ).then_inc(s_hlo, 1)

            x_low(0, 0)

            def step(n, it):
                b = it * BU + n
                for hc in range(HC):
                    hidden(b, hc)
                    if hc >= 1:
                        low(b, hc - 1)
                    elif not is_first(b):
                        low(b - 1, HC - 1)
                    if hc == AHEAD + 1 and not is_last(b):
                        x_low(b + 1, n + 1)

            passes(dve, step)
            low(NB - 1, HC - 1)
            for t in range(TILES):
                dve.wait_ge(s_half, t // QW + 1)
                dve.wait_ge(s_high_in[t // QW], 16 * QW)
                dve.scalar_tensor_tensor(x1_sb[:, t, :], y_high[t // cut][:, t % cut, :], mix[:, 1, t:t + 1],
                                         x1_sb[:, t, :], ALU.mult, ALU.add).then_inc(s_sum[t // QW], 1)


def kernel(**inputs):
    import numpy as np
    import concourse.bacc as bacc
    from concourse.bass_utils import run_bass_kernel_spmd

    nc = bacc.Bacc("TRN2", target_bir_lowering=False, num_devices=1)
    laid_out = {
        "x": inputs["x"],
        "adj": inputs["adj"],
        "wq": inputs["L0_gnn_Wq"],
        "wk": inputs["L0_gnn_Wk"],
        "wv_t": np.asarray(inputs["L0_gnn_Wv"]).T,
        "gate_t": np.asarray(inputs["L0_ffn_gate_w"]).T,
        "w1_t": np.asarray(inputs["L0_ffn_w1"]).transpose(0, 2, 1),
        "w3_t": np.asarray(inputs["L0_ffn_w3"]).transpose(0, 2, 1),
        "w2_t": np.asarray(inputs["L0_ffn_w2"]).transpose(0, 2, 1),
    }
    arrays, args = {}, []
    for name, a in laid_out.items():
        a = np.ascontiguousarray(a)
        arrays[f"in_{name}"] = a
        args.append(nc.dram_tensor(f"in_{name}", a.shape, mybir.dt.from_np(a.dtype), kind="ExternalInput").ap())
    args.append(nc.dram_tensor("out_0", laid_out["x"].shape, mybir.dt.float32, kind="ExternalOutput").ap())
    gnn_moe(nc, *args)
    return run_bass_kernel_spmd(nc, [arrays], core_ids=[0]).results[0]["out_0"]
```

```python
import concourse.bass as bass
from concourse import mybir
from contextlib import ExitStack

fp32 = mybir.dt.float32
fp16 = mybir.dt.float16
bf16 = mybir.dt.bfloat16
u8 = mybir.dt.uint8
u32 = mybir.dt.uint32
i32 = mybir.dt.int32
ALU = mybir.AluOpType
ACT = mybir.ActivationFunctionType
AX = mybir.AxisListType
RMAX = bass.bass_isa.ReduceOp.max

P = 128
EPS = 1e-5
TOP = 2
TERMS = ((0, 0), (0, 1), (1, 0))
TB = 256
TBT = TB // P
STAGES = 3


def before_start(v):
    return isinstance(v, int) and v < 0


def gnn_moe(nc, x, adj, wq, wk, wv_t, gate_t, w1_t, w3_t, w2_t, out):
    N, D = x.shape
    E, _, H = w1_t.shape
    TILES = N // P
    REGION = N + TB
    NB = TOP * N // TB + E - 1
    x1_d = nc.dram_tensor("x1_d", (N, D), fp32, kind="Internal").ap()
    xs_d = nc.dram_tensor("xs_d", (E * REGION, 2 * D), fp16, kind="Internal").ap()
    ys_d = nc.dram_tensor("ys_d", (NB * TB, D), fp32, kind="Internal").ap()
    with ExitStack() as ctx:
        def sb(name, shape, dt):
            return ctx.enter_context(nc.sbuf_tensor(name, shape, dt))

        kept = {
            "ident16": sb("ident16", [P, P], fp16),
            "stage": sb("stage", [P, STAGES, D // P * H], fp32),
            "eid": sb("eid", [1, NB], i32),
            "row0": sb("row0", [1, NB], i32),
            "limits": sb("limits", [1, 2], i32),
            "place": sb("place", [P, TOP, TILES], fp32),
            "chosen": sb("chosen", [P, TOP, TILES], fp32),
            "e_top": sb("e_top", [P, TILES], fp32),
            "expert_ids": sb("expert_ids", [P, E], fp32),
            "delta": sb("delta", [P, E], fp32),
            "y_at": sb("y_at", [P, TOP, TILES], u32),
            "mix": sb("mix", [P, TOP, TILES], fp32),
        }
        attention(nc, x, adj, wq, wk, wv_t, gate_t, (w1_t, w3_t, w2_t), x1_d, xs_d, ys_d, kept, REGION, NB)
        experts(nc, (w1_t, w3_t, w2_t), x1_d, xs_d, ys_d, out, kept, REGION, NB)


def load_piece(eng, weights, stage, i, s_loaded):
    e, k = divmod(i, 3)
    eng.dma_start(stage[:, i % STAGES, :].rearrange("p (c n) -> p c n", n=weights[k].shape[2]),
                  weights[k][e].rearrange("(c p) n -> p c n", p=P)).then_inc(s_loaded[i % STAGES], 16)


def attention(nc, x, adj, wq, wk, wv_t, gate_t, weights, x1_d, xs_d, ys_d, kept, REGION, NB):
    N, D = x.shape
    E = weights[0].shape[0]
    DC = D // P
    TILES = N // P
    QB = 256
    QT = QB // P
    BLOCKS = N // QB
    KT = 4
    GROUPS = TILES // KT
    STEPS = BLOCKS * GROUPS
    GW = KT * QB
    SLOTS = 2 * GROUPS
    PASSES = STEPS // SLOTS
    PEELED = 2
    SUB_LAG = GROUPS + 2
    LO_LAG = SUB_LAG + 1
    PV_LAG = SUB_LAG + 2
    DRAIN = 2 * GROUPS + 5
    RING = 4
    BIG = 1.0e30
    VW = D + 1
    VP = VW + 1
    ROW = 2 * D
    MAXIMA = GROUPS + 1
    assert KT == 4 and QT == 2
    FILLED, COUNTED, CONSTANTS = 7, 12, 18
    GATE_SCALE = 2.0 ** 8
    ROUND = 1.5 * 2.0 ** 23
    FILLS = 6

    ctx = ExitStack()
    with ctx:
        def sb(name, shape, dt):
            return ctx.enter_context(nc.sbuf_tensor(name, shape, dt))

        def pb(name, shape):
            return ctx.enter_context(nc.psum_tensor(name, shape, fp32))

        def sem(name):
            return ctx.enter_context(nc.semaphore(name))

        ps_s = [pb(f"ps_scores{i}", [P, KT, QB]) for i in range(2)]
        ps_out = pb("ps_out", [P, QT, 512])
        ps_misc = pb("ps_misc", [P, 2, 512])
        ps_o = [ps_out[:, q, :] for q in range(QT)]
        ps_a, ps_b = ps_misc[:, 0, :], ps_misc[:, 1, :]

        kT = [sb(f"kT_{h}", [P, DC, N], fp16) for h in ("hi", "lo")]
        val = [sb(f"val_{h}", [P, TILES, VP], fp16) for h in ("hi", "lo")]
        m_w = [sb(f"m_{h}", [P, DC, D], fp16) for h in ("hi", "lo")]
        q_t = [sb(f"qT_{h}", [P, 2, DC, QB], fp16) for h in ("hi", "lo")]
        ident = sb("ident", [P, P], fp32)
        ident16 = kept["ident16"]
        ones = sb("ones", [P, P], fp32)
        tri16 = sb("tri16", [P, P], fp16)
        ones16 = sb("ones16", [P, P], fp16)
        scales = sb("scales", [P, 8], fp32)
        place, chosen, expert_ids = (kept[name] for name in ("place", "chosen", "expert_ids"))
        stage = kept["stage"]
        adj_sb = stage[:, :, :].rearrange("p s n -> p (s n)").bitcast(u8)[:, 0:GROUPS * KT * 2 * QB] \
            .rearrange("p (g s q) -> p g s q", g=GROUPS, s=KT)
        mask = sb("mask", [P, 2, GW], bf16)
        t_sb = sb("t_sb", [P, SLOTS, GW], fp32)
        run_max = sb("run_max", [P, GW], fp32)
        block_max = sb("block_max", [P, QB], fp32)
        m_col = sb("m_col", [P, QT], fp32)
        adj_words = GROUPS * KT * 2 * QB // 4
        diag = stage[:, :, :].rearrange("p s n -> p (s n)")[:, adj_words:adj_words + QT * P] \
            .rearrange("p (q k) -> p q k", q=QT)
        m_row = sb("m_row", [P, 2, QB], fp32)
        e_sb = sb("e_sb", [P, 2, GW], fp32)
        p_hi = sb("p_hi", [P, RING, GW], fp16)
        p_lo = sb("p_lo", [P, RING, GW], fp16)
        den = sb("den", [P, 3, QT], fp32)
        x_io = sb("x_io", [P, 2, QT, D], fp32)
        stats2 = sb("stats2", [P, QT, 6], fp32)
        mv2 = sb("mv2", [P, QT, 2], fp32)
        rstd2 = sb("rstd2", [P, 2, QT], fp32)
        xn2 = sb("xn2", [P, QT, D], fp32)
        xn2_t = sb("xn2_t", [P, 2, QT, DC, P], fp16)
        rows = sb("rows", [P, 2, QT, ROW], fp16)
        gate_sb = sb("gate_sb", [P, DC, E], fp32)
        gate_w = sb("gate_w", [P, 2, DC, E], fp16)
        logits = sb("logits", [P, QT, E], fp32)
        top = sb("top", [P, QT, E], fp32)
        top_i = sb("top_i", [P, QT, E], u32)
        hot = sb("hot", [P, TOP, QT, E], fp32)
        both = sb("both", [P, 5, E], fp16)
        rank = sb("rank", [P, QT, E], fp32)
        mixed = sb("mixed", [P, TOP, QT, E], fp32)
        picked = sb("picked", [P, TOP, QT], fp32)
        put = sb("put", [P, TOP, QT], fp32)
        place_u = sb("place_u", [P, 2, TOP, QT], u32)
        logit = sb("logit", [P, TOP, TILES], fp32)
        next_row = sb("next_row", [P, E], fp32)
        block_ids = sb("block_ids", [1, NB], fp32)
        end_row = sb("end_row", [1, E], i32)
        zero = sb("zero", [P, ROW], fp16)
        scrap = sb("scrap", [P, 1], fp32)
        powers = sb("powers", [P, KT], fp32)

        flat = t_sb[:, :, :].rearrange("p s w -> p (s w)")
        taken = [0]

        def early(width, dt=fp32):
            words = width if dt == fp32 else width // 2
            piece = flat[:, taken[0]:taken[0] + words]
            taken[0] += words
            return piece if dt == fp32 else piece.bitcast(dt)

        x_all = early(TILES * D).rearrange("p (t d) -> p t d", d=D)
        wq_sb = early(DC * D).rearrange("p (c d) -> p c d", c=DC)
        wk_sb = early(DC * D).rearrange("p (c d) -> p c d", c=DC)
        wv_sb = early(DC * D).rearrange("p (c d) -> p c d", c=DC)
        wv_w = [early(DC * D, fp16).rearrange("p (c d) -> p c d", c=DC) for _ in range(2)]
        xn = early(2 * KT * D).rearrange("p (r s d) -> p r s d", r=2, s=KT)
        xn_w = [early(2 * KT * D, fp16).rearrange("p (r s d) -> p r s d", r=2, s=KT) for _ in range(2)]
        stats = early(TILES * 6).rearrange("p (t s) -> p t s", s=6)
        mv = early(TILES * 2).rearrange("p (t s) -> p t s", s=2)
        var = early(TILES)
        rstd = early(TILES)
        amax = early(2)
        amax_all = early(2)
        assert taken[0] <= SLOTS * GW

        taken[0] = 0
        region, count, blocks, b_incl, b_first, ones_e = (early(E) for _ in range(6))
        delta = kept["delta"][:, :]
        each = early(NB * E).rearrange("p (b e) -> p b e", e=E)[0:1]
        eidf, row0f = (early(NB)[0:1] for _ in range(2))

        INV_M, INV_V, S_M, S_V, EXP_SCALE, OUT_SCALE = range(6)

        def col(i):
            return scales[:, i:i + 1]

        tr_ps = [[ps_s[i][:, 2 * h:2 * h + 2, :].rearrange("p a b -> p (a b)").bitcast(fp16)
                  .rearrange("p (c q) -> p c q", c=DC) for h in range(2)] for i in range(2)]
        first_q = ps_s[0][:, 0:2, :].rearrange("p a b -> p (a b)")
        v_ps = [t[:, :, :].rearrange("p a (b d) -> p (a b) d", d=D) for t in (ps_misc, ps_out)]

        s_x_load = [sem(f"s_x_load{i}") for i in range(GROUPS)]
        s_w = sem("s_w")
        s_gate = sem("s_gate")
        s_ghi = sem("s_ghi")
        s_glo = sem("s_glo")
        s_const = sem("s_const")
        s_stats = sem("s_stats")
        s_mv = sem("s_mv")
        s_var = sem("s_var")
        s_rstd = sem("s_rstd")
        s_chain = sem("s_chain")
        s_m_ps = sem("s_m_ps")
        s_amax = sem("s_amax")
        s_amax_all = sem("s_amax_all")
        s_scale = sem("s_scale")
        s_whi = sem("s_whi")
        s_wlo = sem("s_wlo")
        s_xn = sem("s_xn")
        s_xhi = sem("s_xhi")
        s_xlo = sem("s_xlo")
        s_tr = sem("s_tr")
        s_khi = sem("s_khi")
        s_klo = sem("s_klo")
        s_v_ps = sem("s_v_ps")
        s_vhi = sem("s_vhi")
        s_vlo = sem("s_vlo")
        s_adj = [sem(f"s_adj{g}") for g in range(GROUPS)]
        s_mask = sem("s_mask")
        s_q_ps = sem("s_q_ps")
        s_qhi = sem("s_qhi")
        s_qlo = sem("s_qlo")
        s_scores = sem("s_scores")
        s_evac = sem("s_evac")
        s_max = sem("s_max")
        s_max_t = sem("s_max_t")
        s_mcol = sem("s_mcol")
        s_diag = sem("s_diag")
        s_mrow_ps = sem("s_mrow_ps")
        s_mrow = sem("s_mrow")
        s_sub = sem("s_sub")
        s_exp = sem("s_exp")
        s_phi = sem("s_phi")
        s_plo = sem("s_plo")
        s_pv = sem("s_pv")
        s_den = sem("s_den")
        s_x1 = sem("s_x1")
        s_xin = [sem(f"s_xin{i}") for i in range(2)]
        s_x1_out = [sem(f"s_x1_out{i}") for i in range(2)]
        s_stats2 = sem("s_stats2")
        s_mv2 = sem("s_mv2")
        s_var2 = sem("s_var2")
        s_rstd2 = sem("s_rstd2")
        s_xn2 = sem("s_xn2")
        s_rhi = sem("s_rhi")
        s_rlo = sem("s_rlo")
        s_xn2_ps = sem("s_xn2_ps")
        s_xn2_t = sem("s_xn2_t")
        s_logit_ps = sem("s_logit_ps")
        s_both = sem("s_both")
        s_rank_ps = sem("s_rank_ps")
        s_pick = sem("s_pick")
        s_put = sem("s_put")
        s_place = sem("s_place")
        s_route = sem("s_route")
        s_scatter = [sem(f"s_scatter{i}") for i in range(2)]
        s_end_row = sem("s_end_row")
        s_first_w = [sem(f"s_first_w{i}") for i in range(STAGES)]
        s_diff = sem("s_diff")
        s_expd = sem("s_expd")
        s_pad = sem("s_pad")
        s_fill = sem("s_fill")

        x_t = x.rearrange("(t p) d -> p t d", p=P)
        x1_t = x1_d.rearrange("(t p) d -> p t d", p=P)
        adj_t = adj.rearrange("(g s p) i -> p g s i", p=P, s=KT)

        def alive(b):
            return not isinstance(b, int) or 0 <= b < BLOCKS

        def alive_step(at):
            return not isinstance(at, int) or 0 <= at < STEPS

        def passes(eng, step):
            for it in range(PEELED):
                for n in range(SLOTS):
                    step(n, it)
            with eng.Fori(PEELED, PASSES - 1) as it:
                for n in range(SLOTS):
                    step(n, it)
            for n in range(SLOTS):
                step(n, PASSES - 1)
            for n in range(DRAIN):
                step(n, PASSES)

        def where(n, it):
            return it * SLOTS + n, it * (SLOTS // GROUPS) + n // GROUPS, n % GROUPS

        def pad(eng, experts):
            eng.wait_ge(s_end_row, 1)
            for e in experts:
                end = eng.value_load(end_row[0:1, e:e + 1], min_val=e * REGION, max_val=e * REGION + N)
                eng.dma_start(xs_d[bass.ds(end, TB), :].rearrange("(q p) r -> p q r", p=P),
                              zero[:, None, :].to_broadcast([P, TBT, ROW])).then_inc(s_pad, 16)

        block = ctx.enter_context(nc.Block())

        @block.sync
        def _(sp):
            for i in range(GROUPS):
                sp.dma_start(x_all[:, KT * i:KT * (i + 1), :], x_t[:, KT * i:KT * (i + 1), :]
                             ).then_inc(s_x_load[i], 16)
                if i == 1:
                    sp.dma_start(wq_sb, wq.rearrange("(c p) d -> p c d", p=P)).then_inc(s_w, 16)
                    sp.dma_start(wk_sb, wk.rearrange("(c p) d -> p c d", p=P)).then_inc(s_w, 16)
                    sp.dma_start(wv_sb, wv_t.rearrange("(c p) d -> p c d", p=P)).then_inc(s_w, 16)
            sp.dma_start(gate_sb[:, :, :], gate_t.rearrange("(c p) e -> p c e", p=P)).then_inc(s_gate, 16)
            for g in range(GROUPS):
                sp.dma_start(adj_sb[:, g, :, :], adj_t[:, g, :, 0:2 * QB]).then_inc(s_adj[g], 16)
            for r in range(2):
                sp.dma_start(x_io[:, r, :, :], x_t[:, r * QT:r * QT + QT, :]).then_inc(s_xin[r], 16)

            sp.wait_ge(s_const, FILLED)
            fill = ys_d.rearrange("(a q p) d -> p a q d", p=P, a=FILLS)
            for i in range(FILLS):
                sp.dma_start(fill[:, i, :, :], zero[:, :].bitcast(fp32)[:, None, :]
                             .to_broadcast([P, ys_d.shape[0] // P // FILLS, D])).then_inc(s_fill, 16)

            def one_pass(it):
                adj_src = [adj_t[:, g, :, bass.ds(it * (2 * QB), 2 * QB)] for g in range(GROUPS)]
                x_src = [x_t[:, bass.ds(it * (2 * QT) + r * QT, QT), :] for r in range(2)]
                x1_dst = [x1_t[:, bass.ds(it * (2 * QT) - (2 - r) * QT, QT), :] for r in range(2)]
                if not isinstance(it, int):
                    for ap in adj_src:
                        sp.compute_val(ap.offset)
                    for ap in x_src + x1_dst:
                        sp.compute_val(ap.offset * 4)
                for g in range(GROUPS):
                    sp.wait_ge(s_mask, it * SLOTS - GROUPS + g + 1)
                    sp.dma_start(adj_sb[:, g, :, :], adj_src[g]).then_inc(s_adj[g], 16)
                for r in range(2):
                    sp.wait_ge(s_x1, it * 2 - 1 + r)
                    sp.dma_start(x1_dst[r], x_io[:, r, :, :]).then_inc(s_x1_out[r], 16)
                    sp.wait_ge(s_xn2, it * 2 - 1 + r)
                    sp.wait_ge(s_x1_out[r], it * 16)
                    sp.dma_start(x_io[:, r, :, :], x_src[r]).then_inc(s_xin[r], 16)

            with sp.Fori(1, PASSES) as it:
                one_pass(it)
            sp.wait_ge(s_mask, STEPS)
            sp.wait_ge(s_mrow_ps, BLOCKS)
            for i in range(3):
                load_piece(sp, weights, stage, i, s_first_w)
            for r in range(2):
                sp.wait_ge(s_x1, BLOCKS - 1 + r)
                at = TILES - (2 - r) * QT
                sp.dma_start(x1_t[:, at:at + QT, :], x_io[:, r, :, :]).then_inc(s_x1_out[r], 16)
            sp.wait_ge(s_const, FILLED)
            pad(sp, range(0, E // 2))
            for r in range(2):
                sp.wait_ge(s_x1_out[r], 16 * BLOCKS // 2)
            for i in range(3):
                sp.wait_ge(s_first_w[i], 16)
            sp.wait_ge(s_pad, 16 * E)
            sp.wait_ge(s_fill, 16 * FILLS)

        @block.gpsimd
        def _(pool):
            pool.memset(ident[:, :], 0.0).then_inc(s_const, 1)
            pool.memset(ones[:, :], 1.0).then_inc(s_const, 1)
            pool.memset(tri16[:, :], 1.0).then_inc(s_const, 1)
            pool.memset(powers[:, :], -0.5).then_inc(s_const, 1)
            pool.memset(val[0][:, :, D:VP], 1.0).then_inc(s_const, 1)
            pool.memset(val[1][:, :, D:VP], 0.0).then_inc(s_const, 1)
            pool.memset(zero[:, :], 0.0).then_inc(s_const, 1)
            pool.wait_ge(s_const, FILLED)
            pool.affine_select(out=ident[:, :], in_=ident[:, :], compare_op=ALU.not_equal, fill=1.0,
                               base=0, pattern=[[-1, P]], channel_multiplier=1).then_inc(s_const, 1)
            pool.affine_select(out=tri16[:, :], in_=tri16[:, :], compare_op=ALU.is_gt, fill=0.0,
                               base=0, pattern=[[1, P]], channel_multiplier=-1).then_inc(s_const, 1)
            pool.iota(expert_ids[:, :].bitcast(i32), pattern=[[1, E]], base=0, channel_multiplier=0
                      ).then_inc(s_const, 1)
            pool.iota(next_row[:, :].bitcast(i32), pattern=[[REGION, E]], base=0, channel_multiplier=0
                      ).then_inc(s_const, 1)
            pool.iota(block_ids[:, :].bitcast(i32), pattern=[[1, NB]], base=0, channel_multiplier=0
                      ).then_inc(s_const, 1)
            pool.wait_ge(s_const, COUNTED)
            pool.tensor_copy(block_ids[:, :], block_ids[:, :].bitcast(i32)).then_inc(s_const, 1)
            pool.memset(ones16[:, :], 1.0).then_inc(s_const, 1)
            pool.memset(both[:, :, :], 0.0).then_inc(s_const, 1)
            pool.tensor_copy(ident16[:, :], ident[:, :]).then_inc(s_const, 1)
            pool.tensor_copy(expert_ids[:, :], expert_ids[:, :].bitcast(i32)).then_inc(s_const, 1)
            pool.tensor_copy(next_row[:, :], next_row[:, :].bitcast(i32)).then_inc(s_const, 1)

            def inverse_root(dst, src, tmp, ready, s_sum, s_done, n):
                if not isinstance(n, int):
                    pool.compute_val(n)
                pool.wait_ge(s_const, CONSTANTS)
                pool.wait_ge(ready, n)
                pool.tensor_scalar(tmp, src, EPS, 1.0, ALU.add, ALU.mult).then_inc(s_sum, 1)
                pool.wait_ge(s_sum, n)
                pool.tensor_tensor(dst, tmp, powers[:, 0:dst.shape[1]], ALU.pow).then_inc(s_done, 1)

            def first_norm(i):
                cut = slice(i * KT, (i + 1) * KT)
                inverse_root(rstd[:, cut], mv[:, cut, 1], var[:, cut], s_mv, s_var, s_rstd, i + 1)

            first_norm(0)
            for i in range(GROUPS):
                pool.wait_ge(s_xn, i + 1)
                pool.wait_ge(s_xhi, i + 1)
                if i >= 2:
                    pool.wait_ge(s_tr, i - 1)
                pool.tensor_tensor(xn_w[1][:, i % 2, :, :], xn[:, i % 2, :, :], xn_w[0][:, i % 2, :, :], ALU.subtract
                                   ).then_inc(s_xlo, 1)
                if i == 0:
                    first_norm(1)
                    pool.wait_ge(s_amax, 2)
                    pool.partition_all_reduce(amax_all, amax, P, RMAX).then_inc(s_amax_all, 1)
                if i + 2 < GROUPS:
                    first_norm(i + 2)

            def second_norm(b):
                if not before_start(b - 1):
                    pool.wait_ge(s_xn2, b)
                inverse_root(rstd2[:, 0, :], mv2[:, :, 1], rstd2[:, 1, :], s_mv2, s_var2, s_rstd2, b + 1)

            def scatter(b, r):
                pool.wait_ge(s_const, CONSTANTS)
                pool.wait_ge(s_route, b + 1)
                pool.wait_ge(s_rhi, b + 1)
                pool.wait_ge(s_rlo, b + 1)
                for q in range(QT):
                    for k in range(TOP):
                        pool.indirect_dma_start(
                            xs_d, bass.IndirectOffsetOnAxis(ap=place_u[:, r, k, q:q + 1], axis=0),
                            rows[:, r, q, :], None).then_inc(s_scatter[r], 16)

            def pair(it):
                for r in range(2):
                    b = it * 2 + r
                    if alive(b):
                        second_norm(b)
                    if alive(b - 1):
                        scatter(b - 1, (r + 1) % 2)

            pair(0)
            with pool.Fori(1, BLOCKS // 2) as it:
                pair(it)
            pair(BLOCKS // 2)
            for r in range(2):
                pool.wait_ge(s_scatter[r], 16 * TOP * QT * BLOCKS // 2)

        @block.tensor
        def _(pe):
            pe.wait_ge(s_w, 48)
            for c in range(DC):
                for k in range(DC):
                    last = pe.matmul(ps_a[:, c * D:(c + 1) * D], wq_sb[:, k, c * P:(c + 1) * P], wk_sb[:, k, :],
                                     start=(k == 0), stop=(k == DC - 1))
            last.then_inc(s_m_ps, 1)
            pe.wait_ge(s_const, CONSTANTS)

            def transposes(i):
                pe.wait_ge(s_xhi, i + 1)
                pe.wait_ge(s_xlo, i + 1)
                if i >= 2:
                    pe.wait_ge(s_khi, i - 1)
                    pe.wait_ge(s_klo, i - 1)
                for h in range(2):
                    for c in range(DC):
                        for s in range(KT):
                            last = pe.transpose(tr_ps[i % 2][h][:, c, s * P:(s + 1) * P],
                                                xn_w[h][:, i % 2, s, c * P:(c + 1) * P], ident16[:, :])
                last.then_inc(s_tr, 1)

            def values(i):
                pe.wait_ge(s_khi, i + 1)
                pe.wait_ge(s_klo, i + 1)
                if i == 0:
                    pe.wait_ge(s_whi, 2)
                    pe.wait_ge(s_wlo, 2)
                if i >= 2:
                    pe.wait_ge(s_vhi, i - 1)
                    pe.wait_ge(s_vlo, i - 1)
                terms = [(c, a, w) for c in range(DC) for a, w in TERMS]
                for s in range(KT):
                    t = i * KT + s
                    for j, (c, a, w) in enumerate(terms):
                        last = pe.matmul(v_ps[i % 2][:, s, :], kT[a][:, c, t * P:(t + 1) * P], wv_w[w][:, c, :],
                                         start=(j == 0), stop=(j == len(terms) - 1))
                last.then_inc(s_v_ps, 1)

            def queries(b, bank):
                terms = [(k, a, w) for k in range(DC) for a, w in TERMS]
                for c in range(DC):
                    for i, (k, a, w) in enumerate(terms):
                        last = pe.matmul(bank[:, c * QB:(c + 1) * QB], m_w[w][:, k, c * P:(c + 1) * P],
                                         kT[a][:, k, bass.ds(b * QB, QB)],
                                         start=(i == 0), stop=(i == len(terms) - 1))
                last.then_inc(s_q_ps, 1)

            for i in range(GROUPS + 1):
                if i < GROUPS:
                    transposes(i)
                if i == GROUPS:
                    pe.wait_ge(s_khi, GROUPS - 1)
                    pe.wait_ge(s_klo, GROUPS - 1)
                    queries(0, first_q)
                if i >= 1:
                    values(i - 1)
            pe.wait_ge(s_khi, GROUPS)
            pe.wait_ge(s_klo, GROUPS)

            def scores(n, at):
                g, r = n % GROUPS, n // GROUPS % 2
                if not before_start(at - 2):
                    pe.wait_ge(s_evac, at - 1)
                terms = [(c, a, w) for c in range(DC) for a, w in TERMS]
                for s in range(KT):
                    kt = g * KT + s
                    for i, (c, a, w) in enumerate(terms):
                        last = pe.matmul(ps_s[n % 2][:, s, :], kT[a][:, c, kt * P:(kt + 1) * P],
                                         q_t[w][:, r, c, :], start=(i == 0), stop=(i == len(terms) - 1))
                last.then_inc(s_scores, 1)

            def maxima_transposed(b):
                pe.wait_ge(s_max, (b + 1) * MAXIMA)
                for q in range(QT):
                    last = pe.transpose(ps_b[:, q * P:(q + 1) * P], block_max[:, q * P:(q + 1) * P], ident[:, :])
                last.then_inc(s_max_t, 1)

            def maxima_spread(b):
                pe.wait_ge(s_diag, (b + 1) * QT)
                pe.matmul(ps_b[:, 0:QB], ones[:, :], diag[:, :, :].rearrange("p q k -> p (q k)"),
                          start=True, stop=True).then_inc(s_mrow_ps, 1)

            def values_product(n, m):
                g, slot = (n - PV_LAG) % GROUPS, (n - PV_LAG) % RING
                pe.wait_ge(s_phi, m + 1)
                pe.wait_ge(s_plo, m + 1)
                for q in range(QT):
                    for s in range(KT):
                        kt = g * KT + s
                        for a, w in TERMS:
                            width = VW if w == 0 else D
                            last = pe.matmul(ps_o[q][:, 0:width],
                                             (p_hi, p_lo)[a][:, slot, s * QB + q * P:s * QB + (q + 1) * P],
                                             val[w][:, kt, 0:width],
                                             start=(g == 0 and s == 0 and (a, w) == TERMS[0]),
                                             stop=(g == GROUPS - 1 and s == KT - 1 and (a, w) == TERMS[-1]))
                last.then_inc(s_pv, 1)

            def tokens_transposed(b, r):
                pe.wait_ge(s_rhi, b + 1)
                pe.wait_ge(s_rlo, b + 1)
                if not before_start(b - 1):
                    pe.wait_ge(s_place, b)
                dst = ps_a.bitcast(fp16)
                for h in range(2):
                    for q in range(QT):
                        for c in range(DC):
                            at = ((h * QT + q) * DC + c) * P
                            last = pe.transpose(dst[:, at:at + P], rows[:, r, q, h * D + c * P:h * D + (c + 1) * P],
                                                ident16[:, :])
                last.then_inc(s_xn2_ps, 1)

            def gate(b):
                if isinstance(b, int) and b == 0:
                    pe.wait_ge(s_ghi, 1)
                    pe.wait_ge(s_glo, 1)
                pe.wait_ge(s_xn2_t, b + 1)
                terms = [(c, a, w) for c in range(DC) for a, w in TERMS]
                for q in range(QT):
                    for i, (c, a, w) in enumerate(terms):
                        last = pe.matmul(ps_a[:, q * E:(q + 1) * E], xn2_t[:, a, q, c, :], gate_w[:, w, c, :],
                                         start=(i == 0), stop=(i == len(terms) - 1))
                last.then_inc(s_logit_ps, 1)

            def ranks(b):
                pe.wait_ge(s_both, b + 1)
                for i, (w, at) in enumerate(((tri16, 2), (ones16, 1), (ones16, 0))):
                    last = pe.matmul(ps_a[:, 0:(QT + 1) * E], w[:, :],
                                     both[:, at:at + QT + 1, :].rearrange("p q e -> p (q e)"),
                                     start=(i == 0), stop=(i == 2))
                last.then_inc(s_rank_ps, 1)


            def step(n, it):
                at, b, g = where(n, it)
                if alive(b):
                    if g == 0:
                        pe.wait_ge(s_qhi, b + 1)
                        pe.wait_ge(s_qlo, b + 1)
                    scores(n, at)
                    if g == 4 and alive(b + 1):
                        if alive(b - 1):
                            pe.wait_ge(s_mrow, b)
                        if isinstance(b, int) and b == 0:
                            pe.wait_ge(s_vlo, GROUPS)
                            pe.wait_ge(s_vhi, GROUPS)
                        queries(b + 1, ps_b)
                if alive(b - 1):
                    if g == 0:
                        maxima_transposed(b - 1)
                    if g == 1:
                        maxima_spread(b - 1)
                if alive_step(at - PV_LAG):
                    if (n - PV_LAG) % GROUPS == 0 and not before_start(at - PV_LAG - GROUPS):
                        pe.wait_ge(s_x1, it * (SLOTS // GROUPS) + (n - PV_LAG) // GROUPS)
                    values_product(n, at - PV_LAG)
                if g == 7 and alive(b - 2):
                    tokens_transposed(b - 2, n // GROUPS % 2)
                if g == 1 and alive(b - 3):
                    gate(b - 3)
                if g == 3 and alive(b - 3):
                    ranks(b - 3)

            passes(pe, step)

        @block.scalar
        def _(act):
            def query_high(b, r, bank):
                act.wait_ge(s_q_ps, b + 1)
                act.activation(q_t[0][:, r, :, :], bank.rearrange("p (c q) -> p c q", c=DC), ACT.Copy,
                               scale=0.25).then_inc(s_qhi, 1)

            for i in range(GROUPS + 2):
                if i == 1:
                    act.wait_ge(s_scale, 1)
                    act.activation(m_w[0][:, :, :], ps_a.rearrange("p (c d) -> p c d", c=DC), ACT.Copy,
                                   scale=col(S_M)).then_inc(s_whi, 1)
                    act.activation(wv_w[0], wv_sb, ACT.Copy, scale=col(S_V)).then_inc(s_whi, 1)
                if i < GROUPS:
                    act.wait_ge(s_xn, i + 1)
                    if i >= 2:
                        act.wait_ge(s_tr, i - 1)
                    act.activation(xn_w[0][:, i % 2, :, :], xn[:, i % 2, :, :], ACT.Copy).then_inc(s_xhi, 1)
                if 1 <= i <= GROUPS:
                    act.wait_ge(s_tr, i)
                    act.activation(kT[0][:, :, (i - 1) * KT * P:i * KT * P], tr_ps[(i - 1) % 2][0],
                                   ACT.Copy).then_inc(s_khi, 1)
                    act.activation(kT[1][:, :, (i - 1) * KT * P:i * KT * P], tr_ps[(i - 1) % 2][1],
                                   ACT.Copy).then_inc(s_klo, 1)
                if i == GROUPS + 1:
                    query_high(0, 0, first_q)
                if i >= 2:
                    act.wait_ge(s_v_ps, i - 1)
                    act.activation(val[0][:, (i - 2) * KT:(i - 1) * KT, 0:D], v_ps[i % 2], ACT.Copy, scale=0.25
                                   ).then_inc(s_vhi, 1)

            def make_mask(n, it):
                at, _, g = where(n, it)
                act.wait_ge(s_adj[g], it * 16 + 16)
                if not before_start(at - 2):
                    act.wait_ge(s_evac, at - 1)
                h = n // GROUPS % 2
                act.activation(mask[:, n % 2, :].rearrange("p (s q) -> p s q", s=KT),
                               adj_sb[:, g, :, h * QB:(h + 1) * QB], ACT.Copy, scale=BIG, bias=-BIG
                               ).then_inc(s_mask, 1)

            make_mask(0, 0)
            act.wait_ge(s_gate, 16)
            act.activation(gate_w[:, 0, :, :], gate_sb[:, :, :], ACT.Copy, scale=GATE_SCALE).then_inc(s_ghi, 1)

            def step(n, it):
                at, b, g = where(n, it)
                if alive_step(at) and alive_step(at + 1):
                    make_mask((n + 1) % SLOTS, it + (n + 1) // SLOTS)
                if g == 6 and alive(b - 2):
                    r = n // GROUPS % 2
                    act.wait_ge(s_xn2, b - 1)
                    if alive(b - 4):
                        act.wait_ge(s_scatter[r], 16 * TOP * QT * (it - 1))
                    act.activation(rows[:, r, :, 0:D], xn2[:, :, :], ACT.Copy).then_inc(s_rhi, 1)
                if g == 0 and alive(b - 3):
                    act.wait_ge(s_xn2_ps, b - 2)
                    if alive(b - 4):
                        act.wait_ge(s_logit_ps, b - 3)
                    act.activation(xn2_t[:, :, :, :, :].rearrange("p h q c k -> p (h q c k)"), ps_a.bitcast(fp16),
                                   ACT.Copy).then_inc(s_xn2_t, 1)
                if g == 1 and alive(b - 1):
                    act.wait_ge(s_mrow_ps, b)
                    if not before_start(b - 3):
                        act.wait_ge(s_sub, (b - 2) * GROUPS)
                    act.activation(m_row[:, (n // GROUPS + 1) % 2, :], ps_b[:, 0:QB], ACT.Copy
                                   ).then_inc(s_mrow, 1)
                if g == 5 and alive(b) and alive(b + 1):
                    query_high(b + 1, (n // GROUPS + 1) % 2, ps_b)
                m = at - SUB_LAG
                if alive_step(m):
                    slot = (n - SUB_LAG) % SLOTS
                    act.wait_ge(s_sub, m + 1)
                    if not before_start(m - 2):
                        act.wait_ge(s_plo, m - 1)
                    act.activation(e_sb[:, (n - SUB_LAG) % 2, :], t_sb[:, slot, :], ACT.Exp,
                                   scale=col(EXP_SCALE)).then_inc(s_exp, 1)
                    if not before_start(m - RING):
                        act.wait_ge(s_pv, m - RING + 1)
                    act.activation(p_hi[:, (n - SUB_LAG) % RING, :], t_sb[:, slot, :], ACT.Exp,
                                   scale=col(EXP_SCALE)).then_inc(s_phi, 1)

            passes(act, step)
            pad(act, range(E // 2, E))
            act.wait_ge(s_diff, 1)
            act.activation(kept["e_top"][:, :], kept["e_top"][:, :], ACT.Exp).then_inc(s_expd, 1)
            act.wait_ge(s_expd, 1)
            act.activation(scrap[:, :], kept["e_top"][:, 0:1], ACT.Silu)

        @block.vector
        def _(dve):
            chain = [0]

            def link(ins):
                chain[0] += 1
                ins.then_inc(s_chain, 1)
                dve.wait_ge(s_chain, chain[0])

            def statistics(i):
                dve.wait_ge(s_x_load[i], 16)
                for t in range(i * KT, (i + 1) * KT):
                    last = dve.bn_stats(stats[:, t, :], x_all[:, t, :])
                last.then_inc(s_stats, 1)
                dve.wait_ge(s_stats, i + 1)
                for t in range(i * KT, (i + 1) * KT):
                    last = dve.bn_aggr(mv[:, t, :], stats[:, t, :])
                last.then_inc(s_mv, 1)

            def query_low(b, r, bank):
                dve.wait_ge(s_qhi, b + 1)
                dve.scalar_tensor_tensor(q_t[1][:, r, :, :], bank.rearrange("p (c q) -> p c q", c=DC), 0.25,
                                         q_t[0][:, r, :, :], ALU.mult, ALU.subtract).then_inc(s_qlo, 1)

            def weight_scales():
                link(dve.tensor_scalar(amax, amax_all, 2.0 ** -100, None, ALU.max))
                link(dve.tensor_single_scalar(amax.bitcast(u32), amax.bitcast(u32), 0x7F800000, ALU.bitwise_and))
                link(dve.tensor_scalar(scales[:, INV_M:INV_V + 1], amax, 2.0 ** -8, None, ALU.mult))
                link(dve.reciprocal(scales[:, S_M:S_V + 1], scales[:, INV_M:INV_V + 1]))
                dve.tensor_scalar(scales[:, EXP_SCALE:OUT_SCALE + 1], scales[:, INV_M:INV_V + 1], 4.0, None, ALU.mult
                                  ).then_inc(s_scale, 1)
                dve.wait_ge(s_scale, 1)

            statistics(0)
            for i in range(GROUPS + 3):
                if i < GROUPS:
                    dve.wait_ge(s_rstd, i + 1)
                    if i >= 2:
                        dve.wait_ge(s_xhi, i - 1)
                        dve.wait_ge(s_xlo, i - 1)
                    for s in range(KT):
                        t = i * KT + s
                        last = dve.tensor_scalar(xn[:, i % 2, s, :], x_all[:, t, :], mv[:, t, 0:1], rstd[:, t:t + 1],
                                                 ALU.subtract, ALU.mult)
                    last.then_inc(s_xn, 1)
                if i == 0:
                    statistics(1)
                if i + 2 < GROUPS:
                    statistics(i + 2)
                if i == 0:
                    dve.wait_ge(s_m_ps, 1)
                    dve.tensor_reduce(amax[:, 0:1], ps_a, axis=AX.X, op=ALU.max,
                                      apply_absolute_value=True).then_inc(s_amax, 1)
                    dve.wait_ge(s_w, 48)
                    dve.tensor_reduce(amax[:, 1:2], wv_sb.rearrange("p c d -> p (c d)"), axis=AX.X, op=ALU.max,
                                      apply_absolute_value=True).then_inc(s_amax, 1)
                    dve.wait_ge(s_amax_all, 1)
                    weight_scales()
                if i == 1:
                    dve.wait_ge(s_whi, 1)
                    dve.scalar_tensor_tensor(m_w[1][:, :, :].rearrange("p c d -> p (c d)"), ps_a, col(S_M),
                                             m_w[0][:, :, :].rearrange("p c d -> p (c d)"), ALU.mult, ALU.subtract
                                             ).then_inc(s_wlo, 1)
                    dve.wait_ge(s_whi, 2)
                    dve.scalar_tensor_tensor(wv_w[1], wv_sb, col(S_V), wv_w[0], ALU.mult, ALU.subtract
                                             ).then_inc(s_wlo, 1)
                if i == GROUPS + 2:
                    query_low(0, 0, first_q)
                if i >= 3:
                    dve.wait_ge(s_vhi, i - 2)
                    dve.scalar_tensor_tensor(val[1][:, (i - 3) * KT:(i - 2) * KT, 0:D], v_ps[(i - 3) % 2], 0.25,
                                             val[0][:, (i - 3) * KT:(i - 2) * KT, 0:D],
                                             ALU.mult, ALU.subtract).then_inc(s_vlo, 1)

            dve.wait_ge(s_ghi, 1)
            dve.scalar_tensor_tensor(gate_w[:, 1, :, :], gate_sb[:, :, :], GATE_SCALE, gate_w[:, 0, :, :],
                                     ALU.mult, ALU.subtract).then_inc(s_glo, 1)

            def output(part, b, r, it):
                if part == 0:
                    dve.wait_ge(s_pv, (b + 1) * GROUPS)
                    for q in range(QT):
                        last = dve.tensor_scalar(den[:, 0, q:q + 1], ps_o[q][:, D:VW], 0.5, None, ALU.max)
                    last.then_inc(s_den, 1)
                if part == 1:
                    dve.wait_ge(s_den, b * 3 + 1)
                    dve.reciprocal(den[:, 1, :], den[:, 0, :]).then_inc(s_den, 1)
                if part == 2:
                    dve.wait_ge(s_den, b * 3 + 2)
                    dve.tensor_scalar(den[:, 2, :], den[:, 1, :], col(OUT_SCALE), None, ALU.mult).then_inc(s_den, 1)
                if part == 3:
                    dve.wait_ge(s_den, b * 3 + 3)
                    dve.wait_ge(s_xin[r], it * 16)
                    for q in range(QT):
                        last = dve.scalar_tensor_tensor(x_io[:, r, q, :], ps_o[q][:, 0:D], den[:, 2, q:q + 1],
                                                        x_io[:, r, q, :], ALU.mult, ALU.add)
                    last.then_inc(s_x1, 1)
                if part == 4:
                    dve.wait_ge(s_x1, b + 1)
                    for q in range(QT):
                        last = dve.bn_stats(stats2[:, q, :], x_io[:, r, q, :])
                    last.then_inc(s_stats2, 1)
                if part == 5:
                    dve.compute_val(b + 1)
                    dve.wait_ge(s_const, CONSTANTS)
                    dve.wait_ge(s_stats2, b + 1)
                    for q in range(QT):
                        last = dve.bn_aggr(mv2[:, q, :], stats2[:, q, :])
                    last.then_inc(s_mv2, 1)

            def normalised(b, r):
                dve.wait_ge(s_rstd2, b + 1)
                if not before_start(b - 1):
                    dve.wait_ge(s_rhi, b)
                    dve.wait_ge(s_rlo, b)
                for q in range(QT):
                    last = dve.tensor_scalar(xn2[:, q, :], x_io[:, r, q, :], mv2[:, q, 0:1], rstd2[:, 0, q:q + 1],
                                             ALU.subtract, ALU.mult)
                last.then_inc(s_xn2, 1)

            def row_low(b, r):
                dve.wait_ge(s_rhi, b + 1)
                dve.tensor_tensor(rows[:, r, :, D:ROW], xn2[:, :, :], rows[:, r, :, 0:D], ALU.subtract
                                  ).then_inc(s_rlo, 1)

            def choose(part, b, tiles):
                count = b * 6
                if part == 0:
                    dve.wait_ge(s_logit_ps, b + 1)
                    dve.tensor_scalar(logits[:, :, :].rearrange("p q e -> p (q e)"), ps_a[:, 0:QT * E],
                                      1.0 / GATE_SCALE, None, ALU.mult).then_inc(s_pick, 1)
                if part == 1:
                    dve.compute_val(count + 1)
                    dve.wait_ge(s_const, CONSTANTS)
                    dve.wait_ge(s_pick, count + 1)
                    for q in range(QT):
                        last = dve.max(top[:, q, :], logits[:, q, :])
                    last.then_inc(s_pick, 1)
                if part == 2:
                    dve.compute_val(count + 2)
                    dve.wait_ge(s_const, CONSTANTS)
                    dve.wait_ge(s_pick, count + 2)
                    for q in range(QT):
                        last = dve.max_index(top_i[:, q, :], top[:, q, :], logits[:, q, :])
                    last.then_inc(s_pick, 1)
                if part == 3:
                    dve.wait_ge(s_pick, count + 3)
                    dve.tensor_copy(logit[:, :, tiles], top[:, :, 0:TOP].rearrange("p q k -> p k q")
                                    ).then_inc(s_pick, 1)
                    dve.tensor_copy(picked[:, :, :], top_i[:, :, 0:TOP].rearrange("p q k -> p k q")
                                    ).then_inc(s_pick, 1)
                if part == 4:
                    dve.wait_ge(s_pick, count + 5)
                    dve.tensor_copy(chosen[:, :, tiles], picked[:, :, :])
                    dve.tensor_tensor(hot[:, :, :, :].rearrange("p k q e -> p (k q) e"),
                                      picked[:, :, :].rearrange("p k q -> p (k q)")[:, :, None]
                                      .to_broadcast([P, TOP * QT, E]),
                                      expert_ids[:, None, :].to_broadcast([P, TOP * QT, E]), ALU.is_equal
                                      ).then_inc(s_pick, 1)
                if part == 5:
                    dve.wait_ge(s_pick, count + 6)
                    dve.tensor_tensor(both[:, 2:4, :], hot[:, 0, :, :], hot[:, 1, :, :], ALU.add
                                      ).then_inc(s_both, 1)

            def put_down(part, b, r, tiles):
                if part == 0:
                    dve.wait_ge(s_rank_ps, b + 1)
                    ranks = ps_a[:, 0:QT * E].rearrange("p (q e) -> p q e", e=E)
                    dve.tensor_tensor(rank[:, :, :], ranks, next_row[:, None, :].to_broadcast([P, QT, E]), ALU.add
                                      ).then_inc(s_put, 1)
                if part == 1:
                    dve.wait_ge(s_put, b * 3 + 1)
                    dve.tensor_tensor(next_row[:, :], ps_a[:, QT * E:(QT + 1) * E], next_row[:, :], ALU.add
                                      ).then_inc(s_place, 1)
                    dve.tensor_tensor(mixed[:, :, :, :], hot[:, :, :, :],
                                      rank[:, None, :, :].to_broadcast([P, TOP, QT, E]), ALU.mult
                                      ).then_inc(s_put, 1)
                if part == 2:
                    dve.wait_ge(s_put, b * 3 + 2)
                    dve.tensor_reduce(put[:, :, :], mixed[:, :, :, :], axis=AX.X, op=ALU.add).then_inc(s_put, 1)
                if part == 3:
                    dve.wait_ge(s_put, b * 3 + 3)
                    dve.tensor_copy(place[:, :, tiles], put[:, :, :])
                    dve.tensor_copy(place_u[:, r, :, :], put[:, :, :]).then_inc(s_route, 1)

            def maximum(n, b, g):
                if g == 1:
                    if not before_start(b - 1):
                        dve.wait_ge(s_max, b * MAXIMA)
                    before = t_sb[:, n - 1, :]
                else:
                    dve.wait_ge(s_max, b * MAXIMA + g - 1)
                    before = run_max[:, :]
                dve.tensor_tensor(run_max[:, :], before, t_sb[:, n, :], ALU.max).then_inc(s_max, 1)

            dve.wait_ge(s_const, CONSTANTS)

            def step(n, it):
                at, b, g = where(n, it)
                r = n // GROUPS % 2
                if alive(b - 3):
                    tiles = bass.ds(it * (2 * QT) + (n // GROUPS - 3) * QT, QT)

                def small(part):
                    if g == 4 and alive(b - 2):
                        output(part, b - 2, r, it + n // SLOTS)
                    if g == 4 and alive(b - 3):
                        put_down(part, b - 3, (r + 1) % 2, tiles)
                    if g == 2 and alive(b - 3):
                        choose(part, b - 3, tiles)

                small(0)
                if alive(b) and g >= 2:
                    dve.wait_ge(s_evac, at)
                    maximum(n - 1, b, g - 1)
                small(1)
                m = at - SUB_LAG
                if alive_step(m):
                    dve.wait_ge(s_mrow, it * (SLOTS // GROUPS) + (n - SUB_LAG) // GROUPS + 1)
                    part = t_sb[:, (n - SUB_LAG) % SLOTS, :].rearrange("p (s q) -> p s q", s=KT)
                    row = m_row[:, (n - SUB_LAG) // GROUPS % 2, None, :].to_broadcast([P, KT, QB])
                    dve.tensor_tensor(part, part, row, ALU.subtract).then_inc(s_sub, 1)
                small(2)
                small(3)
                m = at - LO_LAG
                if alive_step(m):
                    dve.wait_ge(s_exp, m + 1)
                    dve.wait_ge(s_phi, m + 1)
                    if not before_start(m - RING):
                        dve.wait_ge(s_pv, m - RING + 1)
                    dve.tensor_tensor(p_lo[:, (n - LO_LAG) % RING, :], e_sb[:, (n - LO_LAG) % 2, :],
                                      p_hi[:, (n - LO_LAG) % RING, :], ALU.subtract).then_inc(s_plo, 1)
                small(4)
                if g == 5 and alive(b) and alive(b + 1):
                    query_low(b + 1, (r + 1) % 2, ps_b)
                if alive(b):
                    dve.wait_ge(s_scores, at + 1)
                    dve.wait_ge(s_mask, at + 1)
                    if not before_start(at - SLOTS):
                        dve.wait_ge(s_phi, at - SLOTS + 1)
                    dve.tensor_tensor(t_sb[:, n, :], ps_s[n % 2][:, :, :].rearrange("p s q -> p (s q)"),
                                      mask[:, n % 2, :], ALU.add).then_inc(s_evac, 1)
                small(5)
                if alive(b) and g == GROUPS - 1:
                    dve.wait_ge(s_evac, at + 1)
                    maximum(n, b, g)
                    dve.wait_ge(s_max, b * MAXIMA + g)
                    dve.tensor_tensor(run_max[:, 0:GW // 2], run_max[:, 0:GW // 2], run_max[:, GW // 2:GW],
                                      ALU.max).then_inc(s_max, 1)
                    dve.wait_ge(s_max, b * MAXIMA + g + 1)
                    if not before_start(b - 1):
                        dve.wait_ge(s_max_t, b)
                    dve.tensor_tensor(block_max[:, :], run_max[:, 0:QB], run_max[:, QB:2 * QB],
                                      ALU.max).then_inc(s_max, 1)
                if g == 0 and alive(b - 1):
                    dve.wait_ge(s_max_t, b)
                    dve.tensor_reduce(m_col[:, :], ps_b[:, 0:QB].rearrange("p (q k) -> p q k", q=QT),
                                      axis=AX.X, op=ALU.max).then_inc(s_mcol, 1)
                if g == 0 and alive(b - 1):
                    dve.wait_ge(s_mcol, b)
                    for q in range(QT):
                        if not before_start(b - 2):
                            dve.wait_ge(s_mrow_ps, b - 1)
                        dve.tensor_scalar(diag[:, q, :], ident[:, :], m_col[:, q:q + 1], -0.1 * BIG,
                                          ALU.mult, ALU.max).then_inc(s_diag, 1)
                if g == 5 and alive(b - 2):
                    normalised(b - 2, r)
                if g == 6 and alive(b - 2):
                    row_low(b - 2, r)

            passes(dve, step)
            dve.wait_ge(s_place, BLOCKS)
            dve.tensor_copy(end_row[:, :], next_row[0:1, :]).then_inc(s_end_row, 1)

            dve.tensor_tensor(kept["e_top"][:, :], logit[:, 1, :], logit[:, 0, :], ALU.subtract).then_inc(s_diff, 1)

            link(dve.tensor_scalar(region, expert_ids[:, :], float(REGION), None, ALU.mult))
            dve.tensor_scalar(ones_e, expert_ids[:, :], 0.0, 1.0, ALU.mult, ALU.add)
            link(dve.tensor_tensor(count, next_row[:, :], region, ALU.subtract))
            link(dve.tensor_scalar(count, count, 1.0 / TB, (TB - 1.0) / TB - 0.5 + 0.5 / TB, ALU.mult, ALU.add))
            link(dve.tensor_scalar(blocks, count, ROUND, ROUND, ALU.add, ALU.subtract))
            link(dve.tensor_tensor_scan(b_incl, ones_e, blocks, 0.0, ALU.mult, ALU.add))
            link(dve.tensor_tensor(b_first, b_incl, blocks, ALU.subtract))
            link(dve.scalar_tensor_tensor(delta, b_first, float(TB), region, ALU.mult, ALU.subtract))
            per_block = [1, NB, E]
            link(dve.tensor_tensor(each, block_ids[:, :, None].to_broadcast(per_block),
                                   b_incl[0:1, None, :].to_broadcast(per_block), ALU.is_ge))
            link(dve.tensor_reduce(eidf, each, axis=AX.X, op=ALU.add))
            link(dve.tensor_scalar(eidf, eidf, E - 1.0, None, ALU.min))
            link(dve.tensor_tensor(each, eidf[:, :, None].to_broadcast(per_block),
                                   expert_ids[0:1, None, :].to_broadcast(per_block), ALU.is_equal))
            link(dve.tensor_tensor(each, each, delta[0:1, None, :].to_broadcast(per_block), ALU.mult))
            link(dve.tensor_reduce(row0f, each, axis=AX.X, op=ALU.add))
            link(dve.scalar_tensor_tensor(row0f, block_ids[:, :], float(TB), row0f, ALU.mult, ALU.subtract))
            link(dve.tensor_scalar(row0f, row0f, next_row[0:1, E - 1:E], None, ALU.min))
            dve.tensor_copy(kept["eid"][:, :], eidf)
            dve.tensor_copy(kept["limits"][:, :], b_incl[0:1, E - 2:E])
            dve.tensor_copy(kept["row0"][:, :], row0f)


def experts(nc, weights, x1_d, xs_d, ys_d, out, kept, REGION, NB):
    N, D = x1_d.shape
    E, _, H = weights[0].shape
    DC = D // P
    TILES = N // P
    HC = H // P
    BU = 3
    assert NB % BU == 0 and HC % BU == 0
    PASSES = NB // BU
    S2_LAG = 2
    AHEAD = 3
    PIECES = 3 * E
    PARTS = 8
    PW = TILES // PARTS
    EARLY = range(0, 3)
    LATE = range(3, 6)
    SHARED = range(6, 8)
    W_SCALE = 2.0 ** 8
    A_INV = 1.0 / W_SCALE
    H_SCALE = 2.0 ** -5
    Y_INV = 1.0 / (W_SCALE * W_SCALE * H_SCALE)
    ROW = 2 * D

    ctx = ExitStack()
    with ctx:
        def sb(name, shape, dt):
            return ctx.enter_context(nc.sbuf_tensor(name, shape, dt))

        def pb(name, shape):
            return ctx.enter_context(nc.psum_tensor(name, shape, fp32))

        def sem(name):
            return ctx.enter_context(nc.semaphore(name))

        ps_ab = [pb(f"ps_ab{i}", [P, 2, TB]) for i in range(BU)]
        ps_y = [pb(f"ps_y{i}", [P, 512]) for i in range(TBT)]
        ps_t = [pb(f"ps_t{i}", [P, 512]) for i in range(2)]

        w_all = [sb(f"w_{h}", [P, E, 3, DC * H], fp16) for h in ("hi", "lo")]
        x_rows = sb("x_rows", [P, BU, TBT, ROW], fp16)
        xs_t = [sb(f"xs_t_{h}", [P, BU, DC, TB], fp16) for h in ("hi", "lo")]
        act_a = sb("act_a", [P, BU, TB], fp32)
        hid = sb("hid", [P, BU, TB], fp32)
        h_w = [sb(f"h_{h}", [P, BU, TB], fp16) for h in ("hi", "lo")]
        y_sb = sb("y_sb", [P, TBT, D], fp32)
        stage, ident16, y_at, mix, eid, row0, limits = (
            kept[name] for name in ("stage", "ident16", "y_at", "mix", "eid", "row0", "limits"))

        which = sb("which", [P, TOP * TILES, E], fp32)
        y_row = sb("y_row", [P, TOP, TILES], fp32)
        first_lower = sb("first_lower", [P, TILES], fp32)
        first_upper = sb("first_upper", [P, TILES], fp32)
        part = sb("part", [P, TOP, TILES], fp32)
        w_top = sb("w_top", [P, TOP, TILES], fp32)

        done_w = [w_all[h][:, 0:E - 1, :, :].rearrange("p e k n -> p (e k n)").bitcast(fp32) for h in range(2)]
        cut = TILES // 2
        y_low = done_w[0][:, 0:TILES * D].rearrange("p (t d) -> p t d", d=D)
        x1_sb = done_w[1][:, 0:TILES * D].rearrange("p (t d) -> p t d", d=D)
        assert (TILES + cut) * D <= (E - 1) * 3 * DC * H // 2
        y_high = [done_w[h][:, TILES * D:(TILES + cut) * D].rearrange("p (t d) -> p t d", d=D) for h in range(2)]

        s_stage = [sem(f"b_stage{i}") for i in range(STAGES)]
        s_whi = sem("b_whi")
        s_wlo = sem("b_wlo")
        s_split = sem("b_split")
        s_chain = sem("b_chain")
        s_rows = sem("b_rows")
        s_ready_13 = sem("b_ready_13")
        s_ready_2 = sem("b_ready_2")
        s_xr = [sem(f"b_xr{i}") for i in range(BU)]
        s_tps = sem("b_tps")
        s_txhi = sem("b_txhi")
        s_txlo = sem("b_txlo")
        s_ab = sem("b_ab")
        s_silu = sem("b_silu")
        s_hid = sem("b_hid")
        s_hhi = sem("b_hhi")
        s_hlo = sem("b_hlo")
        s_h_used = sem("b_h_used")
        s_y_ps = sem("b_y_ps")
        s_y = sem("b_y")
        s_ys = sem("b_ys")
        s_x1_in = [sem(f"b_x1_in{i}") for i in range(PARTS)]
        s_low_in = [sem(f"b_low_in{i}") for i in range(PARTS)]
        s_high_in = [sem(f"b_high_in{i}") for i in range(PARTS)]
        s_weighed = sem("b_weighed")
        s_weighed_low = sem("b_weighed_low")
        s_weighed_high = sem("b_weighed_high")
        s_early = sem("b_early")
        s_low_sum = sem("b_low_sum")
        s_half_sum = sem("b_half_sum")
        s_sum = [sem(f"b_sum{i}") for i in range(PARTS)]
        s_fin = sem("b_fin")

        x1_t = x1_d.rearrange("(t p) d -> p t d", p=P)
        out_t = out.rearrange("(t p) d -> p t d", p=P)
        ys_v = ys_d.rearrange("(q p) d -> p q d", p=P)

        def passes(eng, step):
            for n in range(BU):
                step(n, 0)
            with eng.Fori(1, PASSES - 1) as it:
                for n in range(BU):
                    step(n, it)
            for n in range(BU):
                step(n, PASSES - 1)

        def is_first(b):
            return isinstance(b, int) and b == 0

        def is_last(b):
            return isinstance(b, int) and b == NB - 1

        def tiles(i):
            return slice(i * PW, (i + 1) * PW)

        block = ctx.enter_context(nc.Block())

        @block.sync
        def _(sp):
            def step(n, it):
                b = it * BU + n
                at = sp.value_load(row0[0:1, bass.ds(b, 1)], min_val=0, max_val=E * REGION - TB)
                src = xs_d[bass.ds(at, TB), :].rearrange("(q p) r -> p q r", p=P)
                sp.compute_val(src.offset * 2)
                if not (isinstance(it, int) and it == 0):
                    sp.wait_ge(s_tps, b - BU + 1)
                sp.dma_start(x_rows[:, n, :, :], src).then_inc(s_xr[n], 16)

            passes(sp, step)
            before_last = sp.value_load(limits[0:1, 0:1], min_val=1, max_val=NB)
            sp.compute_val(before_last * 16)
            sp.wait_ge(s_ys, before_last * 16)
            for i in (*LATE, *SHARED):
                sp.dma_start(x1_sb[:, tiles(i), :], x1_t[:, tiles(i), :]).then_inc(s_x1_in[i], 16)
            for i in (*EARLY, *LATE[:2], SHARED[0], *LATE[2:], *SHARED[1:]):
                sp.wait_ge(s_sum[i], 1)
                sp.dma_start(out_t[:, tiles(i), :], x1_sb[:, tiles(i), :]).then_inc(s_fin, 16)
            sp.wait_ge(s_fin, 16 * PARTS)

        @block.gpsimd
        def _(pool):
            done = 0
            for i in range(2, PIECES):
                e, k = divmod(i, 3)
                if i >= STAGES:
                    pool.wait_ge(s_stage[i % STAGES], 16 * (i // STAGES))
                w = stage[:, i % STAGES, :]
                pool.tensor_scalar(w, w, W_SCALE, 0.0, ALU.mult, ALU.add).then_inc(s_split, 1)
                pool.wait_ge(s_split, done + 1)
                pool.tensor_scalar(w_all[0][:, e, k, :], w, 1.0, 0.0, ALU.mult, ALU.add).then_inc(s_split, 1)
                pool.wait_ge(s_split, done + 2)
                pool.tensor_tensor(w_all[1][:, e, k, :], w, w_all[0][:, e, k, :], ALU.subtract).then_inc(s_split, 1)
                done += 3
                if i + STAGES < PIECES or k >= 1:
                    pool.wait_ge(s_split, done)
                if i + STAGES < PIECES:
                    load_piece(pool, weights, stage, i + STAGES, s_stage)
                if i == 2:
                    for j in range(2):
                        pool.wait_ge(s_whi, j + 1)
                        pool.wait_ge(s_wlo, j + 1)
                        load_piece(pool, weights, stage, STAGES + j, s_stage)
                if k >= 1:
                    pool.sem_inc(s_ready_13 if k == 1 else s_ready_2, 1)
            before_last = pool.value_load(limits[0:1, 0:1], min_val=1, max_val=NB)
            in_all = pool.value_load(limits[0:1, 1:2], min_val=1, max_val=NB)
            pool.compute_val(before_last * 16)
            pool.wait_ge(s_rows, 1)
            pool.wait_ge(s_ys, before_last * 16)
            for i in range(PARTS):
                if i in EARLY:
                    pool.dma_start(x1_sb[:, tiles(i), :], x1_t[:, tiles(i), :]).then_inc(s_x1_in[i], 16)
                for t in range(i * PW, (i + 1) * PW):
                    pool.indirect_dma_start(y_low[:, t, :], None, ys_d,
                                            bass.IndirectOffsetOnAxis(ap=y_at[:, 0, t:t + 1], axis=0)
                                            ).then_inc(s_low_in[i], 16)
            for i in EARLY:
                pool.wait_ge(s_low_in[i], 16 * PW)
                for t in range(i * PW, (i + 1) * PW):
                    last = pool.tensor_scalar(y_low[:, t, :], y_low[:, t, :], mix[:, 0, t:t + 1], 0.0,
                                              ALU.mult, ALU.add)
                last.then_inc(s_weighed, 1)
                pool.wait_ge(s_weighed, i - EARLY[0] + 1)
                pool.wait_ge(s_x1_in[i], 16)
                pool.tensor_tensor(x1_sb[:, tiles(i), :], y_low[:, tiles(i), :], x1_sb[:, tiles(i), :], ALU.add
                                   ).then_inc(s_early, 1)
            pool.compute_val(in_all * 16)
            pool.wait_ge(s_rows, 1)
            pool.wait_ge(s_ys, in_all * 16)
            for t in range(TILES):
                pool.indirect_dma_start(y_high[t // cut][:, t % cut, :], None, ys_d,
                                        bass.IndirectOffsetOnAxis(ap=y_at[:, 1, t:t + 1], axis=0)
                                        ).then_inc(s_high_in[t // PW], 16)
            for i in SHARED:
                pool.wait_ge(s_weighed_low, i - SHARED[0] + 1)
                pool.wait_ge(s_x1_in[i], 16)
                pool.tensor_tensor(x1_sb[:, tiles(i), :], y_low[:, tiles(i), :], x1_sb[:, tiles(i), :], ALU.add
                                   ).then_inc(s_low_sum, 1)
            for i in SHARED:
                pool.wait_ge(s_low_sum, i - SHARED[0] + 1)
                pool.wait_ge(s_weighed_high, i - SHARED[0] + 1)
                high, at = y_high[i * PW // cut], slice(i * PW % cut, i * PW % cut + PW)
                pool.tensor_tensor(x1_sb[:, tiles(i), :], high[:, at, :], x1_sb[:, tiles(i), :], ALU.add
                                   ).then_inc(s_sum[i], 1)

        @block.tensor
        def _(pe):
            def transposes(n, b):
                if not is_first(b):
                    pe.wait_ge(s_txhi, b)
                    pe.wait_ge(s_txlo, b)
                for h in range(2):
                    dst = ps_t[h][:, :].bitcast(fp16)
                    for c in range(DC):
                        for q in range(TBT):
                            at = c * TB + q * P
                            last = pe.transpose(dst[:, at:at + P],
                                                x_rows[:, n % BU, q, h * D + c * P:h * D + (c + 1) * P], ident16[:, :])
                last.then_inc(s_tps, 1)

            def first(n, b, hc, e):
                if not (is_first(b) and hc < BU):
                    pe.wait_ge(s_hid, b * HC + hc - BU + 1)
                for i in range(2):
                    terms = [(c, a, w) for c in range(DC) for w, a in TERMS]
                    for j, (c, a, w) in enumerate(terms):
                        at = c * H + hc * P
                        last = pe.matmul(ps_ab[hc % BU][:, i, :],
                                         w_all[w][:, bass.ds(e, 1), i, at:at + P].rearrange("p e n -> p (e n)"),
                                         xs_t[a][:, n % BU, c, :], start=(j == 0), stop=(j == len(terms) - 1))
                last.then_inc(s_ab, 1)

            def second(b, hc, e):
                k = b * HC + hc
                if hc == 0 and not is_first(b):
                    pe.wait_ge(s_y, b)
                if hc == 0:
                    pe.wait_ge(s_ready_2, e + 1)
                pe.wait_ge(s_hhi, k + 1)
                pe.wait_ge(s_hlo, k + 1)
                for q in range(TBT):
                    for a, w in TERMS:
                        last = pe.matmul(ps_y[q][:, 0:D], h_w[a][:, hc % BU, q * P:(q + 1) * P],
                                         w_all[w][:, bass.ds(e, 1), 2, hc * D:(hc + 1) * D].rearrange("p e n -> p (e n)"),
                                         start=(hc == 0 and (a, w) == TERMS[0]),
                                         stop=(hc == HC - 1 and (a, w) == TERMS[-1]))
                last.then_inc(s_y_ps if hc == HC - 1 else s_h_used, 1)

            def expert(b):
                return pe.value_load(eid[0:1, bass.ds(b, 1)], min_val=0, max_val=E - 1)

            carried = [pe.alloc_register(f"carried{i}") for i in range(2)]
            pe.wait_ge(s_xr[0], 16)
            transposes(0, 0)
            held = {0: expert(0), -1: None}

            def step(n, it):
                b = it * BU + n
                if n == 0 and not (isinstance(it, int) and it == 0):
                    held[0], held[-1] = (pe.snap(r, min_val=0, max_val=E - 1) for r in carried)
                e, e_before = held[n], held[n - 1]
                pe.wait_ge(s_ready_13, e + 1)
                pe.wait_ge(s_txhi, b + 1)
                pe.wait_ge(s_txlo, b + 1)
                for hc in range(HC):
                    first(n, b, hc, e)
                    if hc == AHEAD and not is_last(b):
                        held[n + 1] = expert(b + 1)
                    if hc >= S2_LAG:
                        second(b, hc - S2_LAG, e)
                    elif not is_first(b):
                        second(b - 1, HC - S2_LAG + hc, e_before)
                    if hc == AHEAD and not is_last(b):
                        pe.wait_ge(s_xr[(n + 1) % BU], (it + (n + 1) // BU) * 16 + 16)
                        transposes(n + 1, b + 1)
                if n == BU - 1 and not is_last(b):
                    pe.reg_mov(carried[0], held[BU])
                    pe.reg_mov(carried[1], held[BU - 1])

            passes(pe, step)
            for hc in range(HC - S2_LAG, HC):
                second(NB - 1, hc, held[BU - 1])

        @block.scalar
        def _(act):
            for k in range(2):
                act.activation(w_all[0][:, 0, k, :], stage[:, k, :], ACT.Copy, scale=W_SCALE).then_inc(s_whi, 1)

            def x_high(b, n):
                act.wait_ge(s_tps, b + 1)
                act.activation(xs_t[0][:, n % BU, :, :], ps_t[0][:, :].bitcast(fp16)[:, 0:DC * TB]
                               .rearrange("p (c q) -> p c q", c=DC), ACT.Copy).then_inc(s_txhi, 1)

            def y_out(b):
                act.wait_ge(s_y_ps, b + 1)
                if not is_first(b):
                    act.wait_ge(s_ys, b * 16)
                for q in range(TBT):
                    last = act.activation(y_sb[:, q, :], ps_y[q][:, 0:D], ACT.Copy, scale=Y_INV)
                last.then_inc(s_y, 1)
                act.wait_ge(s_y, b + 1)
                act.dma_start(ys_v[:, bass.ds(b * TBT, TBT), :], y_sb[:, :, :]).then_inc(s_ys, 16)

            def silu(b, hc):
                act.wait_ge(s_ab, b * HC + hc + 1)
                act.activation(act_a[:, hc % BU, :], ps_ab[hc % BU][:, 0, :], ACT.Silu, scale=A_INV).then_inc(s_silu, 1)

            def high(b, hc):
                act.wait_ge(s_hid, b * HC + hc + 1)
                if not (is_first(b) and hc < BU):
                    if hc < BU:
                        act.wait_ge(s_h_used, b * (HC - 1) - (BU - 1) + hc if hc < BU - 1 else b * (HC - 1))
                        if hc == BU - 1:
                            act.wait_ge(s_y_ps, b)
                    else:
                        act.wait_ge(s_h_used, b * (HC - 1) + hc - BU + 1)
                act.activation(h_w[0][:, hc % BU, :], hid[:, hc % BU, :], ACT.Copy).then_inc(s_hhi, 1)

            x_high(0, 0)

            def step(n, it):
                b = it * BU + n
                for hc in range(HC):
                    if hc == S2_LAG and not is_first(b):
                        y_out(b - 1)
                    silu(b, hc)
                    if hc >= 1:
                        high(b, hc - 1)
                    elif not is_first(b):
                        high(b - 1, HC - 1)
                    if hc == AHEAD + 1 and not is_last(b):
                        x_high(b + 1, n + 1)

            passes(act, step)
            high(NB - 1, HC - 1)
            y_out(NB - 1)
            for i in SHARED:
                act.wait_ge(s_low_in[i], 16 * PW)
                for t in range(i * PW, (i + 1) * PW):
                    last = act.activation(y_low[:, t, :], y_low[:, t, :], ACT.Copy, scale=mix[:, 0, t:t + 1])
                last.then_inc(s_weighed_low, 1)
            for i in SHARED:
                act.wait_ge(s_high_in[i], 16 * PW)
                for t in range(i * PW, (i + 1) * PW):
                    high = y_high[t // cut][:, t % cut, :]
                    last = act.activation(high, high, ACT.Copy, scale=mix[:, 1, t:t + 1])
                last.then_inc(s_weighed_high, 1)
            act.wait_ge(s_ys, 16 * NB)

        @block.vector
        def _(dve):
            for k in range(2):
                dve.wait_ge(s_whi, k + 1)
                dve.scalar_tensor_tensor(w_all[1][:, 0, k, :], stage[:, k, :], W_SCALE, w_all[0][:, 0, k, :],
                                         ALU.mult, ALU.subtract).then_inc(s_wlo, 1)
            dve.wait_ge(s_wlo, 2)
            dve.sem_inc(s_ready_13, 1)

            def x_low(b, n):
                dve.wait_ge(s_tps, b + 1)
                dve.tensor_copy(xs_t[1][:, n % BU, :, :], ps_t[1][:, :].bitcast(fp16)[:, 0:DC * TB]
                                .rearrange("p (c q) -> p c q", c=DC)).then_inc(s_txlo, 1)

            def hidden(b, hc):
                k = b * HC + hc
                dve.wait_ge(s_silu, k + 1)
                if not (is_first(b) and hc < BU):
                    dve.wait_ge(s_hhi, k - BU + 1)
                    dve.wait_ge(s_hlo, k - BU + 1)
                dve.scalar_tensor_tensor(hid[:, hc % BU, :], act_a[:, hc % BU, :], H_SCALE, ps_ab[hc % BU][:, 1, :],
                                         ALU.mult, ALU.mult).then_inc(s_hid, 1)

            def low(b, hc):
                dve.wait_ge(s_hhi, b * HC + hc + 1)
                dve.tensor_tensor(h_w[1][:, hc % BU, :], hid[:, hc % BU, :], h_w[0][:, hc % BU, :], ALU.subtract
                                  ).then_inc(s_hlo, 1)

            x_low(0, 0)

            place, chosen, e_top, expert_ids, delta = (
                kept[name] for name in ("place", "chosen", "e_top", "expert_ids", "delta"))
            chain = [0]

            def link(ins):
                chain[0] += 1
                ins.then_inc(s_chain, 1)
                dve.wait_ge(s_chain, chain[0])

            flat_kt = lambda v: v[:, :, :].rearrange("p k t -> p (k t)")
            per_choice = [P, TOP * TILES, E]
            link(dve.tensor_tensor(which[:, :, :], flat_kt(chosen)[:, :, None].to_broadcast(per_choice),
                                   expert_ids[:, None, :].to_broadcast(per_choice), ALU.is_equal))
            link(dve.tensor_tensor(which[:, :, :], which[:, :, :], delta[:, None, :].to_broadcast(per_choice), ALU.mult))
            link(dve.tensor_reduce(flat_kt(y_row), which[:, :, :], axis=AX.X, op=ALU.add))
            link(dve.tensor_tensor(flat_kt(y_row), flat_kt(y_row), flat_kt(place), ALU.add))
            dve.tensor_tensor(y_at[:, 0, :], y_row[:, 0, :], y_row[:, 1, :], ALU.min)
            dve.tensor_tensor(y_at[:, 1, :], y_row[:, 0, :], y_row[:, 1, :], ALU.max)
            dve.tensor_tensor(first_upper[:, :], y_row[:, 0, :], y_row[:, 1, :], ALU.is_gt)
            link(dve.tensor_tensor(first_lower[:, :], y_row[:, 0, :], y_row[:, 1, :], ALU.is_lt))
            link(dve.tensor_scalar(part[:, 0, :], e_top[:, :], 1.0, None, ALU.add))
            link(dve.reciprocal(w_top[:, 0, :], part[:, 0, :]))
            link(dve.tensor_tensor(w_top[:, 1, :], e_top[:, :], w_top[:, 0, :], ALU.mult))
            for k, own in enumerate((first_lower, first_upper)):
                other = (first_upper, first_lower)[k]
                dve.tensor_tensor(part[:, 0, :], own[:, :], w_top[:, 0, :], ALU.mult)
                link(dve.tensor_tensor(part[:, 1, :], other[:, :], w_top[:, 1, :], ALU.mult))
                link(dve.tensor_tensor(mix[:, k, :], part[:, 0, :], part[:, 1, :], ALU.add))
            dve.sem_inc(s_rows, 1)

            def step(n, it):
                b = it * BU + n
                for hc in range(HC):
                    hidden(b, hc)
                    if hc >= 1:
                        low(b, hc - 1)
                    elif not is_first(b):
                        low(b - 1, HC - 1)
                    if hc == AHEAD + 1 and not is_last(b):
                        x_low(b + 1, n + 1)

            passes(dve, step)
            low(NB - 1, HC - 1)
            for i in (*EARLY, *LATE):
                if i in EARLY:
                    dve.wait_ge(s_early, i - EARLY[0] + 1)
                else:
                    dve.wait_ge(s_x1_in[i], 16)
                    dve.wait_ge(s_low_in[i], 16 * PW)
                    for t in range(i * PW, (i + 1) * PW):
                        last = dve.scalar_tensor_tensor(x1_sb[:, t, :], y_low[:, t, :], mix[:, 0, t:t + 1],
                                                        x1_sb[:, t, :], ALU.mult, ALU.add)
                    last.then_inc(s_half_sum, 1)
                    dve.wait_ge(s_half_sum, i - LATE[0] + 1)
                dve.wait_ge(s_high_in[i], 16 * PW)
                for t in range(i * PW, (i + 1) * PW):
                    last = dve.scalar_tensor_tensor(x1_sb[:, t, :], y_high[t // cut][:, t % cut, :],
                                                    mix[:, 1, t:t + 1], x1_sb[:, t, :], ALU.mult, ALU.add)
                last.then_inc(s_sum[i], 1)


def kernel(**inputs):
    import numpy as np
    import concourse.bacc as bacc
    from concourse.bass_utils import run_bass_kernel_spmd

    nc = bacc.Bacc("TRN2", target_bir_lowering=False, num_devices=1)
    laid_out = {
        "x": inputs["x"],
        "adj": inputs["adj"],
        "wq": inputs["L0_gnn_Wq"],
        "wk": inputs["L0_gnn_Wk"],
        "wv_t": np.asarray(inputs["L0_gnn_Wv"]).T,
        "gate_t": np.asarray(inputs["L0_ffn_gate_w"]).T,
        "w1_t": np.asarray(inputs["L0_ffn_w1"]).transpose(0, 2, 1),
        "w3_t": np.asarray(inputs["L0_ffn_w3"]).transpose(0, 2, 1),
        "w2_t": np.asarray(inputs["L0_ffn_w2"]).transpose(0, 2, 1),
    }
    arrays, args = {}, []
    for name, a in laid_out.items():
        a = np.ascontiguousarray(a)
        arrays[f"in_{name}"] = a
        args.append(nc.dram_tensor(f"in_{name}", a.shape, mybir.dt.from_np(a.dtype), kind="ExternalInput").ap())
    args.append(nc.dram_tensor("out_0", laid_out["x"].shape, mybir.dt.float32, kind="ExternalOutput").ap())
    gnn_moe(nc, *args)
    return run_bass_kernel_spmd(nc, [arrays], core_ids=[0]).results[0]["out_0"]
```
